# Optimizing a Trainium2 kernel written in Bass

```python
import numpy as np
import jax
import jax.numpy as jnp

def _softmax(x, axis=-1):
    return jax.nn.softmax(x, axis=axis)

def _gelu(x):
    return jax.nn.gelu(x, approximate=True)

def _silu(x):
    return jax.nn.silu(x)

def _sigmoid(x):
    return jax.nn.sigmoid(x)

def _layernorm(x, axis=-1, eps=1e-05):
    m = jnp.mean(x, axis=axis, keepdims=True)
    v = jnp.var(x, axis=axis, keepdims=True)
    return (x - m) / jnp.sqrt(v + eps)

def _scatter_add(tgt, idx, src, axis=0):
    return tgt.at[idx].add(src)

def _segment_sum(src, seg, n):
    return jax.ops.segment_sum(src, seg, n)
kernel_name = 'mk_prb_d4_jaxref_r8_f5133f'

def setup_inputs(seed: int=0):
    np.random.seed(seed)
    _w = jnp.asarray

    def _L0_attn_setup():
        import jax, jax.numpy as jnp
        import numpy as np
        from jax import lax
        B, L = (2, 256)
        DIM, HEADS = (128, 16)
        HD = DIM // HEADS
        D_STATE, D_CONV = (16, 4)
        D_INNER = 2 * DIM
        DT_RANK = DIM // 16

        def _mqa(x, wqkv, bqkv, w_attn_out, b_attn_out):
            b, l, d = x.shape
            qkv = x @ wqkv + bqkv
            q = qkv[..., :DIM].reshape(b, l, HEADS, HD)
            k = qkv[..., DIM:DIM + HD]
            v = qkv[..., DIM + HD:]
            scores = jnp.einsum('blhd,bmd->bhlm', q, k) / np.sqrt(HD).astype(np.float32)
            causal = jnp.tril(jnp.ones((l, l), bool))
            scores = jnp.where(causal, scores, jnp.finfo(scores.dtype).min)
            attn = jax.nn.softmax(scores, axis=-1)
            out = jnp.einsum('bhlm,bmd->blhd', attn, v).reshape(b, l, DIM)
            return out @ w_attn_out + b_attn_out

        def _mamba(x, w_in, conv_w, conv_b, w_xproj, w_dt, b_dt, A_log, Dp, w_out):
            b, l, d = x.shape
            xr = x @ w_in
            u0, res = (xr[..., :D_INNER], xr[..., D_INNER:])
            lhs = u0.transpose(0, 2, 1)
            rhs = conv_w[:, None, :]
            xc = lax.conv_general_dilated(lhs, rhs, window_strides=(1,), padding=[(D_CONV - 1, 0)], dimension_numbers=('NCH', 'OIH', 'NCH'), feature_group_count=D_INNER)
            u = jax.nn.silu((xc + conv_b[None, :, None]).transpose(0, 2, 1))
            x_dbl = u @ w_xproj
            delta = jax.nn.softplus(x_dbl[..., :DT_RANK] @ w_dt + b_dt)
            Bm = x_dbl[..., DT_RANK:DT_RANK + D_STATE]
            Cm = x_dbl[..., DT_RANK + D_STATE:]
            A = -jnp.exp(A_log)

            def step(h, inp):
                d_t, b_t, c_t, u_t = inp
                dA = jnp.exp(d_t[..., None] * A)
                h = dA * h + (d_t * u_t)[..., None] * b_t[:, None, :]
                y = jnp.einsum('bdn,bn->bd', h, c_t)
                return (h, y)
            xs = (delta.transpose(1, 0, 2), Bm.transpose(1, 0, 2), Cm.transpose(1, 0, 2), u.transpose(1, 0, 2))
            h0 = jnp.zeros((b, D_INNER, D_STATE), u.dtype)
            _, ys = lax.scan(step, h0, xs)
            y = ys.transpose(1, 0, 2) + u * Dp
            y = y * jax.nn.silu(res)
            return y @ w_out
        key = jax.random.key(seed)
        ks = jax.random.split(key, 12)
        w = lambda k, shape, s=0.02: jax.random.normal(k, shape, jnp.float32) * s
        A_log = jnp.log(jnp.tile(jnp.arange(1, D_STATE + 1, dtype=jnp.float32), (D_INNER, 1)))
        return {'x': jax.random.normal(ks[0], (B, L, DIM), jnp.float32), 'wqkv': w(ks[1], (DIM, DIM + 2 * HD)), 'bqkv': jnp.zeros((DIM + 2 * HD,), jnp.float32), 'w_attn_out': w(ks[2], (DIM, DIM)), 'b_attn_out': jnp.zeros((DIM,), jnp.float32), 'w_in': w(ks[3], (DIM, 2 * D_INNER)), 'conv_w': w(ks[4], (D_INNER, D_CONV), 0.1), 'conv_b': jnp.zeros((D_INNER,), jnp.float32), 'w_xproj': w(ks[5], (D_INNER, DT_RANK + 2 * D_STATE)), 'w_dt': w(ks[6], (DT_RANK, D_INNER)), 'b_dt': w(ks[7], (D_INNER,), 0.01), 'A_log': A_log, 'Dp': jnp.ones((D_INNER,), jnp.float32), 'w_out': w(ks[8], (D_INNER, DIM))}
    _L0_attn_in = _L0_attn_setup()

    def _L0_ffn_setup():
        import jax, jax.numpy as jnp
        import numpy as np
        B, S, D, E, H, K = (64, 256, 128, 32, 512, 8)
        key = jax.random.key(seed)
        k0, k1, k2, k3 = jax.random.split(key, 4)
        x = jax.random.normal(k0, (B, S, D), jnp.float32)
        gate_w = jax.random.normal(k1, (E, D), jnp.float32) * (1.0 / np.sqrt(D))
        gate_b = jnp.zeros((E,), jnp.float32)
        w1 = jax.random.normal(k2, (E, D + 1, H), jnp.float32) * (1.0 / np.sqrt(D + 1))
        w2 = jax.random.normal(k3, (E, H + 1, D), jnp.float32) * (1.0 / np.sqrt(H + 1))
        return {'x': x, 'gate_w': gate_w, 'gate_b': gate_b, 'w1': w1, 'w2': w2}
    _L0_ffn_in = _L0_ffn_setup()

    def _L1_attn_setup():
        import jax, jax.numpy as jnp
        import numpy as np
        B, S, D, H, A = (2, 256, 128, 16, 64)
        INIT_STD = 0.02
        key = jax.random.key(seed)
        ks = jax.random.split(key, 5)
        return {'residual': jax.random.normal(ks[0], (B, S, D), dtype=jnp.float32), 'Wq': jax.random.normal(ks[1], (H, D, A), dtype=jnp.float32) * INIT_STD, 'Wk': jax.random.normal(ks[2], (H, D, A), dtype=jnp.float32) * INIT_STD, 'Wv': jax.random.normal(ks[3], (H, D, A), dtype=jnp.float32) * INIT_STD, 'Wo': jax.random.normal(ks[4], (H, A, D), dtype=jnp.float32) * INIT_STD, 'bq': jnp.zeros((H, A), dtype=jnp.float32), 'bk': jnp.zeros((H, A), dtype=jnp.float32), 'bv': jnp.zeros((H, A), dtype=jnp.float32), 'bo': jnp.zeros((D,), dtype=jnp.float32)}
    _L1_attn_in = _L1_attn_setup()

    def _L1_ffn_setup():
        import jax, jax.numpy as jnp
        import numpy as np
        BLOCK = 16
        _GRID = jnp.array([0.0, 0.5, 1.0, 1.5, 2.0, 3.0, 4.0, 6.0], dtype=jnp.float32)
        _MID = jnp.array([0.25, 0.75, 1.25, 1.75, 2.5, 3.5, 5.0], dtype=jnp.float32)

        def fp4_quant_dequant(x):
            shape = x.shape
            xb = x.reshape(shape[:-1] + (shape[-1] // BLOCK, BLOCK))
            scale = jnp.max(jnp.abs(xb), axis=-1, keepdims=True) / 6.0
            scale = jnp.maximum(scale, jnp.float32(1e-12))
            xn = xb / scale
            idx = jnp.searchsorted(_MID, jnp.abs(xn))
            q = _GRID[idx] * jnp.sign(xn) * scale
            return q.reshape(shape)

        def fp4_linear(x, w):
            xq = fp4_quant_dequant(x)
            wq = fp4_quant_dequant(w)
            return jnp.einsum('bsk,nk->bsn', xq, wq)
        key = jax.random.key(seed)
        k1, k2, k3, k4 = jax.random.split(key, 4)
        H, I = (128, 352)
        x = jax.random.normal(k1, (4, 512, H), dtype=jnp.float32)
        w_gate = jax.random.normal(k2, (I, H), dtype=jnp.float32) * 0.02
        w_up = jax.random.normal(k3, (I, H), dtype=jnp.float32) * 0.02
        w_down = jax.random.normal(k4, (H, I), dtype=jnp.float32) * 0.02
        return {'x': x, 'w_gate': w_gate, 'w_up': w_up, 'w_down': w_down}
    _L1_ffn_in = _L1_ffn_setup()

    def _L2_attn_setup():
        import jax, jax.numpy as jnp
        import numpy as np
        B, S, H, NH = (2, 256, 128, 16)
        HD = H // NH
        key = jax.random.key(seed)
        ks = jax.random.split(key, 9)
        w = lambda k: jax.random.normal(k, (H, H), dtype=jnp.float32) * 0.02
        b = lambda k: jax.random.normal(k, (H,), dtype=jnp.float32) * 0.02
        return {'hidden_states': jax.random.normal(ks[0], (B, S, H), dtype=jnp.float32), 'Wq': w(ks[1]), 'bq': b(ks[2]), 'Wk': w(ks[3]), 'bk': b(ks[4]), 'Wv': w(ks[5]), 'bv': b(ks[6]), 'Wo': w(ks[7]), 'bo': b(ks[8])}
    _L2_attn_in = _L2_attn_setup()

    def _L2_ffn_setup():
        import jax, jax.numpy as jnp
        import numpy as np
        D_MODEL = 128
        EXPERT_DIM = 512
        N_EXPERTS = 8
        CAP_FACTOR = 0.5
        key = jax.random.key(seed)
        ks = jax.random.split(key, 7)
        inp = {'input': jax.random.normal(ks[0], (4, 512, D_MODEL), dtype=jnp.float32), 'w_switch': jax.random.normal(ks[1], (D_MODEL, N_EXPERTS), dtype=jnp.float32) * 0.02, 'b_switch': jnp.zeros((N_EXPERTS,), jnp.float32), 'w1': jax.random.normal(ks[2], (N_EXPERTS, D_MODEL, EXPERT_DIM), dtype=jnp.float32) * 0.02, 'b1': jnp.zeros((N_EXPERTS, EXPERT_DIM), jnp.float32), 'w2': jax.random.normal(ks[3], (N_EXPERTS, EXPERT_DIM, D_MODEL), dtype=jnp.float32) * 0.02, 'b2': jnp.zeros((N_EXPERTS, D_MODEL), jnp.float32)}
        return inp
    _L2_ffn_in = _L2_ffn_setup()

    def _L3_attn_setup():
        import jax, jax.numpy as jnp
        import numpy as np
        D_MODEL = 128
        STATE_DIM = 16
        LN_EPS = 1e-05
        IMP_TEMP = 0.5

        def _layer_norm(x, gamma, beta):
            mu = jnp.mean(x, axis=-1, keepdims=True)
            var = jnp.mean(jnp.square(x - mu), axis=-1, keepdims=True)
            return (x - mu) * jax.lax.rsqrt(var + LN_EPS) * gamma + beta

        def _ssm_scan(x, delta, A, B_sel, C_sel):
            Bb, S, D = x.shape
            N = A.shape[1]

            def step(h, inp):
                d_t, x_t, b_t, c_t = inp
                decay = jnp.exp(d_t[:, :, None] * A)
                h = h * decay + (d_t * x_t)[:, :, None] * b_t[:, None, :]
                y_t = jnp.einsum('bdn,bn->bd', h, c_t)
                return (h, y_t)
            xs = (jnp.moveaxis(delta, 1, 0), jnp.moveaxis(x, 1, 0), jnp.moveaxis(B_sel, 1, 0), jnp.moveaxis(C_sel, 1, 0))
            h0 = jnp.zeros((Bb, D, N), dtype=x.dtype)
            _, ys = jax.lax.scan(step, h0, xs)
            return jnp.moveaxis(ys, 0, 1)

        def _reference_tuple_inner(x, A_log, W_delta, W_B, W_C, ln_gamma, ln_beta, W_ctx, context_scale, W_imp):
            delta = jax.nn.softplus(jnp.einsum('bsd,ed->bse', x, W_delta))
            B_sel = jnp.einsum('bsd,nd->bsn', x, W_B)
            C_sel = jnp.einsum('bsd,nd->bsn', x, W_C)
            A = -jnp.exp(A_log)
            ssm_out = _ssm_scan(x, delta, A, B_sel, C_sel)
            ssm_out = _layer_norm(ssm_out, ln_gamma, ln_beta)
            context = jnp.einsum('bsd,ed->bse', ssm_out, W_ctx) * context_scale
            h_final = ssm_out[:, -1, :]
            h_proj = jnp.einsum('bd,ed->be', h_final, W_imp)
            raw_importance = jnp.einsum('bsd,bd->bs', x, h_proj)
            importance = jax.nn.softmax(raw_importance / IMP_TEMP, axis=-1)
            return (importance, context, raw_importance)
        key = jax.random.key(seed)
        ks = jax.random.split(key, 8)
        B, S, D, N = (2, 512, D_MODEL, STATE_DIM)
        x = jax.random.normal(ks[0], (B, S, D), dtype=jnp.float32)
        A_log = jax.random.normal(ks[1], (D, N), dtype=jnp.float32) * 0.1
        W_delta = jax.random.normal(ks[2], (D, D), dtype=jnp.float32) * 0.02
        W_B = jax.random.normal(ks[3], (N, D), dtype=jnp.float32) * 0.02
        W_C = jax.random.normal(ks[4], (N, D), dtype=jnp.float32) * 0.02
        ln_gamma = jnp.ones((D,), dtype=jnp.float32)
        ln_beta = jnp.zeros((D,), dtype=jnp.float32)
        W_ctx = jax.random.normal(ks[5], (D, D), dtype=jnp.float32) * 0.02
        context_scale = jnp.float32(0.1)
        W_imp = jax.random.normal(ks[6], (D, D), dtype=jnp.float32) * 0.02
        return {'x': x, 'A_log': A_log, 'W_delta': W_delta, 'W_B': W_B, 'W_C': W_C, 'ln_gamma': ln_gamma, 'ln_beta': ln_beta, 'W_ctx': W_ctx, 'context_scale': context_scale, 'W_imp': W_imp}
    _L3_attn_in = _L3_attn_setup()

    def _L3_ffn_setup():
        import jax, jax.numpy as jnp
        import numpy as np
        BEST_K = 2

        def _expert(xf, w1, w3, w2):
            return jax.nn.silu(xf @ w1) * (xf @ w3) @ w2
        key = jax.random.key(seed)
        ks = jax.random.split(key, 9)
        E, S_sh, D, H = (8, 2, 128, 64)
        B, S = (2, 256)
        w = lambda k, shape: jax.random.normal(k, shape, dtype=jnp.float32) * 0.02
        return {'x': jax.random.normal(ks[0], (B, S, D), dtype=jnp.float32), 'router_w': w(ks[1], (D, E)), 'router_b': jnp.zeros((E,), dtype=jnp.float32), 'routed_w1': w(ks[2], (E, D, H)), 'routed_w3': w(ks[3], (E, D, H)), 'routed_w2': w(ks[4], (E, H, D)), 'shared_w1': w(ks[5], (S_sh, D, H)), 'shared_w3': w(ks[6], (S_sh, D, H)), 'shared_w2': w(ks[7], (S_sh, H, D))}
    _L3_ffn_in = _L3_ffn_setup()
    _d = {'L0_attn_x': _L0_attn_in['x'], 'L0_attn_wqkv': _L0_attn_in['wqkv'], 'L0_attn_bqkv': _L0_attn_in['bqkv'], 'L0_attn_w_attn_out': _L0_attn_in['w_attn_out'], 'L0_attn_b_attn_out': _L0_attn_in['b_attn_out'], 'L0_attn_w_in': _L0_attn_in['w_in'], 'L0_attn_conv_w': _L0_attn_in['conv_w'], 'L0_attn_conv_b': _L0_attn_in['conv_b'], 'L0_attn_w_xproj': _L0_attn_in['w_xproj'], 'L0_attn_w_dt': _L0_attn_in['w_dt'], 'L0_attn_b_dt': _L0_attn_in['b_dt'], 'L0_attn_A_log': _L0_attn_in['A_log'], 'L0_attn_Dp': _L0_attn_in['Dp'], 'L0_attn_w_out': _L0_attn_in['w_out'], 'L0_ffn_gate_w': _L0_ffn_in['gate_w'], 'L0_ffn_gate_b': _L0_ffn_in['gate_b'], 'L0_ffn_w1': _L0_ffn_in['w1'], 'L0_ffn_w2': _L0_ffn_in['w2'], 'L1_attn_Wq': _L1_attn_in['Wq'], 'L1_attn_Wk': _L1_attn_in['Wk'], 'L1_attn_Wv': _L1_attn_in['Wv'], 'L1_attn_Wo': _L1_attn_in['Wo'], 'L1_attn_bq': _L1_attn_in['bq'], 'L1_attn_bk': _L1_attn_in['bk'], 'L1_attn_bv': _L1_attn_in['bv'], 'L1_attn_bo': _L1_attn_in['bo'], 'L1_ffn_w_gate': _L1_ffn_in['w_gate'], 'L1_ffn_w_up': _L1_ffn_in['w_up'], 'L1_ffn_w_down': _L1_ffn_in['w_down'], 'L2_attn_Wq': _L2_attn_in['Wq'], 'L2_attn_bq': _L2_attn_in['bq'], 'L2_attn_Wk': _L2_attn_in['Wk'], 'L2_attn_bk': _L2_attn_in['bk'], 'L2_attn_Wv': _L2_attn_in['Wv'], 'L2_attn_bv': _L2_attn_in['bv'], 'L2_attn_Wo': _L2_attn_in['Wo'], 'L2_attn_bo': _L2_attn_in['bo'], 'L2_ffn_w_switch': _L2_ffn_in['w_switch'], 'L2_ffn_b_switch': _L2_ffn_in['b_switch'], 'L2_ffn_w1': _L2_ffn_in['w1'], 'L2_ffn_b1': _L2_ffn_in['b1'], 'L2_ffn_w2': _L2_ffn_in['w2'], 'L2_ffn_b2': _L2_ffn_in['b2'], 'L3_attn_A_log': _L3_attn_in['A_log'], 'L3_attn_W_delta': _L3_attn_in['W_delta'], 'L3_attn_W_B': _L3_attn_in['W_B'], 'L3_attn_W_C': _L3_attn_in['W_C'], 'L3_attn_ln_gamma': _L3_attn_in['ln_gamma'], 'L3_attn_ln_beta': _L3_attn_in['ln_beta'], 'L3_attn_W_ctx': _L3_attn_in['W_ctx'], 'L3_attn_context_scale': _L3_attn_in['context_scale'], 'L3_attn_W_imp': _L3_attn_in['W_imp'], 'L3_ffn_router_w': _L3_ffn_in['router_w'], 'L3_ffn_router_b': _L3_ffn_in['router_b'], 'L3_ffn_routed_w1': _L3_ffn_in['routed_w1'], 'L3_ffn_routed_w3': _L3_ffn_in['routed_w3'], 'L3_ffn_routed_w2': _L3_ffn_in['routed_w2'], 'L3_ffn_shared_w1': _L3_ffn_in['shared_w1'], 'L3_ffn_shared_w3': _L3_ffn_in['shared_w3'], 'L3_ffn_shared_w2': _L3_ffn_in['shared_w2']}
    _x0 = _d['L0_attn_x']
    _d['L0_attn_x'] = jax.random.normal(jax.random.fold_in(jax.random.key(seed), 1), (16, 256, 128), dtype=_x0.dtype)
    del _x0
    return _d

def reference(L0_attn_x, L0_attn_wqkv, L0_attn_bqkv, L0_attn_w_attn_out, L0_attn_b_attn_out, L0_attn_w_in, L0_attn_conv_w, L0_attn_conv_b, L0_attn_w_xproj, L0_attn_w_dt, L0_attn_b_dt, L0_attn_A_log, L0_attn_Dp, L0_attn_w_out, L0_ffn_gate_w, L0_ffn_gate_b, L0_ffn_w1, L0_ffn_w2, L1_attn_Wq, L1_attn_Wk, L1_attn_Wv, L1_attn_Wo, L1_attn_bq, L1_attn_bk, L1_attn_bv, L1_attn_bo, L1_ffn_w_gate, L1_ffn_w_up, L1_ffn_w_down, L2_attn_Wq, L2_attn_bq, L2_attn_Wk, L2_attn_bk, L2_attn_Wv, L2_attn_bv, L2_attn_Wo, L2_attn_bo, L2_ffn_w_switch, L2_ffn_b_switch, L2_ffn_w1, L2_ffn_b1, L2_ffn_w2, L2_ffn_b2, L3_attn_A_log, L3_attn_W_delta, L3_attn_W_B, L3_attn_W_C, L3_attn_ln_gamma, L3_attn_ln_beta, L3_attn_W_ctx, L3_attn_context_scale, L3_attn_W_imp, L3_ffn_router_w, L3_ffn_router_b, L3_ffn_routed_w1, L3_ffn_routed_w3, L3_ffn_routed_w2, L3_ffn_shared_w1, L3_ffn_shared_w3, L3_ffn_shared_w2):

    def _L0_attn_ref(x, wqkv, bqkv, w_attn_out, b_attn_out, w_in, conv_w, conv_b, w_xproj, w_dt, b_dt, A_log, Dp, w_out):
        import jax, jax.numpy as jnp
        import numpy as np
        from jax import lax
        B, L = (2, 256)
        DIM, HEADS = (128, 16)
        HD = DIM // HEADS
        D_STATE, D_CONV = (16, 4)
        D_INNER = 2 * DIM
        DT_RANK = DIM // 16

        def _mqa(x, wqkv, bqkv, w_attn_out, b_attn_out):
            b, l, d = x.shape
            qkv = x @ wqkv + bqkv
            q = qkv[..., :DIM].reshape(b, l, HEADS, HD)
            k = qkv[..., DIM:DIM + HD]
            v = qkv[..., DIM + HD:]
            scores = jnp.einsum('blhd,bmd->bhlm', q, k) / np.sqrt(HD).astype(np.float32)
            causal = jnp.tril(jnp.ones((l, l), bool))
            scores = jnp.where(causal, scores, jnp.finfo(scores.dtype).min)
            attn = jax.nn.softmax(scores, axis=-1)
            out = jnp.einsum('bhlm,bmd->blhd', attn, v).reshape(b, l, DIM)
            return out @ w_attn_out + b_attn_out

        def _mamba(x, w_in, conv_w, conv_b, w_xproj, w_dt, b_dt, A_log, Dp, w_out):
            b, l, d = x.shape
            xr = x @ w_in
            u0, res = (xr[..., :D_INNER], xr[..., D_INNER:])
            lhs = u0.transpose(0, 2, 1)
            rhs = conv_w[:, None, :]
            xc = lax.conv_general_dilated(lhs, rhs, window_strides=(1,), padding=[(D_CONV - 1, 0)], dimension_numbers=('NCH', 'OIH', 'NCH'), feature_group_count=D_INNER)
            u = jax.nn.silu((xc + conv_b[None, :, None]).transpose(0, 2, 1))
            x_dbl = u @ w_xproj
            delta = jax.nn.softplus(x_dbl[..., :DT_RANK] @ w_dt + b_dt)
            Bm = x_dbl[..., DT_RANK:DT_RANK + D_STATE]
            Cm = x_dbl[..., DT_RANK + D_STATE:]
            A = -jnp.exp(A_log)

            def step(h, inp):
                d_t, b_t, c_t, u_t = inp
                dA = jnp.exp(d_t[..., None] * A)
                h = dA * h + (d_t * u_t)[..., None] * b_t[:, None, :]
                y = jnp.einsum('bdn,bn->bd', h, c_t)
                return (h, y)
            xs = (delta.transpose(1, 0, 2), Bm.transpose(1, 0, 2), Cm.transpose(1, 0, 2), u.transpose(1, 0, 2))
            h0 = jnp.zeros((b, D_INNER, D_STATE), u.dtype)
            _, ys = lax.scan(step, h0, xs)
            y = ys.transpose(1, 0, 2) + u * Dp
            y = y * jax.nn.silu(res)
            return y @ w_out
        attended = _mqa(x, wqkv, bqkv, w_attn_out, b_attn_out)
        x1 = attended + x
        y = _mamba(x1, w_in, conv_w, conv_b, w_xproj, w_dt, b_dt, A_log, Dp, w_out)
        return y + x1

    def _L0_ffn_ref(x, gate_w, gate_b, w1, w2):
        import jax, jax.numpy as jnp
        import numpy as np
        B, S, D, E, H, K = (64, 256, 128, 32, 512, 8)
        b, s, d = x.shape
        logits = jnp.einsum('bsd,ed->bse', x, gate_w) + gate_b
        probs = jax.nn.softmax(logits, axis=-2)
        vals_t, idx_t = jax.lax.top_k(probs.transpose(0, 2, 1), K)
        vals = vals_t.transpose(0, 2, 1)
        idx = idx_t.transpose(0, 2, 1)
        flat_idx = idx.reshape(b, K * E)
        tok = jnp.take_along_axis(x, flat_idx[:, :, None], axis=1)
        tok = tok.reshape(b, K, E, d)
        merged = jnp.einsum('bked,bke->bed', tok, vals)
        ones = jnp.ones(merged.shape[:-1] + (1,), merged.dtype)
        h = jnp.einsum('bei,eih->beh', jnp.concatenate([merged, ones], -1), w1)
        h = jax.nn.gelu(h, approximate=False)
        o = jnp.einsum('bej,ejo->beo', jnp.concatenate([h, ones], -1), w2)
        out_tok = jnp.einsum('beo,bke->bkeo', o, vals).reshape(b, K * E, d)
        out = jnp.zeros_like(x).at[jnp.arange(b)[:, None], flat_idx].add(out_tok)
        return out

    def _L1_attn_ref(residual, Wq, Wk, Wv, Wo, bq, bk, bv, bo):
        import jax, jax.numpy as jnp
        import numpy as np
        B, S, D, H, A = (2, 256, 128, 16, 64)
        INIT_STD = 0.02
        q = jnp.einsum('bsd,hda->bhsa', residual, Wq) + bq[None, :, None, :]
        k = jnp.einsum('bsd,hda->bhsa', residual, Wk) + bk[None, :, None, :]
        v = jnp.einsum('bsd,hda->bhsa', residual, Wv) + bv[None, :, None, :]
        scale = 1.0 / jnp.sqrt(jnp.float32(q.shape[-1]))
        scores = jnp.einsum('bhsa,bhta->bhst', q, k) * scale
        s = scores.shape[-1]
        causal = jnp.tril(jnp.ones((s, s), dtype=bool))
        masked = jnp.where(causal, scores, jnp.float32(-100000.0))
        pattern = jax.nn.softmax(masked, axis=-1)
        z = jnp.einsum('bhst,bhta->bshа'.replace('а', 'a'), pattern, v)
        out = jnp.einsum('bsha,had->bsd', z, Wo) + bo
        return out

    def _L1_ffn_ref(x, w_gate, w_up, w_down):
        import jax, jax.numpy as jnp
        import numpy as np
        BLOCK = 16
        _GRID = jnp.array([0.0, 0.5, 1.0, 1.5, 2.0, 3.0, 4.0, 6.0], dtype=jnp.float32)
        _MID = jnp.array([0.25, 0.75, 1.25, 1.75, 2.5, 3.5, 5.0], dtype=jnp.float32)

        def fp4_quant_dequant(x):
            shape = x.shape
            xb = x.reshape(shape[:-1] + (shape[-1] // BLOCK, BLOCK))
            scale = jnp.max(jnp.abs(xb), axis=-1, keepdims=True) / 6.0
            scale = jnp.maximum(scale, jnp.float32(1e-12))
            xn = xb / scale
            idx = jnp.searchsorted(_MID, jnp.abs(xn))
            q = _GRID[idx] * jnp.sign(xn) * scale
            return q.reshape(shape)

        def fp4_linear(x, w):
            xq = fp4_quant_dequant(x)
            wq = fp4_quant_dequant(w)
            return jnp.einsum('bsk,nk->bsn', xq, wq)
        gate = fp4_linear(x, w_gate)
        y = fp4_linear(x, w_up)
        h = jax.nn.silu(gate) * y
        return fp4_linear(h, w_down)

    def _L2_attn_ref(hidden_states, Wq, bq, Wk, bk, Wv, bv, Wo, bo):
        import jax, jax.numpy as jnp
        import numpy as np
        B, S, H, NH = (2, 256, 128, 16)
        HD = H // NH
        b, s, h = hidden_states.shape
        nh, hd = (NH, h // NH)

        def proj(W, bias):
            y = hidden_states @ W.T + bias
            return y.reshape(b, s, nh, hd).transpose(0, 2, 1, 3)
        q = proj(Wq, bq)
        k = proj(Wk, bk)
        v = proj(Wv, bv)
        scale = jnp.sqrt(jnp.asarray(hd, dtype=q.dtype))
        scores = jnp.einsum('bhqd,bhkd->bhqk', q, k) / scale
        pos = jnp.arange(s)
        causal = pos[:, None] < pos[None, :]
        scores = jnp.where(causal[None, None], -jnp.inf, scores)
        attn = jax.nn.softmax(scores, axis=-1)
        out = jnp.einsum('bhqk,bhkd->bhqd', attn, v)
        out = out.transpose(0, 2, 1, 3).reshape(b, s, h)
        return out @ Wo.T + bo

    def _L2_ffn_ref(input, w_switch, b_switch, w1, b1, w2, b2):
        import jax, jax.numpy as jnp
        import numpy as np
        D_MODEL = 128
        EXPERT_DIM = 512
        N_EXPERTS = 8
        CAP_FACTOR = 0.5
        B, S, D = input.shape
        T = B * S
        E = b_switch.shape[0]
        capacity = int(CAP_FACTOR * T / E)
        x = input.reshape(T, D)
        logits = x @ w_switch + b_switch
        probs = jax.nn.softmax(logits, axis=-1)
        pmax = probs.max(axis=-1)
        routes = probs.argmax(axis=-1)
        oh = (routes[:, None] == jnp.arange(E)[None, :]).astype(jnp.int32)
        pos = (jnp.cumsum(oh, axis=0) * oh).sum(-1) - 1
        keep = pos < capacity
        slot = jnp.where(keep, routes * capacity + pos, E * capacity)
        buf = jnp.zeros((E * capacity + 1, D), x.dtype).at[slot].set(x)
        buf_e = buf[:E * capacity].reshape(E, capacity, D)
        h = jax.nn.relu(jnp.einsum('ecd,edh->ech', buf_e, w1) + b1[:, None, :])
        y = jnp.einsum('ech,ehd->ecd', h, w2) + b2[:, None, :]
        y_flat = jnp.concatenate([y.reshape(E * capacity, D), jnp.zeros((1, D), x.dtype)], axis=0)
        out = jnp.where(keep[:, None], y_flat[slot], x)
        scale = pmax / jax.lax.stop_gradient(pmax)
        out = out * scale[:, None]
        return out.reshape(B, S, D)

    def _L3_attn_ref(x, A_log, W_delta, W_B, W_C, ln_gamma, ln_beta, W_ctx, context_scale, W_imp):
        import jax, jax.numpy as jnp
        import numpy as np
        D_MODEL = 128
        STATE_DIM = 16
        LN_EPS = 1e-05
        IMP_TEMP = 0.5

        def _layer_norm(x, gamma, beta):
            mu = jnp.mean(x, axis=-1, keepdims=True)
            var = jnp.mean(jnp.square(x - mu), axis=-1, keepdims=True)
            return (x - mu) * jax.lax.rsqrt(var + LN_EPS) * gamma + beta

        def _ssm_scan(x, delta, A, B_sel, C_sel):
            Bb, S, D = x.shape
            N = A.shape[1]

            def step(h, inp):
                d_t, x_t, b_t, c_t = inp
                decay = jnp.exp(d_t[:, :, None] * A)
                h = h * decay + (d_t * x_t)[:, :, None] * b_t[:, None, :]
                y_t = jnp.einsum('bdn,bn->bd', h, c_t)
                return (h, y_t)
            xs = (jnp.moveaxis(delta, 1, 0), jnp.moveaxis(x, 1, 0), jnp.moveaxis(B_sel, 1, 0), jnp.moveaxis(C_sel, 1, 0))
            h0 = jnp.zeros((Bb, D, N), dtype=x.dtype)
            _, ys = jax.lax.scan(step, h0, xs)
            return jnp.moveaxis(ys, 0, 1)

        def _reference_tuple_inner(x, A_log, W_delta, W_B, W_C, ln_gamma, ln_beta, W_ctx, context_scale, W_imp):
            delta = jax.nn.softplus(jnp.einsum('bsd,ed->bse', x, W_delta))
            B_sel = jnp.einsum('bsd,nd->bsn', x, W_B)
            C_sel = jnp.einsum('bsd,nd->bsn', x, W_C)
            A = -jnp.exp(A_log)
            ssm_out = _ssm_scan(x, delta, A, B_sel, C_sel)
            ssm_out = _layer_norm(ssm_out, ln_gamma, ln_beta)
            context = jnp.einsum('bsd,ed->bse', ssm_out, W_ctx) * context_scale
            h_final = ssm_out[:, -1, :]
            h_proj = jnp.einsum('bd,ed->be', h_final, W_imp)
            raw_importance = jnp.einsum('bsd,bd->bs', x, h_proj)
            importance = jax.nn.softmax(raw_importance / IMP_TEMP, axis=-1)
            return (importance, context, raw_importance)
        return _reference_tuple_inner(x, A_log, W_delta, W_B, W_C, ln_gamma, ln_beta, W_ctx, context_scale, W_imp)[1]

    def _L3_ffn_ref(x, router_w, router_b, routed_w1, routed_w3, routed_w2, shared_w1, shared_w3, shared_w2):
        import jax, jax.numpy as jnp
        import numpy as np
        BEST_K = 2

        def _expert(xf, w1, w3, w2):
            return jax.nn.silu(xf @ w1) * (xf @ w3) @ w2
        B, S, D = x.shape
        T = B * S
        xf = x.reshape(T, D)
        logits = xf @ router_w + router_b
        topk_vals, topk_idx = jax.lax.top_k(logits, BEST_K)
        sparse = jnp.full_like(logits, -jnp.inf)
        sparse = sparse.at[jnp.arange(T)[:, None], topk_idx].set(topk_vals)
        gates = jax.nn.softmax(sparse, axis=-1)
        routed = jax.vmap(_expert, in_axes=(None, 0, 0, 0))(xf, routed_w1, routed_w3, routed_w2)
        routed_out = jnp.einsum('etd,te->td', routed, gates)
        shared_out = jax.vmap(_expert, in_axes=(None, 0, 0, 0))(xf, shared_w1, shared_w3, shared_w2).sum(axis=0)
        return (routed_out + shared_out).reshape(B, S, D)
    x = L0_attn_x
    xn = _layernorm(x, axis=-1)
    x = x + _L0_attn_ref(xn, L0_attn_wqkv, L0_attn_bqkv, L0_attn_w_attn_out, L0_attn_b_attn_out, L0_attn_w_in, L0_attn_conv_w, L0_attn_conv_b, L0_attn_w_xproj, L0_attn_w_dt, L0_attn_b_dt, L0_attn_A_log, L0_attn_Dp, L0_attn_w_out) + _L0_ffn_ref(xn, L0_ffn_gate_w, L0_ffn_gate_b, L0_ffn_w1, L0_ffn_w2)
    xn = _layernorm(x, axis=-1)
    x = x + _L1_attn_ref(xn, L1_attn_Wq, L1_attn_Wk, L1_attn_Wv, L1_attn_Wo, L1_attn_bq, L1_attn_bk, L1_attn_bv, L1_attn_bo) + _L1_ffn_ref(xn, L1_ffn_w_gate, L1_ffn_w_up, L1_ffn_w_down)
    xn = _layernorm(x, axis=-1)
    x = x + _L2_attn_ref(xn, L2_attn_Wq, L2_attn_bq, L2_attn_Wk, L2_attn_bk, L2_attn_Wv, L2_attn_bv, L2_attn_Wo, L2_attn_bo) + _L2_ffn_ref(xn, L2_ffn_w_switch, L2_ffn_b_switch, L2_ffn_w1, L2_ffn_b1, L2_ffn_w2, L2_ffn_b2)
    xn = _layernorm(x, axis=-1)
    x = x + _L3_attn_ref(xn, L3_attn_A_log, L3_attn_W_delta, L3_attn_W_B, L3_attn_W_C, L3_attn_ln_gamma, L3_attn_ln_beta, L3_attn_W_ctx, L3_attn_context_scale, L3_attn_W_imp) + _L3_ffn_ref(xn, L3_ffn_router_w, L3_ffn_router_b, L3_ffn_routed_w1, L3_ffn_routed_w3, L3_ffn_routed_w2, L3_ffn_shared_w1, L3_ffn_shared_w3, L3_ffn_shared_w2)
    return x

_drawn_inputs = setup_inputs


def setup_inputs(seed=0):
    import zlib

    import numpy as np

    out = dict(_drawn_inputs(seed))
    spreads = {'L0_attn_bqkv': (0.0, 0.1),
     'L0_attn_b_attn_out': (0.0, 0.1),
     'L0_attn_conv_b': (0.0, 0.8),
     'L0_attn_Dp': (1.0, 0.6),
     'L0_ffn_gate_b': (0.0, 0.8),
     'L1_attn_bq': (0.0, 0.8),
     'L1_attn_bk': (0.0, 0.8),
     'L1_attn_bv': (0.0, 0.1),
     'L1_attn_bo': (0.0, 0.1),
     'L2_ffn_b_switch': (0.0, 0.1),
     'L2_ffn_b1': (0.0, 0.8),
     'L2_ffn_b2': (0.0, 0.308),
     'L3_attn_ln_gamma': (1.0, 0.6),
     'L3_attn_ln_beta': (0.0, 0.8),
     'L3_ffn_router_b': (0.0, 0.8)}
    factors = {'L0_attn_wqkv': 4.429,
     'L0_attn_w_in': 8.0,
     'L0_attn_conv_w': 8.0,
     'L0_attn_w_xproj': 8.0,
     'L0_attn_w_dt': 8.0,
     'L0_attn_b_dt': 8.0,
     'L0_attn_A_log': 8.0,
     'L0_attn_w_out': 7.421,
     'L0_ffn_gate_w': 2.731,
     'L1_attn_Wq': 6.57,
     'L1_attn_Wk': 6.538,
     'L1_ffn_w_gate': 3.353,
     'L1_ffn_w_up': 3.065,
     'L1_ffn_w_down': 4.488,
     'L2_attn_Wq': 8.0,
     'L2_attn_bq': 8.0,
     'L2_attn_Wk': 8.0,
     'L2_attn_bk': 8.0,
     'L2_attn_Wv': 8.0,
     'L2_attn_bv': 8.0,
     'L2_attn_Wo': 8.0,
     'L2_attn_bo': 7.023,
     'L2_ffn_w1': 3.601,
     'L2_ffn_w2': 2.79,
     'L3_attn_A_log': 8.0,
     'L3_attn_W_delta': 8.0,
     'L3_attn_W_B': 6.367,
     'L3_attn_W_C': 6.184,
     'L3_attn_W_ctx': 6.25,
     'L3_ffn_router_w': 8.0,
     'L3_ffn_routed_w1': 8.0,
     'L3_ffn_routed_w3': 8.0,
     'L3_ffn_routed_w2': 8.0,
     'L3_ffn_shared_w1': 8.0,
     'L3_ffn_shared_w3': 8.0,
     'L3_ffn_shared_w2': 8.0}
    for name, (base, spread) in spreads.items():
        noise = np.random.default_rng([zlib.crc32(name.encode()), seed]).standard_normal(out[name].shape)
        drawn = base * np.exp(spread * noise) if base else spread * noise
        out[name] = jnp.asarray(drawn.astype(out[name].dtype))
    for name, factor in factors.items():
        out[name] = (out[name] * factor).astype(out[name].dtype)
    return out
```

```python
from contextlib import ExitStack, contextmanager

import numpy as np
import concourse.bass as bass
from concourse import mybir
from concourse.alu_op_type import AluOpType as ALU

ACT = mybir.ActivationFunctionType
AX = mybir.AxisListType
F32, BF16, U32, I32 = mybir.dt.float32, mybir.dt.bfloat16, mybir.dt.uint32, mybir.dt.int32

P = 128
D = 128
NB, L = 16, 256
QT = L // P
NT = NB * QT
HEADS = 16
DI, NS, DTR, CONV = 256, 16, 8, 4
CI = DI // P
E0, H0 = 32, 512
A1 = 64
I1, BLK = 352, 16
E2, H2, CAP = 8, 512, NB * L // 16
E3, SH3, H3 = 8, 2, 64
EPS = 1e-5
NEG = -1e30


class Mark:

    def __init__(self, stream, off, turn):
        self.stream, self.off, self.turn = stream, off, turn


class Stream:

    def __init__(self, core, eng, name, step=1):
        self.core, self.eng, self.name, self.step = core, eng, name, step
        self.sem = core.nc.alloc_semaphore("s_" + name)
        self.base = self.off = 0
        self.waited = {}
        core.streams.append(self)

    def need(self, mark):
        core = self.core
        if mark is None:
            return
        if mark.turn == core.turn:
            if self.waited.get(mark.stream.name, 0) >= mark.off:
                return
            self.waited[mark.stream.name] = mark.off
            self.eng.wait_ge(mark.stream.sem, core.value(mark.stream, mark.off, 0))
        else:
            self.eng.wait_ge(mark.stream.sem, core.value(mark.stream, mark.off, 1))

    def needs(self, marks):
        for m in marks:
            if isinstance(m, (list, tuple)):
                self.needs(m)
            else:
                self.need(m)

    def do(self, issue, *marks):
        self.needs(marks)
        issue(self.eng).then_inc(self.sem, self.step)
        self.off += self.step
        return Mark(self, self.off, self.core.turn)

    def quiet(self, issue, *marks):
        self.needs(marks)
        issue(self.eng)

    def last(self):
        return Mark(self, self.off, self.core.turn) if self.off else None


class Slot:

    def __init__(self, core, name, tensor):
        self.core, self.name, self.t, self.back = core, name, tensor, None
        core.slots.append(self)

    def __getitem__(self, key):
        return self.t[key]

    def handed_back(self):
        if self.back is not None:
            return self.back
        return [Mark(self.core.by_name[s], off, "before")
                for s, off in self.core.turn_ends.get((self.core.loop_name, self.name), [])]

    def hand_back(self, *marks):
        self.back = [m for m in marks if m is not None]


class Core:
    def __init__(self, nc, turn_ends):
        self.nc, self.turn_ends = nc, turn_ends
        self.streams, self.slots, self.loop_name, self.i, self.turn = [], [], None, None, 0
        self.pe = Stream(self, nc.tensor, "pe")
        self.ve = Stream(self, nc.vector, "ve")
        self.ac = Stream(self, nc.scalar, "ac")
        self.po = Stream(self, nc.gpsimd, "po")
        self.by_name = {s.name: s for s in self.streams}

    def dma_stream(self, eng, name):
        s = Stream(self, eng, name, 16)
        self.by_name[name] = s
        return s

    def value(self, stream, off, back):
        if self.loop_name is None:
            return stream.base + off
        per = self.turn_ends.get((self.loop_name, "per", stream.name), 0)
        return stream.base + per * (1 - back) + off + self.i * per

    def join(self):
        for eng in (self.nc.tensor, self.nc.vector, self.nc.scalar, self.nc.gpsimd, self.nc.sync):
            for s in self.streams:
                if s.base + s.off:
                    eng.wait_ge(s.sem, s.base + s.off)
        self.fresh()

    def fresh(self):
        self.turn += 1
        for s in self.streams:
            s.base, s.off, s.waited = s.base + s.off, 0, {}
        for b in self.slots:
            b.back = None

    def loop(self, name, n, body, tables="natural_log_exp_and_others"):
        self.join()
        pers = {s.name: self.turn_ends.get((name, "per", s.name), 0) for s in self.streams}
        for s in self.streams:
            if pers[s.name]:
                self.nc.sync.nop().then_inc(s.sem, pers[s.name])
        self.loop_name = name
        self.nc.scalar.preload_act_table_set(tables)
        with self.nc.Fori(0, n) as i:
            self.i = i
            body(i)
        self.loop_name = None
        for b in self.slots:
            if b.back is not None:
                self.turn_ends[(name, b.name)] = [(m.stream.name, m.off) for m in b.back]
        for s in self.streams:
            self.turn_ends[(name, "per", s.name)] = s.off
            s.base, s.off = s.base + s.off * n + pers[s.name], 0
        self.fresh()
        self.join()


def bcast(ap, n, axis):
    ap = ap.unsqueeze(axis)
    shape = list(ap.shape)
    shape[axis] = n
    return ap.broadcast_to(tuple(shape))


class Program:
    def __init__(self, nc, turn_ends, ins, packed, out, debug):
        self.nc, self.ins, self.packed, self.out, self.debug = nc, ins, packed, out, debug
        c = self.c = Core(nc, turn_ends)
        self.pe, self.ve, self.ac, self.po = c.pe, c.ve, c.ac, c.po
        self.load = c.dma_stream(nc.sync, "load")
        self.stack, self.taken = ExitStack(), 0
        self.X = self.sb("X", [P, NT, D])
        self.bank = [Slot(c, f"bank{i}", nc.alloc_psum_tensor(f"bank{i}", [P, 512], F32)) for i in range(8)]
        self.pack = {}
        self.w = {}

    @contextmanager
    def scope(self):
        outer, self.stack = self.stack, ExitStack()
        with self.stack:
            yield
            self.c.join()
        self.stack = outer

    def sb(self, name, shape, dt=F32):
        self.taken += 1
        return self.stack.enter_context(self.nc.sbuf_tensor(f"{name}_{self.taken}", shape, dt))

    def slot(self, name, shape, dt=F32):
        return Slot(self.c, name, self.sb(name, shape, dt))

    def load_all(self):
        ld = self.load
        ld.do(lambda e: e.dma_start(self.X[:, :, :], self.ins["x"].rearrange("(t p) d -> p t d", p=P)))
        self.dummy = self.sb("dummy", [P, 4])
        self.dummy_ve, self.dummy_po = Slot(self.c, "dummy_ve", None), Slot(self.c, "dummy_po", None)
        self.ve.do(lambda e: e.memset(self.dummy[:, :], 0.0))
        self.load_packs("wf")
        w, ve = self.w, self.ve
        small = {n: self.sb(n, [P, k], BF16) for n, k in (("identb", P), ("mask0", P), ("mask1", L), ("upto", P), ("onesb", P))}
        sel = self.sb("selb", [96, 2 * NS, P], BF16)
        with self.scope():
            self.load_packs("wb")
            for n, t in small.items():
                ve.do(lambda e: e.tensor_copy(t[:, :], w[n]))
                w[n] = t[:, :]
            ve.do(lambda e: e.tensor_copy(sel[:, :, :], bcast(w["sel"], P, 2)))
            w["sel"] = sel[:, :, :]

    def load_packs(self, *names):
        ld, marks = self.load, []
        for pname in names:
            width, parts = self.packed[pname]
            t = self.sb("pack_" + pname, [P, width])
            marks.append(ld.do(lambda e: e.dma_start(t[:, :], self.ins[pname])))
            for name, (o, rows, shape) in parts.items():
                n = int(np.prod(shape))
                ap = t[0:rows, o:o + n]
                if len(shape) == 2:
                    ap = ap.rearrange("p (a b) -> p a b", a=shape[0])
                if len(shape) == 3:
                    ap = ap.rearrange("p (a b c) -> p a b c", a=shape[0], b=shape[1])
                self.w[name] = ap
        self.c.join()

    def gate(self, *marks):
        self.dummy_ve.hand_back(self.ve.do(lambda e: e.tensor_copy(self.dummy[:, 0:1], self.dummy[:, 1:2]),
                                      self.dummy_ve.handed_back(), *marks))

    def gate_po(self, *marks):
        self.dummy_po.hand_back(self.po.do(lambda e: e.tensor_tensor(self.dummy[:, 2:3], self.dummy[:, 3:4],
                                                                self.dummy[:, 3:4], ALU.add), self.dummy_po.handed_back(), *marks))

    def alloc_common(self, layer):
        self.xs = self.slot("xs", [P, QT, D])
        self.xn = self.slot("xn", [P, QT, D])
        self.xnT = self.slot("xnT", [P, L])
        self.stats = self.slot("stats", [P, QT, 6])
        self.mv = self.slot("mv", [P, QT, 2])
        self.lnv = self.slot("lnv", [P, QT])
        self.rstd = self.slot("rstd", [P, QT])
        if layer == 3:
            return
        g, hd = (8, A1) if layer == 1 else (4, 8)
        self.qT = self.slot("qT", [P, g, L])
        self.kT = self.slot("kT", [P, 1 if layer == 0 else g, L])
        self.v = self.slot("v", [P, QT, HEADS * hd])
        self.mx = [self.slot(f"mx{i}", [P, 4]) for i in range(2)]
        self.nb = [self.slot(f"nb{i}", [P, 4]) for i in range(2)]
        self.pr = [self.slot(f"pr{i}", [P, 512]) for i in range(2)]
        self.prT = [self.slot(f"prT{i}", [P, 512]) for i in range(2)]
        self.sums = [self.slot(f"sums{i}", [P, HEADS]) for i in range(QT)]
        self.rsum = [self.slot(f"rsum{i}", [P, HEADS]) for i in range(QT)]
        self.o = [self.slot(f"o{i}", [P, HEADS * hd]) for i in range(QT)]
        self.oT = [self.slot(f"oT{i}", [P, HEADS * hd // P, P]) for i in range(QT)]
        self.x1 = self.slot("x1", [P, QT, D])

    def layer_norm(self, b, src=None, ready=None):
        ve, ac, pe = self.ve, self.ac, self.pe
        if src is None:
            self.gate(self.xs.handed_back(), ready)
            t = ve.do(lambda e: e.tensor_copy(self.xs[:, :, :], self.X[:, bass.ds(b * QT, QT), :]))
            src = self.xs
        else:
            t = ready
        for q in range(QT):
            t1 = ve.do(lambda e: e.bn_stats(self.stats[:, q, :], src[:, q, :]), t)
        self.gate(t1, self.mv.handed_back())
        for q in range(QT):
            t2 = ve.do(lambda e: e.bn_aggr(self.mv[:, q, :], self.stats[:, q, :]))
        t3 = ac.do(lambda e: e.activation(self.lnv[:, :], self.mv[:, :, 1], ACT.Ln, bias=self.w["eps"], scale=1.0), t2)
        t4 = ac.do(lambda e: e.activation(self.rstd[:, :], self.lnv[:, :], ACT.Exp, scale=-0.5), t3, self.rstd.handed_back())
        for q in range(QT):
            t5 = ve.do(lambda e: e.tensor_scalar(self.xn[:, q, :], src[:, q, :], self.mv[:, q, 0:1],
                                                 self.rstd[:, q:q + 1], ALU.subtract, ALU.mult), t4, self.xn.handed_back())
        self.mv.hand_back(t3, t5)
        self.rstd.hand_back(t5)
        self.xs.hand_back(t5)
        bk = self.bank[7]
        for q in range(QT):
            t6 = pe.do(lambda e: e.transpose(bk[:, q * P:(q + 1) * P], self.xn[:, q, :], self.w["ident"]), t5, bk.handed_back())
        t7 = ac.do(lambda e: e.activation(self.xnT[:, :], bk[:, 0:L], ACT.Copy), t6, self.xnT.handed_back())
        bk.hand_back(t7)
        self.xn.hand_back(t6)
        return t5, t7

    def attention(self, layer, txnT):
        ve, ac, pe, w = self.ve, self.ac, self.pe, self.w
        hd = A1 if layer == 1 else 8
        scale = float(hd) ** -0.5
        groups, rows = (8, 64) if layer == 1 else (4, 32)
        per = P // rows
        kg = 1 if layer == 0 else groups
        wq, wk, wv = w[f"wq{layer}"], w[f"wk{layer}"], w[f"wv{layer}"]
        bq, bk_, bv = w[f"bq{layer}"], w[f"bk{layer}"], w[f"bv{layer}"]
        nv = 8 if layer == 0 else HEADS * hd
        turn = 0
        tq = None
        for dst, wt, bias, n in ((self.qT, wq, bq, groups), (self.kT, wk, bk_, kg)):
            for g in range(n):
                if g % 2 == 0:
                    bk = self.bank[turn % 4]
                    turn += 1
                o = (g % 2) * L
                t = pe.do(lambda e: e.matmul(bk[:, o:o + L], wt[:, g, :], self.xnT[:, :], start=True, stop=True),
                          txnT, bk.handed_back() if g % 2 == 0 else None)
                if g % 2 or g == n - 1:
                    ts = []
                    for gg in range(g - g % 2, g + 1):
                        oo = (gg % 2) * L
                        eng = ac if turn % 2 == 0 else ve
                        if eng is ac:
                            tq = ac.do(lambda e: e.activation(dst[:, gg, :], bk[:, oo:oo + L], ACT.Identity,
                                                              bias=bias[:, gg:gg + 1]), t, dst.handed_back())
                        else:
                            tq = ve.do(lambda e: e.tensor_scalar(dst[:, gg, :], bk[:, oo:oo + L], bias[:, gg:gg + 1],
                                                                 None, ALU.add), t, dst.handed_back())
                        ts.append(tq)
                    bk.hand_back(*ts)
        tqa, tqv = ac.last(), ve.last()
        for q in range(QT):
            for c0 in range(0, nv, 512):
                cn = min(512, nv - c0)
                bk = self.bank[turn % 4]
                turn += 1
                t = pe.do(lambda e: e.matmul(bk[:, 0:cn], self.xnT[:, q * P:(q + 1) * P], wv[:, c0:c0 + cn],
                                             start=True, stop=True), bk.handed_back())
                tv = ve.do(lambda e: e.tensor_tensor(self.v[:, q, c0:c0 + cn], bk[:, 0:cn], bv[:, c0:c0 + cn],
                                                     ALU.add), t, self.v.handed_back())
                bk.hand_back(tv)
        self.xnT.hand_back(t)
        yield

        order = sorted(range(HEADS), key=lambda h: (h % per, h))
        units = [(0, order[4 * u:4 * u + 4]) for u in range(4)] + [(1, order[2 * u:2 * u + 2]) for u in range(8)]
        sc, tr = self.bank[0:2], self.bank[2:4]
        opb = [self.bank[4], self.bank[5]]
        t_exp, t_sc, t_pT, t_pv = {}, {}, {}, {}
        touched = set()

        def scores(u):
            q, heads = units[u]
            bk = sc[u % 2]
            wid = P * (q + 1)
            for n, h in enumerate(heads):
                r = rows * (h % per)
                kk = 0 if layer == 0 else h // per
                dst = bk[:, n * wid:(n + 1) * wid]
                pe.quiet(lambda e: e.matmul(dst, w["identb"], w[f"mask{q}"][:, 0:wid], start=True, stop=False),
                         bk.handed_back() if n == 0 else None, tqa, tqv)
                f = lambda e: e.matmul(dst, self.qT[r:r + hd, h // per, q * P:(q + 1) * P],
                                       self.kT[r:r + hd, kk, 0:wid], start=False, stop=True)
                if n == len(heads) - 1:
                    t_sc[u] = pe.do(f)
                else:
                    pe.quiet(f)

        def softmax(u):
            q, heads = units[u]
            bk, nh, wid = sc[u % 2], len(heads), P * (q + 1)
            mx, nb, pr = self.mx[u % 2], self.nb[u % 2], self.pr[u % 2]
            v3 = bk[:, :].rearrange("p (h k) -> p h k", h=nh)
            t = ve.do(lambda e: e.tensor_reduce(mx[:, 0:nh], v3, AX.X, ALU.max), t_sc[u])
            t = ve.do(lambda e: e.tensor_scalar(nb[:, 0:nh], mx[:, 0:nh], -scale, None, ALU.mult), t, nb.handed_back())
            for n, h in enumerate(heads):
                te = ac.do(lambda e: e.activation(pr[:, n * wid:(n + 1) * wid], bk[:, n * wid:(n + 1) * wid], ACT.Exp,
                                                  bias=nb[:, n:n + 1], scale=scale,
                                                  accum_out=self.sums[q][:, h:h + 1]),
                           t, pr.handed_back(), self.sums[q].handed_back() if h == 0 else None)
            nb.hand_back(te)
            bk.hand_back(te)
            t_exp[u] = te

        def turn_p(u):
            bk, pr, prT = tr[u % 2], self.pr[u % 2], self.prT[u % 2]
            for j in range(3):
                pe.quiet(lambda e: e.transpose(bk[:, j * P:(j + 1) * P], pr[:, j * P:(j + 1) * P], w["ident"]),
                         bk.handed_back(), t_exp[u])
            t = pe.do(lambda e: e.transpose(bk[:, 3 * P:], pr[:, 3 * P:], w["ident"]))
            pr.hand_back(t)
            if u % 3 == 2:
                t = ac.do(lambda e: e.activation(prT[:, :], bk[:, :], ACT.Copy), t, prT.handed_back())
            else:
                t = ve.do(lambda e: e.tensor_copy(prT[:, :], bk[:, :]), t, prT.handed_back())
            bk.hand_back(t)
            t_pT[u] = t

        def values(u):
            q, heads = units[u]
            prT = self.prT[u % 2]
            for n, h in enumerate(heads):
                if hd == 8:
                    ob, oc = opb[q], h * 8
                else:
                    ob, oc = opb[h // 8], (h % 8) * 64
                first = (q, ob.name) not in touched
                touched.add((q, ob.name))
                vc = 0 if layer == 0 else h * hd
                for kb in range(q + 1):
                    blk = n * (q + 1) + kb
                    f = lambda e: e.matmul(ob[:, oc:oc + hd], prT[:, blk * P:(blk + 1) * P],
                                           self.v[:, kb, vc:vc + hd], start=kb == 0, stop=kb == q)
                    fr = ob.handed_back() if first and kb == 0 else None
                    if kb == q and n == len(heads) - 1:
                        t_pv[u] = pe.do(f, t_pT[u], tv, fr)
                    else:
                        pe.quiet(f, t_pT[u], tv, fr)
            prT.hand_back(t_pv[u])

        def finish(q, t):
            o, oT, rs = self.o[q], self.oT[q], self.rsum[q]
            t1 = ve.do(lambda e: e.reciprocal(rs[:, :], self.sums[q][:, :]), t_exp[3 if q == 0 else 11])
            self.sums[q].hand_back(t1)
            nb_ = 1 if hd == 8 else 2
            ts = []
            for i in range(nb_):
                ob = opb[q] if hd == 8 else opb[i]
                hs = HEADS // nb_
                ov = o[:, i * hs * hd:(i + 1) * hs * hd].rearrange("p (h d) -> p h d", h=hs)
                pv = ob[:, 0:hs * hd].rearrange("p (h d) -> p h d", h=hs)
                t2 = ve.do(lambda e: e.tensor_tensor(ov, pv, bcast(rs[:, i * hs:(i + 1) * hs], hd, 2), ALU.mult),
                           t1, t, o.handed_back())
                ob.hand_back(t2)
            nch = HEADS * hd // P
            for c0 in range(0, nch, 4):
                cn = min(4, nch - c0)
                bk = tr[(c0 // 4) % 2] if hd != 8 else self.bank[6]
                for ch in range(c0, c0 + cn):
                    t3 = pe.do(lambda e: e.transpose(bk[:, (ch - c0) * P:(ch - c0 + 1) * P], o[:, ch * P:(ch + 1) * P],
                                                     w["ident"]), t2, bk.handed_back())
                ts = ac.do(lambda e: e.activation(oT[:, c0:c0 + cn, :].rearrange("p c t -> p (c t)"),
                                                  bk[:, 0:cn * P], ACT.Copy), t3, oT.handed_back())
                bk.hand_back(ts)
            o.hand_back(t3)
            return ts

        t_o = {}
        n_u = len(units)
        scores(0)
        for u in range(n_u + 2):
            if u + 1 < n_u:
                scores(u + 1)
            if u < n_u:
                softmax(u)
            if 1 <= u <= n_u:
                turn_p(u - 1)
            if u >= 2:
                values(u - 2)
            if u == 5:
                t_o[0] = finish(0, t_pv[3])
            yield
        t_o[1] = finish(1, t_pv[n_u - 1])
        self.qT.hand_back(t_sc[n_u - 1])
        self.kT.hand_back(t_sc[n_u - 1])
        self.v.hand_back(t_pv[n_u - 1])
        nch = HEADS * hd // P
        bk = self.bank[6]
        for q in range(QT):
            for ch in range(nch):
                f = lambda e: e.matmul(bk[:, q * P:(q + 1) * P], self.oT[q][:, ch, :], w[f"wo{layer}"][:, ch, :],
                                       start=ch == 0, stop=ch == nch - 1)
                t = pe.do(f, t_o[q], bk.handed_back() if q == 0 and ch == 0 else None)
            self.oT[q].hand_back(t)
        t1 = ve.do(lambda e: e.tensor_tensor(self.x1[:, :, :], bk[:, 0:L].rearrange("p (q d) -> p q d", q=QT),
                                             bcast(w[f"bo{layer}"], QT, 1), ALU.add), t, self.x1.handed_back())
        bk.hand_back(t1)
        self.t_x1 = t1

    def sigmoid_times(self, out, z, tmp, ready, free, z_is_psum_ok=True):
        t = self.ac.do(lambda e: e.activation(tmp, z, ACT.Exp, scale=-1.0), ready)
        t = self.ve.do(lambda e: e.tensor_scalar(tmp, tmp, 1.0, None, ALU.add), t)
        t = self.ve.do(lambda e: e.reciprocal(tmp, tmp), t)
        return self.ve.do(lambda e: e.tensor_tensor(out, z, tmp, ALU.mult), t, free)

    def add_to_x(self, b, src, ready):
        xv = self.X[:, bass.ds(b * QT, QT), :]
        return self.ve.do(lambda e: e.tensor_tensor(xv, xv, src, ALU.add), ready, self.ve.last())

    def alloc_scan(self, CI):
        self.zin = self.slot("zin", [P, CI, L])
        self.zab = self.slot("zab", [P, CI, L])
        self.zmx = self.slot("zmx", [P, CI, L])
        self.delta = self.slot("delta", [P, CI, L])
        self.dtu = self.slot("dtu", [P, CI, L])
        self.split = self.slot("split", [96, L], BF16)
        self.sx = self.slot("sx", [96, L])
        self.sr = self.slot("sr", [96, L])
        self.sh = self.slot("sh", [96, L], BF16)
        self.dA = [self.slot(f"dA{i}", [P, NS, L]) for i in range(CI)]
        self.h = [self.slot(f"h{i}", [P, NS, L]) for i in range(CI)]
        self.Crep = self.slot("Crep", [P, NS, L])
        self.yT = self.slot("yT", [P, CI, L])

    def softplus(self, n, ready):
        ve, ac = self.ve, self.ac
        z, a, m, dl = (x[:, 0:n, :] for x in (self.zin, self.zab, self.zmx, self.delta))
        t = ac.do(lambda e: e.activation(a, z, ACT.Abs), ready)
        t = ac.do(lambda e: e.activation(a, a, ACT.Exp, scale=-1.0), t)
        t = ac.do(lambda e: e.activation(a, a, ACT.Ln, bias=1.0), t)
        t1 = ve.do(lambda e: e.tensor_scalar(m, z, 0.0, None, ALU.max), ready)
        return ve.do(lambda e: e.tensor_tensor(dl, a, m, ALU.add), t, t1, self.delta.handed_back())

    def split3(self, ps, ready):
        ve = self.ve
        t0 = ve.do(lambda e: e.tensor_copy(self.sx[:, :], ps), ready)
        t = ve.do(lambda e: e.tensor_copy(self.sh[:, :], self.sx[:, :]), t0)
        t1 = ve.do(lambda e: e.tensor_copy(self.split[0:32, :], self.sh[0:32, :]), t, self.split.handed_back())
        t = ve.do(lambda e: e.tensor_tensor(self.sr[:, :], self.sx[:, :], self.sh[:, :], ALU.subtract), t)
        t = ve.do(lambda e: e.tensor_copy(self.sh[:, :], self.sr[:, :]), t)
        t1 = ve.do(lambda e: e.tensor_copy(self.split[32:64, :], self.sh[32:64, :]), t)
        t = ve.do(lambda e: e.tensor_tensor(self.sr[:, :], self.sr[:, :], self.sh[:, :], ALU.subtract), t)
        t = ve.do(lambda e: e.tensor_copy(self.split[64:96, :], self.sr[64:96, :]), t)
        return t0, t

    def scan(self, nch, A, u_ap, t_u, t_delta, t_split, banks, bank_y):
        ve, ac, pe, po, w = self.ve, self.ac, self.pe, self.po, self.w
        t_dtu = ve.do(lambda e: e.tensor_tensor(self.dtu[:, 0:nch, :], self.delta[:, 0:nch, :], u_ap, ALU.mult),
                      t_delta, t_u)
        t_dA = [None] * nch
        for c in range(nch):
            for n in range(NS):
                t = ac.do(lambda e: e.activation(self.dA[c][:, n, :], self.delta[:, c, :], ACT.Exp,
                                                 scale=A[:, c, n:n + 1]), t_delta, self.dA[c].handed_back() if n == 0 else None)
            self.gate_po(t)
            t_dA[c] = po.do(lambda e: e.memset(self.dA[c][:, :, 0:1], 0.0))
            yield
        self.delta.hand_back(ac.last(), t_dtu)
        for n in range(0, NS, 2):
            bk = banks[(n // 2) % 2]
            for j in range(2):
                t = pe.do(lambda e: e.matmul(bk[:, j * L:(j + 1) * L], w["sel"][:, n + j, :], self.split[:, :],
                                             start=True, stop=True), t_split, bk.handed_back() if j == 0 else None)
            for c in range(nch):
                t1 = ve.do(lambda e: e.tensor_tensor(self.h[c][:, n:n + 2, :], bcast(self.dtu[:, c, :], 2, 1),
                                                     bk[:, :].rearrange("p (n t) -> p n t", n=2), ALU.mult),
                           t, t_dtu, self.h[c].handed_back() if n == 0 else None)
            bk.hand_back(t1)
        self.dtu.hand_back(t1)
        yield
        for n in range(0, NS, 2):
            bk = banks[(n // 2) % 2]
            for j in range(2):
                t = pe.do(lambda e: e.matmul(bk[:, j * L:(j + 1) * L], w["sel"][:, NS + n + j, :], self.split[:, :],
                                             start=True, stop=True), bk.handed_back() if j == 0 else None)
            tC = ac.do(lambda e: e.activation(self.Crep[:, n:n + 2, :].rearrange("p n t -> p (n t)"), bk[:, :], ACT.Copy),
                       t, self.Crep.handed_back() if n == 0 else None)
            bk.hand_back(tC)
        self.split.hand_back(t)
        yield
        NG = 4
        for c in range(nch):
            hv = self.h[c]
            for g in range(0, NS, NG):
                f = lambda x: x[:, g:g + NG, :].rearrange("p n t -> p (n t)")
                t = ve.do(lambda e: e.tensor_tensor_scan(f(hv), f(self.dA[c]), f(hv), 0.0, ALU.mult, ALU.add),
                          t_dA[c], t1)
                th = po.do(lambda e: e.tensor_tensor(hv[:, g:g + NG, :], hv[:, g:g + NG, :], self.Crep[:, g:g + NG, :],
                                                     ALU.mult), t, tC)
                for n in range(g, g + NG):
                    tp = pe.do(lambda e: e.matmul(bank_y[:, c * L:(c + 1) * L], w["ident"], hv[:, n, :],
                                                  start=n == 0, stop=n == NS - 1), th,
                               bank_y.handed_back() if n == 0 and c == 0 else None)
                yield
            self.dA[c].hand_back(t)
            hv.hand_back(tp)
        self.Crep.hand_back(th)
        self.t_scan = tp

    def alloc0(self):
        self.x1T = self.slot("x1T", [P, L])
        self.upad = self.sb("upad", [P, CI, CONV - 1 + L])
        self.upadb = Slot(self.c, "upadb", self.upad)
        self.sg = self.slot("sg", [P, CI, L])
        self.sgt = self.slot("sgt", [P, CI, L])
        self.cv = self.slot("cv", [P, CI, L])
        self.cvt = self.slot("cvt", [P, CI, L])
        self.u = self.slot("u", [P, CI, L])
        self.dtT = self.slot("dtT", [DTR, L])
        self.gz = self.slot("gz", [E0, L])
        self.gs = self.slot("gs", [E0, 4])
        self.gp = self.slot("gp", [E0, L])
        self.g8 = self.slot("g8", [E0, 8])
        self.gr = self.slot("gr", [E0, L])
        self.gv = self.slot("gv", [P, L])
        self.gvT = self.slot("gvT", [P, QT, E0])

    def gate0(self, b, txn, txnT):
        ve, ac, pe, w = self.ve, self.ac, self.pe, self.w
        bk = self.bank[7]
        t = pe.do(lambda e: e.matmul(bk[0:E0, 0:L], w["gate_w"], self.xnT[:, :], start=True, stop=True), txnT, bk.handed_back())
        self.xnT_gate = t
        t = ve.do(lambda e: e.tensor_scalar(self.gz[:, :], bk[0:E0, 0:L], w["gate_b"], None, ALU.add), t)
        bk.hand_back(t)
        t = ve.do(lambda e: e.tensor_reduce(self.gs[:, 0:1], self.gz[:, :], AX.X, ALU.max), t)
        t = ve.do(lambda e: e.tensor_scalar(self.gs[:, 1:2], self.gs[:, 0:1], -1.0, None, ALU.mult), t)
        t = ac.do(lambda e: e.activation(self.gp[:, :], self.gz[:, :], ACT.Exp, bias=self.gs[:, 1:2],
                                         accum_out=self.gs[:, 2:3]), t)
        t = ve.do(lambda e: e.reciprocal(self.gs[:, 3:4], self.gs[:, 2:3]), t)
        t = ve.do(lambda e: e.tensor_scalar(self.gp[:, :], self.gp[:, :], self.gs[:, 3:4], None, ALU.mult), t)
        self.gate(t)
        t = ve.do(lambda e: e.max(self.g8[:, :], self.gp[:, :]))
        self.gate(t)
        t = ve.do(lambda e: e.match_replace(self.gr[:, :], self.g8[:, :], self.gp[:, :], 0.0))
        t = ve.do(lambda e: e.tensor_tensor(self.gv[0:E0, :], self.gp[:, :], self.gr[:, :], ALU.subtract), t, self.gv.handed_back())
        ve.do(lambda e: e.tensor_copy(self.PT[:, bass.ds(b, 1), :].rearrange("p a t -> p (a t)"), self.gv[0:E0, :]), t)
        yield
        for q in range(QT):
            t1 = pe.do(lambda e: e.transpose(bk[:, q * P:(q + 1) * P], self.gv[:, q * P:(q + 1) * P], w["ident"]),
                       t, bk.handed_back())
        self.gv.hand_back(t1)
        t1 = ve.do(lambda e: e.tensor_copy(self.gvT[:, :, :], bk[:, 0:L].rearrange("p (q e) -> p q e", q=QT)[:, :, 0:E0]), t1,
                   self.gvT.handed_back())
        bk.hand_back(t1)
        for q in range(QT):
            t2 = pe.do(lambda e: e.matmul(bk[:, 256:256 + E0], self.xn[:, q, :], self.gvT[:, q, :], start=q == 0,
                                          stop=q == QT - 1), t1, txn)
        self.gvT.hand_back(t2)
        self.xn_gate = t2
        t2 = ve.do(lambda e: e.tensor_copy(self.merged[:, :, bass.ds(b, 1)],
                                           bk[:, 256:256 + E0].rearrange("p (e o) -> p e o", o=1)), t2)
        bk.hand_back(t2)

    def mamba(self, b, t_x1):
        ve, ac, pe, w = self.ve, self.ac, self.pe, self.w
        B5, B6, B7 = self.bank[5], self.bank[6], self.bank[7]
        for q in range(QT):
            t = pe.do(lambda e: e.transpose(B7[:, q * P:(q + 1) * P], self.x1[:, q, :], w["ident"]), t_x1, B7.handed_back())
        t = ve.do(lambda e: e.tensor_copy(self.x1T[:, :], B7[:, 0:L]), t, self.x1T.handed_back())
        B7.hand_back(t)
        for part, bk in ((0, B5), (1, B6)):
            for c in range(CI):
                tp = pe.do(lambda e: e.matmul(bk[:, c * L:(c + 1) * L], w["w_in"][:, part * CI + c, :], self.x1T[:, :],
                                              start=True, stop=True), t, bk.handed_back() if c == 0 else None)
            if part == 0:
                t0 = ac.do(lambda e: e.activation(self.upad[:, :, CONV - 1:], bk[:, :].rearrange("p (c t) -> p c t", c=CI),
                                                  ACT.Copy), tp, self.upadb.handed_back())
                bk.hand_back(t0)
            else:
                z = bk[:, :].rearrange("p (c t) -> p c t", c=CI)
                tg = self.sigmoid_times(self.sg[:, :, :], z, self.sgt[:, :, :], tp, self.sg.handed_back())
                bk.hand_back(tg)
        self.x1T.hand_back(tp)
        yield
        for c in range(CI):
            t = ve.do(lambda e: e.tensor_scalar(self.cv[:, c, :], self.upad[:, c, 0:L], w["conv_w"][:, c, 0:1],
                                                w["conv_b"][:, c:c + 1], ALU.mult, ALU.add), t0)
            for j in range(1, CONV):
                t = ve.do(lambda e: e.scalar_tensor_tensor(self.cv[:, c, :], self.upad[:, c, j:j + L],
                                                           w["conv_w"][:, c, j:j + 1], self.cv[:, c, :], ALU.mult,
                                                           ALU.add), t)
        self.upadb.hand_back(t)
        tu = self.sigmoid_times(self.u[:, :, :], self.cv[:, :, :], self.cvt[:, :, :], t, self.u.handed_back())
        yield
        for c in range(CI):
            t = pe.do(lambda e: e.matmul(B5[0:96, 0:L], w["w_bc"][:, c, :], self.u[:, c, :], start=c == 0,
                                         stop=c == CI - 1), tu, B5.handed_back())
        for c in range(CI):
            t = pe.do(lambda e: e.matmul(B6[0:DTR, 0:L], w["w_dtin"][:, c, :], self.u[:, c, :], start=c == 0,
                                         stop=c == CI - 1), B6.handed_back())
        td = ve.do(lambda e: e.tensor_copy(self.dtT[:, :], B6[0:DTR, 0:L]), t)
        B6.hand_back(td)
        t0, t_split = self.split3(B5[0:96, 0:L], t)
        B5.hand_back(t0)
        for c in range(CI):
            t = pe.do(lambda e: e.matmul(B6[:, c * L:(c + 1) * L], w["w_dt"][:, c * P:(c + 1) * P], self.dtT[:, :],
                                         start=True, stop=True), td, B6.handed_back() if c == 0 else None)
        for c in range(CI):
            tz = ve.do(lambda e: e.tensor_scalar(self.zin[:, c, :], B6[:, c * L:(c + 1) * L], w["b_dt"][:, c:c + 1],
                                                 None, ALU.add), t)
        B6.hand_back(tz)
        t_delta = self.softplus(CI, tz)
        yield
        yield from self.scan(CI, self.A0, self.u[:, :, :], tu, t_delta, t_split, (B5, B6), B7)
        for c in range(CI):
            t = ve.do(lambda e: e.scalar_tensor_tensor(self.yT[:, c, :], self.u[:, c, :], w["Dp"][:, c:c + 1],
                                                       B7[:, c * L:(c + 1) * L], ALU.mult, ALU.add),
                      self.t_scan, self.yT.handed_back())
        B7.hand_back(t)
        self.u.hand_back(t)
        t = ve.do(lambda e: e.tensor_tensor(self.yT[:, :, :], self.yT[:, :, :], self.sg[:, :, :], ALU.mult), t, tg)
        for q in range(QT):
            for c in range(CI):
                tp = pe.do(lambda e: e.matmul(B5[:, q * P:(q + 1) * P], self.yT[:, c, q * P:(q + 1) * P],
                                              w["w_out"][:, c, :], start=c == 0, stop=c == CI - 1), t,
                           B5.handed_back() if q == 0 and c == 0 else None)
        self.yT.hand_back(tp)
        t = ve.do(lambda e: e.tensor_tensor(self.x1[:, :, :], self.x1[:, :, :],
                                            B5[:, 0:L].rearrange("p (q d) -> p q d", q=QT), ALU.add), tp)
        B5.hand_back(t)
        t = self.add_to_x(b, self.x1[:, :, :], t)
        self.x1.hand_back(t)

    def neg_exp(self, name, src, n):
        t = self.sb(name, [P, n, NS])
        m = self.ac.do(lambda e: e.activation(t[:, :, :], src, ACT.Exp))
        self.ve.do(lambda e: e.tensor_scalar(t[:, :, :], t[:, :, :], -1.0, None, ALU.mult), m)
        return t

    def layer0(self):
        ve = self.ve
        self.A0 = self.neg_exp("A0", self.w["A_log0"], CI)
        ve.do(lambda e: e.memset(self.upad[:, :, 0:CONV - 1], 0.0))
        ve.do(lambda e: e.memset(self.gv[:, :], 0.0))

        def body(b):
            txn, txnT = self.layer_norm(b)
            for _ in self.gate0(b, txn, txnT):
                pass
            for _ in self.attention(0, txnT):
                pass
            t = ve.do(lambda e: e.tensor_tensor(self.x1[:, :, :], self.x1[:, :, :], self.xn[:, :, :], ALU.add), self.t_x1)
            self.xn.hand_back(t, self.xn_gate)
            for _ in self.mamba(b, t):
                pass
        self.c.loop("layer0", NB, body)

    def experts0(self):
        ve, ac, pe, w, nc = self.ve, self.ac, self.pe, self.w, self.nc
        R = 4
        w1r = [self.slot(f"w1r{i}", [P, H0]) for i in range(R)]
        w2r = [self.slot(f"w2r{i}", [P, H0 // P, D]) for i in range(R)]
        hz = [self.slot(f"hz{i}", [P, H0 // P, NB]) for i in range(2)]
        hg = [self.slot(f"hg{i}", [P, H0 // P, NB]) for i in range(2)]
        lds = [(self.c.dma_stream(nc.sync, f"e0a{i}"), self.c.dma_stream(nc.sync, f"e0b{i}")) for i in range(R)]
        w1d = self.ins["m_w1"]
        w2d = self.ins["m_w2"]
        J = H0 // P

        def body(i):
            ld = []
            for s in range(R):
                ex = i * R + s
                la = lds[s][0].do(lambda e: e.dma_start(w1r[s][:, :], w1d[bass.ds(ex, 1), 0:D, :].rearrange("a p h -> (a p) h")), w1r[s].handed_back())
                lb = lds[s][1].do(lambda e: e.dma_start(w2r[s][:, :, :], w2d[bass.ds(ex, 1), 0:H0, :].rearrange("a (j p) d -> p (a j) d", p=P)), w2r[s].handed_back())
                ld.append((la, lb))
            for s in range(R):
                ex = i * R + s
                bk, bo = self.bank[s % 2], self.bank[2 + s % 2]
                for j in range(J):
                    t = pe.do(lambda e: e.matmul(bk[:, j * NB:(j + 1) * NB], w1r[s][:, j * P:(j + 1) * P],
                                                 self.merged[:, bass.ds(ex, 1), :].rearrange("p a b -> p (a b)"), start=True, stop=True),
                              ld[s][0], bk.handed_back())
                w1r[s].hand_back(t)
                b1v = w["m_b1"][:, bass.ds(ex, 1), :].rearrange("p a j -> p (a j)")
                t = ve.do(lambda e: e.tensor_tensor(hz[s % 2][:, :, :], bk[:, 0:J * NB].rearrange("p (j b) -> p j b", j=J),
                                                    bcast(b1v, NB, 2), ALU.add), t, hz[s % 2].handed_back())
                bk.hand_back(t)
                t = ac.do(lambda e: e.activation(hg[s % 2][:, :, :], hz[s % 2][:, :, :], ACT.Gelu), t, hg[s % 2].handed_back())
                hz[s % 2].hand_back(t)
                for j in range(J):
                    t1 = pe.do(lambda e: e.matmul(bo[:, 0:NB], w2r[s][:, j, :], hg[s % 2][:, j, :], start=j == 0,
                                                  stop=j == J - 1), t, ld[s][1], bo.handed_back())
                w2r[s].hand_back(t1)
                hg[s % 2].hand_back(t1)
                b2v = w["m_b2"][:, bass.ds(ex, 1)]
                t = ve.do(lambda e: e.tensor_tensor(self.oall[:, :, bass.ds(ex, 1)], bo[:, 0:NB].rearrange("p (b o) -> p b o", o=1),
                                                    bcast(b2v, NB, 1), ALU.add), t1)
                bo.hand_back(t)
        self.c.loop("experts0", E0 // R, body, "gelu_and_others")

    def spread0(self, b):
        ve, pe, w, po = self.ve, self.pe, self.w, self.po
        bk = self.bank[7]
        self.gate(self.ob.handed_back(), self.pts.handed_back())
        t = ve.do(lambda e: e.tensor_copy(self.ob[:, :], self.oall[:, bass.ds(b, 1), :].rearrange("p a e -> p (a e)")))
        tp = ve.do(lambda e: e.tensor_copy(self.pts[:, :], self.PT[:, bass.ds(b, 1), :].rearrange("p a t -> p (a t)")))
        t = pe.do(lambda e: e.transpose(bk[0:E0, 256:256 + D], self.ob[:, :], w["ident"]), t, bk.handed_back())
        self.ob.hand_back(t)
        t = ve.do(lambda e: e.tensor_copy(self.oe[:, :], bk[0:E0, 256:256 + D]), t, self.oe.handed_back())
        for q in range(QT):
            t1 = pe.do(lambda e: e.matmul(bk[:, q * P:(q + 1) * P], self.pts[:, q * P:(q + 1) * P], self.oe[:, :],
                                          start=True, stop=True), t, tp)
        self.oe.hand_back(t1)
        self.pts.hand_back(t1)
        t = self.add_to_x(b, bk[:, 0:L].rearrange("p (q d) -> p q d", q=QT), t1)
        bk.hand_back(t)
        return t

    def fp4(self, name, out, src, nblk, ready, free):
        ve, po = self.ve, self.po
        a, t_, wv_ = (x[:, 0:nblk, :] for x in self.f4)
        am, sc, hs = (x[:, 0:nblk] for x in self.f4s)
        ta = self.ac.do(lambda e: e.activation(a, src, ACT.Abs), ready, ve.last())
        t = ve.do(lambda e: e.tensor_reduce(am, src, AX.X, ALU.max, apply_absolute_value=True), ready)
        t = ve.do(lambda e: e.tensor_scalar(sc, am, float(np.float32(1.0) / np.float32(6.0)), 1e-12, ALU.mult, ALU.max), t)
        th = ve.do(lambda e: e.tensor_scalar(hs, sc, 0.5, None, ALU.mult), t)
        t = ve.do(lambda e: e.reciprocal(am, sc), t)
        t = ve.do(lambda e: e.tensor_tensor(a, a, bcast(am, BLK, 2), ALU.mult), t, ta)
        self.gate_po(t)
        t1 = po.do(lambda e: e.tensor_scalar(wv_, a, 1.75, None, ALU.is_gt))
        t = ve.do(lambda e: e.tensor_scalar(t_, a, 5.0, 2.0, ALU.is_gt, ALU.mult), t)
        for m in (3.5, 2.5):
            t = ve.do(lambda e: e.scalar_tensor_tensor(t_, a, m, t_, ALU.is_gt, ALU.add), t)
        t = ve.do(lambda e: e.scalar_tensor_tensor(t_, t_, 2.0, wv_, ALU.mult, ALU.add), t, t1)
        for m in (1.25, 0.75, 0.25):
            t = ve.do(lambda e: e.scalar_tensor_tensor(t_, a, m, t_, ALU.is_gt, ALU.add), t)
        t = ve.do(lambda e: e.tensor_tensor(t_, t_, bcast(hs, BLK, 2), ALU.mult), t)
        return ve.do(lambda e: e.scalar_tensor_tensor(out.bitcast(U32), src.bitcast(U32), 0x80000000, t_.bitcast(U32),
                                                      ALU.bitwise_and, ALU.bitwise_or), t, free)

    def layer1(self):
        ve, ac, pe, w = self.ve, self.ac, self.pe, self.w
        NBH = I1 // BLK
        self.f4 = [self.sb(f"f4{i}", [P, QT * NBH, BLK]) for i in range(3)]
        self.f4s = [self.sb(f"f4s{i}", [P, QT * NBH]) for i in range(3)]
        wqt = self.sb("wgu_q", [P, 6, P])
        wdq = self.sb("wd_q", [P, I1])
        wgT = self.sb("wgT", [P, I1])
        wuT = self.sb("wuT", [P, I1])
        wdT = self.sb("wdT", [P, 3, D])
        xq = self.slot("xq", [P, QT, D])
        xqT = self.slot("xqT", [P, L])
        hh = self.slot("hh", [P, QT, I1])
        he = self.slot("he", [P, I1])
        hq = self.slot("hq", [P, QT, I1])
        hqT = self.slot("hqT", [P, 3, L])
        blk = lambda ap: ap.rearrange("p (n k) -> p n k", k=BLK)
        B6, B7 = self.bank[6], self.bank[7]
        t = ve.last()
        raw = w["wgu1"]
        for i in range(6):
            t = self.fp4("w", blk(wqt[:, i, :]), blk(raw[:, i, :]), D // BLK, t, None)
        t = self.fp4("w", blk(wdq[:, :]), blk(w["wd1"]), NBH, t, None)
        for i in range(6):
            dst = wgT if i < 3 else wuT
            rows = min(P, I1 - (i % 3) * P)
            tp = pe.do(lambda e: e.transpose(B6[:, 0:rows], wqt[0:rows, i, :], w["ident"][0:rows, 0:rows]), t, B6.handed_back())
            tc = ve.do(lambda e: e.tensor_copy(dst[:, (i % 3) * P:(i % 3) * P + rows], B6[:, 0:rows]), tp)
            B6.hand_back(tc)
        for i in range(3):
            rows = min(P, I1 - i * P)
            tp = pe.do(lambda e: e.transpose(B6[0:rows, 0:P], wdq[:, i * P:i * P + rows], w["ident"]), t, B6.handed_back())
            tc = ve.do(lambda e: e.tensor_copy(wdT[0:rows, i, :], B6[0:rows, 0:P]), tp)
            B6.hand_back(tc)

        def ffn(b, txn):
            t = self.fp4("x", xq[:, :, :].rearrange("p q (n k) -> p (q n) k", k=BLK),
                         self.xn[:, :, :].rearrange("p q (n k) -> p (q n) k", k=BLK), QT * D // BLK, txn, xq.handed_back())
            self.xn.hand_back(t, pe.last())
            for q in range(QT):
                tp = pe.do(lambda e: e.transpose(B7[:, q * P:(q + 1) * P], xq[:, q, :], w["ident"]), t, B7.handed_back())
            xq.hand_back(tp)
            t = ac.do(lambda e: e.activation(xqT[:, :], B7[:, 0:L], ACT.Copy), tp, xqT.handed_back())
            B7.hand_back(t)
            yield
            for q in range(QT):
                tg = pe.do(lambda e: e.matmul(B6[:, 0:I1], xqT[:, q * P:(q + 1) * P], wgT[:, :], start=True, stop=True), t, B6.handed_back())
                tu = pe.do(lambda e: e.matmul(B7[:, 0:I1], xqT[:, q * P:(q + 1) * P], wuT[:, :], start=True, stop=True), B7.handed_back())
                ts = self.sigmoid_times(hh[:, q, :], B6[:, 0:I1], he[:, :], tg, None)
                B6.hand_back(ts)
                th = ve.do(lambda e: e.tensor_tensor(hh[:, q, :], hh[:, q, :], B7[:, 0:I1], ALU.mult), ts, tu)
                B7.hand_back(th)
                yield
            xqT.hand_back(tu)
            t = self.fp4("h", hq[:, :, :].rearrange("p q (n k) -> p (q n) k", k=BLK),
                         hh[:, :, :].rearrange("p q (n k) -> p (q n) k", k=BLK), QT * NBH, th, hq.handed_back())
            yield
            for ch in range(3):
                rows = min(P, I1 - ch * P)
                bk = B6 if ch % 2 == 0 else B7
                for q in range(QT):
                    tp = pe.do(lambda e: e.transpose(bk[0:rows, q * P:(q + 1) * P], hq[:, q, ch * P:ch * P + rows],
                                                     w["ident"]), t, bk.handed_back())
                tc = ac.do(lambda e: e.activation(hqT[0:rows, ch, :], bk[0:rows, 0:L], ACT.Copy), tp, hqT.handed_back())
                bk.hand_back(tc)
            hq.hand_back(tp)
            for q in range(QT):
                for ch in range(3):
                    rows = min(P, I1 - ch * P)
                    tp = pe.do(lambda e: e.matmul(B7[:, q * P:(q + 1) * P], hqT[0:rows, ch, q * P:(q + 1) * P],
                                                  wdT[0:rows, ch, :], start=ch == 0, stop=ch == 2), tc, B7.handed_back() if q == 0 and ch == 0 else None)
            hqT.hand_back(tp)
            t = self.add_to_x(b, B7[:, 0:L].rearrange("p (q d) -> p q d", q=QT), tp)
            B7.hand_back(t)
            yield

        def body(b):
            t = self.spread0(b) if 0 in self.debug else None
            txn, txnT = self.layer_norm(b, None, t)
            gens = [self.attention(1, txnT)] + ([ffn(b, txn)])
            for g in gens:
                for _ in g:
                    pass
            t = self.add_to_x(b, self.x1[:, :, :], self.t_x1)
            self.x1.hand_back(t)
        self.c.loop("layer1", NB, body)

    def layer2(self):
        ve, ac, pe, po, w, nc = self.ve, self.ac, self.pe, self.po, self.w, self.nc
        XN = self.sb("XN", [P, NT, D])
        LG = self.sb("LG", [P, NT, E2])
        if 0 in self.debug and 1 not in self.debug:
            self.c.loop("spread0", NB, lambda b: self.spread0(b))
        zero = self.sb("zero", [P, 512])
        t = ve.do(lambda e: e.memset(zero[:, :], 0.0))
        rows = nc.dram_tensor("slots", [E2 * CAP + NB * L, D], F32, kind="Internal").ap()
        zr = self.c.dma_stream(nc.sync, "zero_slots")
        for i in range(4):
            zr.do(lambda e: e.dma_start(rows[i * 512:(i + 1) * 512, :].rearrange("(p r) d -> p (r d)", p=P), zero[:, :]), t)
        own = rows[E2 * CAP:, :].rearrange("(t p) d -> p t d", p=P)

        def body(b):
            txn, txnT = self.layer_norm(b)
            bk = self.bank[7]
            for q in range(QT):
                t = pe.do(lambda e: e.matmul(bk[:, q * E2:(q + 1) * E2], self.xnT[:, q * P:(q + 1) * P], w["w_switch"],
                                             start=True, stop=True), txnT, bk.handed_back())
            t = ve.do(lambda e: e.tensor_tensor(LG[:, bass.ds(b * QT, QT), :], bk[:, 0:QT * E2].rearrange("p (q e) -> p q e", q=QT),
                                                bcast(w["b_switch"], QT, 1), ALU.add), t)
            bk.hand_back(t)
            self.gate_po(txn)
            t = po.do(lambda e: e.tensor_copy(XN[:, bass.ds(b * QT, QT), :], self.xn[:, :, :]))
            td = zr.do(lambda e: e.dma_start(own[:, bass.ds(b * QT, QT), :], self.xn[:, :, :]), txn)
            self.xn.hand_back(t, td, pe.last())
            for _ in self.attention(2, txnT):
                pass
            t = self.add_to_x(b, self.x1[:, :, :], self.t_x1)
            self.x1.hand_back(t)
        self.c.loop("layer2", NB, body)

        prb = self.sb("prb", [P, NT, E2])
        m1 = self.sb("m1", [P, NT])
        pm = self.sb("pm", [P, NT])
        m8 = self.sb("m8", [P, NT, 8])
        i8 = self.sb("i8", [P, NT, 8], U32)
        rt = self.sb("rt", [P, NT])
        oh = self.sb("oh", [P, NT, E2])
        ohb = self.sb("ohb", [P, NT * E2], BF16)
        tot = self.sb("tot", [P, NT, E2])
        off = self.sb("off", [P, NT, E2])
        pos = self.sb("pos", [P, NT])
        keep = self.sb("keep", [P, NT])
        slot = self.sb("slot", [P, NT])
        sloti = self.sb("sloti", [P, NT], I32)
        B0, B1 = self.bank[0], self.bank[1]
        do = lambda f, *n: ve.do(f, ve.last(), *n)
        do(lambda e: e.tensor_reduce(m1[:, :], LG[:, :, :], AX.X, ALU.max))
        t = do(lambda e: e.tensor_tensor(prb[:, :, :], LG[:, :, :], bcast(m1[:, :], E2, 2), ALU.subtract))
        t = ac.do(lambda e: e.activation(prb[:, :, :], prb[:, :, :], ACT.Exp), t)
        do(lambda e: e.tensor_reduce(m1[:, :], prb[:, :, :], AX.X, ALU.add), t)
        do(lambda e: e.reciprocal(m1[:, :], m1[:, :]))
        do(lambda e: e.tensor_tensor(prb[:, :, :], prb[:, :, :], bcast(m1[:, :], E2, 2), ALU.mult))
        do(lambda e: e.tensor_reduce(pm[:, :], prb[:, :, :], AX.X, ALU.max))
        do(lambda e: e.reciprocal(m1[:, :], pm[:, :]))
        scl = self.sb("scl", [P, NT])
        do(lambda e: e.tensor_tensor(scl[:, :], pm[:, :], m1[:, :], ALU.mult))
        t = ve.last()
        self.gate(t)
        for i in range(NT):
            t = ve.do(lambda e: e.max(m8[:, i, :], prb[:, i, :]))
        self.gate(t)
        for i in range(NT):
            ve.do(lambda e: e.max_index(i8[:, i, :], m8[:, i, :], prb[:, i, :]))
        do(lambda e: e.tensor_copy(rt[:, :], i8[:, :, 0]))
        t = do(lambda e: e.tensor_tensor(oh[:, :, :], bcast(w["iota8"], NT, 1), bcast(rt[:, :], E2, 2), ALU.is_equal))
        t = do(lambda e: e.tensor_copy(ohb[:, :], oh[:, :, :].rearrange("p t e -> p (t e)")))
        ta = pe.do(lambda e: e.matmul(B0[:, 0:NT * E2], w["upto"], ohb[:, :], start=True, stop=True), t, B0.handed_back())
        tb = pe.do(lambda e: e.matmul(B1[:, 0:NT * E2], w["onesb"], ohb[:, :], start=True, stop=True), B1.handed_back())
        do(lambda e: e.tensor_copy(tot[:, :, :], B1[:, 0:NT * E2].rearrange("p (t e) -> p t e", t=NT)), tb)
        do(lambda e: e.memset(off[:, 0, :], 0.0))
        for i in range(1, NT):
            do(lambda e: e.tensor_tensor(off[:, i, :], off[:, i - 1, :], tot[:, i - 1, :], ALU.add))
        do(lambda e: e.tensor_tensor(off[:, :, :], off[:, :, :], B0[:, 0:NT * E2].rearrange("p (t e) -> p t e", t=NT), ALU.add), ta)
        do(lambda e: e.tensor_tensor(off[:, :, :], off[:, :, :], oh[:, :, :], ALU.mult))
        do(lambda e: e.tensor_reduce(pos[:, :], off[:, :, :], AX.X, ALU.add))
        do(lambda e: e.tensor_scalar(pos[:, :], pos[:, :], -1.0, None, ALU.add))
        do(lambda e: e.tensor_scalar(keep[:, :], pos[:, :], float(CAP), None, ALU.is_lt))
        do(lambda e: e.scalar_tensor_tensor(slot[:, :], rt[:, :], float(CAP), pos[:, :], ALU.mult, ALU.add))
        do(lambda e: e.tensor_tensor(slot[:, :], slot[:, :], w["own"], ALU.subtract))
        do(lambda e: e.tensor_tensor(slot[:, :], slot[:, :], keep[:, :], ALU.mult))
        do(lambda e: e.tensor_tensor(slot[:, :], slot[:, :], w["own"], ALU.add))
        t = do(lambda e: e.tensor_copy(sloti[:, :], slot[:, :]))
        sct = self.c.dma_stream(nc.gpsimd, "scatter")
        self.c.join()
        for i in range(NT):
            sct.do(lambda e: e.indirect_dma_start(out=rows, out_offset=bass.IndirectOffsetOnAxis(ap=sloti[:, i:i + 1].bitcast(U32), axis=0),
                                                  in_=XN[:, i, :], in_offset=None))
        w1r = [self.slot(f"w1s{i}", [P, H2]) for i in range(2)]
        w2r = [self.slot(f"w2s{i}", [P, H2 // P, D]) for i in range(2)]
        bb = [self.slot(f"bb{i}", [P, QT, D]) for i in range(2)]
        bT = [self.slot(f"bT{i}", [P, CAP]) for i in range(2)]
        hT = [self.slot(f"hT{i}", [P, H2 // P, CAP]) for i in range(2)]
        yy = [self.slot(f"yy{i}", [P, QT, D]) for i in range(2)]
        lw = [(self.c.dma_stream(nc.sync, f"e2a{i}"), self.c.dma_stream(nc.sync, f"e2b{i}"), self.c.dma_stream(nc.sync, f"e2c{i}"),
               self.c.dma_stream(nc.scalar, f"e2d{i}")) for i in range(2)]
        J = H2 // P

        def ebody(i):
            lds = []
            for s in range(2):
                ex = i * 2 + s
                la = lw[s][0].do(lambda e: e.dma_start(w1r[s][:, :], self.ins["s_w1"][bass.ds(ex, 1), :, :].rearrange("a p h -> (a p) h")), w1r[s].handed_back())
                lb = lw[s][1].do(lambda e: e.dma_start(w2r[s][:, :, :], self.ins["s_w2"][bass.ds(ex, 1), :, :].rearrange("a (j p) d -> p (a j) d", p=P)), w2r[s].handed_back())
                lc = lw[s][2].do(lambda e: e.dma_start(bb[s][:, :, :], rows[bass.ds(ex * CAP, CAP), :].rearrange("(q p) d -> p q d", p=P)), bb[s].handed_back())
                lds.append((la, lb, lc))
            for s in range(2):
                ex = i * 2 + s
                la, lb, lc = lds[s]
                bt = self.bank[s]
                for q in range(QT):
                    t = pe.do(lambda e: e.transpose(bt[:, q * P:(q + 1) * P], bb[s][:, q, :], w["ident"]), lc, bt.handed_back())
                bb[s].hand_back(t)
                tT = ve.do(lambda e: e.tensor_copy(bT[s][:, :], bt[:, 0:CAP]), t, bT[s].handed_back())
                bt.hand_back(tT)
                for j in range(J):
                    bh = self.bank[2 + j % 4]
                    t = pe.do(lambda e: e.matmul(bh[:, 0:CAP], w1r[s][:, j * P:(j + 1) * P], bT[s][:, :], start=True, stop=True),
                              la, tT, bh.handed_back())
                    th = ac.do(lambda e: e.activation(hT[s][:, j, :], bh[:, 0:CAP], ACT.Relu,
                                                      bias=w["s_b1"][:, bass.ds(ex, 1), j:j + 1].rearrange("p a j -> p (a j)")),
                               t, hT[s].handed_back() if j == 0 else None)
                    bh.hand_back(th)
                w1r[s].hand_back(t)
                bT[s].hand_back(t)
                by = self.bank[6 + s]
                for q in range(QT):
                    for j in range(J):
                        t = pe.do(lambda e: e.matmul(by[:, q * P:(q + 1) * P], hT[s][:, j, q * P:(q + 1) * P], w2r[s][:, j, :],
                                                     start=j == 0, stop=j == J - 1), th, lb, by.handed_back() if q == 0 and j == 0 else None)
                w2r[s].hand_back(t)
                hT[s].hand_back(t)
                t = ve.do(lambda e: e.tensor_tensor(yy[s][:, :, :], by[:, 0:CAP].rearrange("p (q d) -> p q d", q=QT),
                                                    bcast(w["s_b2"][:, bass.ds(ex, 1), :].rearrange("p a d -> p (a d)"), QT, 1), ALU.add),
                          t, yy[s].handed_back())
                by.hand_back(t)
                t = lw[s][3].do(lambda e: e.dma_start(rows[bass.ds(ex * CAP, CAP), :].rearrange("(q p) d -> p q d", p=P), yy[s][:, :, :]), t, lc)
                yy[s].hand_back(t)
        self.c.loop("experts2", E2 // 2, ebody)
        gat = self.c.dma_stream(nc.gpsimd, "gather")
        YG = XN
        for i in range(NT):
            t = gat.do(lambda e: e.indirect_dma_start(out=YG[:, i, :], out_offset=None, in_=rows,
                                                      in_offset=bass.IndirectOffsetOnAxis(ap=sloti[:, i:i + 1].bitcast(U32), axis=0)))
        do(lambda e: e.tensor_tensor(YG[:, :, :], YG[:, :, :], bcast(scl[:, :], D, 2), ALU.mult), t)
        do(lambda e: e.tensor_tensor(self.X[:, :, :], self.X[:, :, :], YG[:, :, :], ALU.add))

    def layer3(self):
        ve, ac, pe, po, w = self.ve, self.ac, self.pe, self.po, self.w
        A3 = self.neg_exp("A3", w["A_log3"], 1)
        m = ve.do(lambda e: e.tensor_scalar(w["ctx"], w["ctx"], w["ctx_scale"], None, ALU.mult))
        sT = self.slot("sT", [P, L])
        st = self.slot("st", [P, QT, D])
        lT = self.slot("lT", [P, L])
        lg = self.slot("lg3", [P, QT, E3])
        m8 = self.slot("m83", [P, QT, 8])
        i8 = self.slot("i83", [P, QT, 8], U32)
        rf = self.slot("rf3", [P, QT, 8])
        g2 = self.slot("g23", [P, QT, 2])
        gt = self.slot("gt3", [P, QT, E3])
        gt2 = self.slot("gt23", [P, QT, E3])
        NH = E3 * H3
        hs = self.slot("hs3", [P, NH + SH3 * H3])
        he = self.slot("he3", [P, NH + SH3 * H3])
        hT = self.slot("hT3", [P, 5, P])
        acc = self.slot("acc3", [P, QT, D])
        B = self.bank
        st_out = self.c.dma_stream(self.nc.sync, "store")
        outv = self.out.rearrange("(t p) d -> p t d", p=P)

        def ssm(b, txn, txnT):
            B5, B6, B7 = B[5], B[6], B[7]
            t = pe.do(lambda e: e.matmul(B5[0:96, 0:L], w["w_bc3"], self.xnT[:, :], start=True, stop=True), txnT, B5.handed_back())
            t0, t_split = self.split3(B5[0:96, 0:L], t)
            B5.hand_back(t0)
            t = pe.do(lambda e: e.matmul(B6[:, 0:L], w["w_delta"], self.xnT[:, :], start=True, stop=True), B6.handed_back())
            t = ve.do(lambda e: e.tensor_copy(self.zin[:, 0, :], B6[:, 0:L]), t)
            B6.hand_back(t)
            t_delta = self.softplus(1, t)
            u = self.xnT[:, :].rearrange("p (c t) -> p c t", c=1)
            yield from self.scan(1, A3, u, txnT, t_delta, t_split, (B5, B6), B7)
            t = ac.do(lambda e: e.activation(sT[:, :], B7[:, 0:L], ACT.Copy), self.t_scan, sT.handed_back())
            B7.hand_back(t)
            for q in range(QT):
                t1 = pe.do(lambda e: e.transpose(B5[:, q * P:(q + 1) * P], sT[:, q * P:(q + 1) * P], w["ident"]), t, B5.handed_back())
            sT.hand_back(t1)
            t = ve.do(lambda e: e.tensor_copy(st[:, :, :], B5[:, 0:L].rearrange("p (q d) -> p q d", q=QT)), t1, st.handed_back())
            B5.hand_back(t)
            for q in range(QT):
                t1 = ve.do(lambda e: e.bn_stats(self.stats[:, q, :], st[:, q, :]), t)
            self.gate(t1, self.mv.handed_back())
            for q in range(QT):
                t2 = ve.do(lambda e: e.bn_aggr(self.mv[:, q, :], self.stats[:, q, :]))
            t3 = ac.do(lambda e: e.activation(self.lnv[:, :], self.mv[:, :, 1], ACT.Ln, bias=w["eps"], scale=1.0), t2)
            t4 = ac.do(lambda e: e.activation(self.rstd[:, :], self.lnv[:, :], ACT.Exp, scale=-0.5), t3, self.rstd.handed_back())
            for q in range(QT):
                t5 = ve.do(lambda e: e.tensor_scalar(st[:, q, :], st[:, q, :], self.mv[:, q, 0:1],
                                                     self.rstd[:, q:q + 1], ALU.subtract, ALU.mult), t4)
            self.mv.hand_back(t3, t5)
            self.rstd.hand_back(t5)
            for q in range(QT):
                t1 = pe.do(lambda e: e.transpose(B5[:, q * P:(q + 1) * P], st[:, q, :], w["ident"]), t5, B5.handed_back())
            st.hand_back(t1)
            t = ve.do(lambda e: e.tensor_scalar(lT[:, :], B5[:, 0:L], w["gamma"], w["beta"], ALU.mult, ALU.add), t1, lT.handed_back())
            B5.hand_back(t)
            for q in range(QT):
                t1 = pe.do(lambda e: e.matmul(B5[:, q * P:(q + 1) * P], lT[:, q * P:(q + 1) * P], w["ctx"], start=True, stop=True), t, B5.handed_back() if q == 0 else None)
            lT.hand_back(t1)
            t = self.add_to_x(b, B5[:, 0:L].rearrange("p (q d) -> p q d", q=QT), t1)
            B5.hand_back(t)
            yield

        def moe(b, txnT):
            for q in range(QT):
                t = pe.do(lambda e: e.matmul(B[4][:, q * E3:(q + 1) * E3], self.xnT[:, q * P:(q + 1) * P], w["router_w"],
                                             start=True, stop=True), txnT, B[4].handed_back())
            t = ve.do(lambda e: e.tensor_tensor(lg[:, :, :], B[4][:, 0:QT * E3].rearrange("p (q e) -> p q e", q=QT),
                                                bcast(w["router_b"], QT, 1), ALU.add), t)
            B[4].hand_back(t)
            self.gate(t)
            for q in range(QT):
                t = ve.do(lambda e: e.max(m8[:, q, :], lg[:, q, :]))
            self.gate(t)
            for q in range(QT):
                t = ve.do(lambda e: e.max_index(i8[:, q, :], m8[:, q, :], lg[:, q, :]))
            do = lambda f, *n: ve.do(f, ve.last(), *n)
            t = do(lambda e: e.tensor_tensor(g2[:, :, 1], m8[:, :, 1], m8[:, :, 0], ALU.subtract))
            t = ac.do(lambda e: e.activation(g2[:, :, 1], g2[:, :, 1], ACT.Exp), t)
            do(lambda e: e.tensor_copy(rf[:, :, :], i8[:, :, :]))
            do(lambda e: e.tensor_scalar(g2[:, :, 0], g2[:, :, 1], 1.0, None, ALU.add), t)
            do(lambda e: e.reciprocal(g2[:, :, 0], g2[:, :, 0]))
            do(lambda e: e.tensor_tensor(g2[:, :, 1], g2[:, :, 1], g2[:, :, 0], ALU.mult))
            for k, dst in ((0, gt), (1, gt2)):
                do(lambda e: e.tensor_tensor(dst[:, :, :], bcast(w["iota8"], QT, 1), bcast(rf[:, :, k], E3, 2), ALU.is_equal))
                do(lambda e: e.tensor_tensor(dst[:, :, :], dst[:, :, :], bcast(g2[:, :, k], E3, 2), ALU.mult))
            tgt = do(lambda e: e.tensor_tensor(gt[:, :, :], gt[:, :, :], gt2[:, :, :], ALU.add))
            yield
            NA = NH + SH3 * H3
            for q in range(QT):
                xl = self.xnT[:, q * P:(q + 1) * P]
                tm = []
                for bk, wt, c0, cn in ((B[0], "x_w1", 0, 512), (B[1], "x_w1", 512, 128), (B[2], "x_w3", 0, 512), (B[3], "x_w3", 512, 128)):
                    tm.append(pe.do(lambda e: e.matmul(bk[:, 0:cn], xl, w[wt][:, c0:c0 + cn], start=True, stop=True), bk.handed_back()))
                for j, (c0, cn) in enumerate(((0, 512), (512, 128))):
                    t = self.sigmoid_times(hs[:, c0:c0 + cn], B[j][:, 0:cn], he[:, c0:c0 + cn], tm[j], hs.handed_back() if j == 0 else None)
                    B[j].hand_back(t)
                    t = ve.do(lambda e: e.tensor_tensor(hs[:, c0:c0 + cn], hs[:, c0:c0 + cn], B[2 + j][:, 0:cn], ALU.mult), t, tm[2 + j])
                    B[2 + j].hand_back(t)
                v = hs[:, 0:NH].rearrange("p (e h) -> p e h", e=E3)
                tg = po.do(lambda e: e.tensor_tensor(v, v, bcast(gt[:, q, :], H3, 2), ALU.mult), t, tgt)
                for ch in range(5):
                    bk, o = (B[0], ch * P) if ch < 4 else (B[1], 0)
                    t = pe.do(lambda e: e.transpose(bk[:, o:o + P], hs[:, ch * P:(ch + 1) * P], w["ident"]), tg, bk.handed_back() if ch in (0, 4) else None)
                hs.hand_back(t)
                t1 = ac.do(lambda e: e.activation(hT[:, 0:4, :].rearrange("p c t -> p (c t)"), B[0][:, :], ACT.Copy), t, hT.handed_back())
                t2 = ac.do(lambda e: e.activation(hT[:, 4, :], B[1][:, 0:P], ACT.Copy), t)
                B[0].hand_back(t1)
                B[1].hand_back(t2)
                for ch in range(5):
                    t = pe.do(lambda e: e.matmul(B[4][:, 128 + q * P:128 + (q + 1) * P], hT[:, ch, :], w["x_w2"][:, ch, :],
                                                 start=ch == 0, stop=ch == 4), t2, B[4].handed_back() if q == 0 and ch == 0 else None)
                hT.hand_back(t)
                yield
            gt.hand_back(po.last())
            t = self.add_to_x(b, B[4][:, 128:128 + L].rearrange("p (q d) -> p q d", q=QT), t)
            B[4].hand_back(t)

        def body(b):
            txn, txnT = self.layer_norm(b)
            for g in (ssm(b, txn, txnT), moe(b, txnT)):
                for _ in g:
                    pass
            self.xnT.hand_back(pe.last(), ve.last())
            st_out.do(lambda e: e.dma_start(outv[:, bass.ds(b * QT, QT), :], self.X[:, bass.ds(b * QT, QT), :]), ve.last())
        self.c.loop("layer3", NB, body)

    def build(self):
        self.load_all()
        self.PT = self.sb("PT", [E0, NB, L])
        self.merged = self.sb("merged", [P, E0, NB])
        self.oall = self.sb("oall", [P, NB, E0])
        self.ob = self.slot("ob", [P, E0])
        self.oe = self.slot("oe", [E0, D])
        self.pts = self.slot("pts", [E0, L])
        if 0 in self.debug:
            with self.scope():
                self.load_packs("wf0")
                self.alloc_common(0)
                self.alloc_scan(CI)
                self.alloc0()
                self.layer0()
            with self.scope():
                self.load_packs("wf0e")
                self.experts0()
        if 1 in self.debug:
            with self.scope():
                self.load_packs("wf1")
                self.alloc_common(1)
                self.layer1()
        if 2 in self.debug:
            with self.scope():
                self.load_packs("wf2")
                self.alloc_common(2)
                self.layer2()
        if 3 in self.debug:
            with self.scope():
                self.load_packs("wf3")
                self.alloc_common(3)
                self.alloc_scan(1)
                self.layer3()
        else:
            if 0 in self.debug and 1 not in self.debug and 2 not in self.debug:
                self.c.loop("spread0", NB, lambda b: self.spread0(b))
            st = self.c.dma_stream(self.nc.sync, "store")
            st.do(lambda e: e.dma_start(self.out.rearrange("(t p) d -> p t d", p=P), self.X[:, :, :]))
        self.c.join()
        self.stack.close()


def _packs(i):
    f = lambda a: np.asarray(a, np.float32) if np.asarray(a).dtype != np.float32 else np.asarray(a)
    g = {k: f(v) for k, v in i.items()}
    packs = {"wf": []}
    bf = []
    cur = ["wf"]

    def layer(name):
        packs[name] = []
        cur[0] = name

    def put(name, a, shape=None):
        a = np.asarray(a)
        shape = shape or a.shape[1:]
        packs[cur[0]].append((name, a.reshape(a.shape[0], -1), tuple(shape)))

    def rep(v):
        return np.broadcast_to(np.asarray(v).reshape(1, -1), (P, np.asarray(v).size))

    def heads4(wm):
        out = np.zeros((wm.shape[0], 4, 4, 32), np.float32)
        out[:, :, :, 0:8] = wm.reshape(wm.shape[0], 4, 4, 8)
        return out.reshape(wm.shape[0], 4, P)

    def bias4(b):
        return heads4(b.reshape(1, P))[0].T

    put("ident", np.eye(P, dtype=np.float32))
    put("eps", np.full((P, 1), EPS, np.float32))
    put("iota8", rep(np.arange(8, dtype=np.float32)))
    put("own", (E2 * CAP + np.arange(NT)[None, :] * P + np.arange(P)[:, None]).astype(np.float32))
    layer("wf0")
    wqkv, bqkv = g["L0_attn_wqkv"], g["L0_attn_bqkv"]
    put("wq0", heads4(wqkv[:, :P]))
    put("bq0", bias4(bqkv[:P]))
    put("wk0", heads4(np.tile(wqkv[:, P:P + 8], (1, HEADS)))[:, 0:1])
    put("bk0", bias4(np.tile(bqkv[P:P + 8], HEADS))[:, 0:1])
    put("wv0", wqkv[:, P + 8:])
    put("bv0", rep(bqkv[P + 8:]))
    put("wo0", g["L0_attn_w_attn_out"].reshape(P, 1, D))
    put("bo0", rep(g["L0_attn_b_attn_out"]))
    put("w_in", g["L0_attn_w_in"].reshape(D, 2 * CI, P))
    ch = lambda a: np.swapaxes(a.reshape(CI, P, -1), 0, 1)
    put("conv_w", ch(g["L0_attn_conv_w"]))
    put("conv_b", ch(g["L0_attn_conv_b"])[:, :, 0])
    xp = ch(g["L0_attn_w_xproj"])
    put("w_dtin", np.ascontiguousarray(xp[:, :, :DTR]))
    put("w_bc", np.tile(xp[:, :, DTR:], (1, 1, 3)))
    put("w_dt", g["L0_attn_w_dt"])
    put("b_dt", ch(g["L0_attn_b_dt"])[:, :, 0])
    put("A_log0", ch(g["L0_attn_A_log"]))
    put("Dp", ch(g["L0_attn_Dp"])[:, :, 0])
    put("w_out", ch(g["L0_attn_w_out"]))
    put("gate_w", g["L0_ffn_gate_w"].T)
    put("gate_b", g["L0_ffn_gate_b"].reshape(E0, 1))
    layer("wf0e")
    w1, w2 = g["L0_ffn_w1"], g["L0_ffn_w2"]
    put("m_b1", w1[:, D, :].reshape(E0, H0 // P, P).transpose(2, 0, 1))
    put("m_b2", w2[:, H0, :].T)
    layer("wf1")
    for n in "qk":
        put(f"w{n}1", g[f"L1_attn_W{n}"].transpose(1, 0, 2).reshape(D, 8, P))
        put(f"b{n}1", g[f"L1_attn_b{n}"].reshape(8, P).T)
    put("wv1", g["L1_attn_Wv"].transpose(1, 0, 2).reshape(D, HEADS * A1))
    put("bv1", rep(g["L1_attn_bv"]))
    put("wo1", g["L1_attn_Wo"].reshape(8, P, D).transpose(1, 0, 2))
    put("bo1", rep(g["L1_attn_bo"]))
    pad = lambda a: np.concatenate([a, np.zeros((3 * P - I1, a.shape[1]), np.float32)]).reshape(3, P, -1).transpose(1, 0, 2)
    put("wgu1", np.concatenate([pad(g["L1_ffn_w_gate"]), pad(g["L1_ffn_w_up"])], 1))
    put("wd1", g["L1_ffn_w_down"])
    layer("wf2")
    for n in "qk":
        put(f"w{n}2", heads4(g[f"L2_attn_W{n}"].T))
        put(f"b{n}2", bias4(g[f"L2_attn_b{n}"]))
    put("wv2", g["L2_attn_Wv"].T)
    put("bv2", rep(g["L2_attn_bv"]))
    put("wo2", g["L2_attn_Wo"].T.reshape(P, 1, D))
    put("bo2", rep(g["L2_attn_bo"]))
    put("w_switch", g["L2_ffn_w_switch"])
    put("b_switch", rep(g["L2_ffn_b_switch"]))
    put("s_b1", g["L2_ffn_b1"].reshape(E2, H2 // P, P).transpose(2, 0, 1))
    put("s_b2", rep(g["L2_ffn_b2"]), (E2, D))
    layer("wf3")
    put("A_log3", g["L3_attn_A_log"].reshape(P, 1, NS))
    put("w_delta", g["L3_attn_W_delta"].T)
    put("w_bc3", np.tile(np.concatenate([g["L3_attn_W_B"], g["L3_attn_W_C"]]).T, (1, 3)))
    put("gamma", g["L3_attn_ln_gamma"].reshape(P, 1))
    put("beta", g["L3_attn_ln_beta"].reshape(P, 1))
    put("ctx", g["L3_attn_W_ctx"].T)
    put("ctx_scale", rep(g["L3_attn_context_scale"]))
    put("router_w", g["L3_ffn_router_w"])
    put("router_b", rep(g["L3_ffn_router_b"]))
    for n in ("w1", "w3"):
        a = np.concatenate([g["L3_ffn_routed_" + n], g["L3_ffn_shared_" + n]])
        put("x_" + n, a.transpose(1, 0, 2).reshape(D, -1))
    a = np.concatenate([g["L3_ffn_routed_w2"], g["L3_ffn_shared_w2"]])
    put("x_w2", a.reshape(5, P, D).transpose(1, 0, 2))
    tri = np.where(np.arange(P)[:, None] >= np.arange(P)[None, :], 0.0, NEG)

    def putb(name, a):
        a = np.asarray(a)
        bf.append((name, a.reshape(a.shape[0], -1).astype(np.float32), tuple(a.shape[1:])))

    putb("identb", np.eye(P))
    putb("mask0", tri)
    putb("mask1", np.concatenate([np.zeros((P, P)), tri], 1))
    putb("upto", (np.arange(P)[:, None] <= np.arange(P)[None, :]).astype(np.float32))
    putb("onesb", np.ones((P, P)))
    putb("sel", np.arange(96)[:, None] % 32 == np.arange(32)[None, :])

    packed, arrays = {}, {}
    packs["wb"] = bf
    for pname, items in packs.items():
        off, parts, cols = 0, {}, []
        for name, a, shape in items:
            parts[name] = (off, a.shape[0], shape)
            full = np.zeros((P, a.shape[1]), a.dtype)
            full[:a.shape[0]] = a
            cols.append(full)
            off += a.shape[1]
        arrays[pname] = np.ascontiguousarray(np.concatenate(cols, 1))
        packed[pname] = (off, parts)
    return packed, arrays


LAYERS = (0, 1, 2, 3)


def kernel(**inputs):
    import concourse.bacc as _bacc
    from concourse.bass_utils import run_bass_kernel_spmd as _run

    inputs = {k: np.asarray(v) for k, v in inputs.items()}
    packed, arrays = _packs(inputs)
    arrays["x"] = np.ascontiguousarray(inputs["L0_attn_x"]).reshape(NB * L, D)
    arrays["m_w1"] = np.ascontiguousarray(inputs["L0_ffn_w1"])
    arrays["m_w2"] = np.ascontiguousarray(inputs["L0_ffn_w2"])
    arrays["s_w1"] = np.ascontiguousarray(inputs["L2_ffn_w1"])
    arrays["s_w2"] = np.ascontiguousarray(inputs["L2_ffn_w2"])
    turn_ends = {}
    for _ in range(2):
        nc = _bacc.Bacc("TRN2", target_bir_lowering=False, num_devices=1)
        ins = {n: nc.dram_tensor(n, list(a.shape), mybir.dt.from_np(a.dtype), kind="ExternalInput").ap()
               for n, a in arrays.items()}
        out = nc.dram_tensor("out", [NB * L, D], F32, kind="ExternalOutput").ap()
        Program(nc, turn_ends, ins, packed, out, LAYERS).build()
    r = _run(nc, [arrays], core_ids=[0])
    return r.results[0]["out"].reshape(NB, L, D)
```

```python
from contextlib import ExitStack, contextmanager

import numpy as np
import concourse.bass as bass
from concourse import mybir
from concourse.alu_op_type import AluOpType as ALU

ACT = mybir.ActivationFunctionType
AX = mybir.AxisListType
F32, BF16, U32, I32 = mybir.dt.float32, mybir.dt.bfloat16, mybir.dt.uint32, mybir.dt.int32

P = 128
D = 128
NB, L = 16, 256
QT = L // P
NT = NB * QT
HEADS = 16
NG = 4
DI, NS, DTR, CONV = 256, 16, 8, 4
CI = DI // P
E0, H0 = 32, 512
A1 = 64
I1, BLK = 352, 16
E2, H2, CAP = 8, 512, NB * L // 16
E3, SH3, H3 = 8, 2, 64
EPS = 1e-5
NEG = -1e30


class Mark:

    def __init__(self, stream, off, turn):
        self.stream, self.off, self.turn = stream, off, turn


class Stream:

    def __init__(self, core, eng, name, step=1):
        self.core, self.eng, self.name, self.step = core, eng, name, step
        self.sem = core.nc.alloc_semaphore("s_" + name)
        self.base = self.off = 0
        self.waited = {}
        core.streams.append(self)

    def need(self, mark):
        core = self.core
        if mark is None:
            return
        back = 0 if mark.turn == core.turn else 1
        if back and core.loop_name is None:
            return
        if self.waited.get(mark.stream.name, (-1, 0)) >= (-back, mark.off):
            return
        self.waited[mark.stream.name] = (-back, mark.off)
        self.eng.wait_ge(mark.stream.sem, core.value(mark.stream, mark.off, back))

    def needs(self, marks):
        for m in marks:
            if isinstance(m, (list, tuple)):
                self.needs(m)
            else:
                self.need(m)

    def do(self, issue, *marks):
        self.needs(marks)
        issue(self.eng).then_inc(self.sem, self.step)
        self.off += self.step
        return Mark(self, self.off, self.core.turn)

    def quiet(self, issue, *marks):
        self.needs(marks)
        issue(self.eng)

    def last(self):
        return Mark(self, self.off, self.core.turn) if self.off else None


class Slot:

    def __init__(self, core, name, tensor):
        self.core, self.name, self.t, self.back, self.full = core, name, tensor, None, None
        core.slots.append(self)

    def __getitem__(self, key):
        return self.t[key]

    def handed_back(self):
        if self.back is not None:
            return self.back
        return [Mark(self.core.by_name[s], off, "before")
                for s, off in self.core.turn_ends.get((self.core.loop_name, self.name), [])]

    def hand_back(self, *marks):
        self.back = [m for m in marks if m is not None]

    def fill(self, *marks):
        self.full = [m for m in marks if m is not None]

    def filled(self):
        if self.full is not None:
            return self.full
        return [Mark(self.core.by_name[s], off, "before")
                for s, off in self.core.turn_ends.get((self.core.loop_name, self.name, "full"), [])]


class Core:
    def __init__(self, nc, turn_ends):
        self.nc, self.turn_ends = nc, turn_ends
        self.steps = {}
        self.streams, self.slots, self.loop_name, self.i, self.turn = [], [], None, None, 0
        self.pe = Stream(self, nc.tensor, "pe")
        self.ve = Stream(self, nc.vector, "ve")
        self.ac = Stream(self, nc.scalar, "ac")
        self.po = Stream(self, nc.gpsimd, "po")
        self.by_name = {s.name: s for s in self.streams}

    def dma_stream(self, eng, name):
        s = Stream(self, eng, name, 16)
        self.by_name[name] = s
        return s

    def value(self, stream, off, back):
        if self.loop_name is None:
            return stream.base + off
        per = self.turn_ends.get((self.loop_name, "per", stream.name), 0)
        return stream.base + per * (1 - back) + off + self.i * per

    def join(self):
        for eng in (self.nc.tensor, self.nc.vector, self.nc.scalar, self.nc.gpsimd, self.nc.sync):
            for s in self.streams:
                if s.base + s.off:
                    eng.wait_ge(s.sem, s.base + s.off)
        self.fresh()

    def fresh(self):
        self.turn += 1
        for s in self.streams:
            s.base, s.off, s.waited = s.base + s.off, 0, {}
        for b in self.slots:
            b.back = b.full = None

    def loop(self, name, n, body, tables="natural_log_exp_and_others"):
        self.join()
        pers = {s.name: self.turn_ends.get((name, "per", s.name), 0) for s in self.streams}
        for s in self.streams:
            if pers[s.name]:
                self.nc.sync.nop().then_inc(s.sem, pers[s.name])
        self.loop_name = name
        self.nc.scalar.preload_act_table_set(tables)
        with self.nc.Fori(0, n) as i:
            self.i = i
            body(i)
        self.loop_name = None
        for b in self.slots:
            if b.back is not None:
                self.turn_ends[(name, b.name)] = [(m.stream.name, m.off) for m in b.back]
            if b.full is not None:
                self.turn_ends[(name, b.name, "full")] = [(m.stream.name, m.off) for m in b.full]
        for s in self.streams:
            self.turn_ends[(name, "per", s.name)] = s.off
            s.base, s.off = s.base + s.off * n + pers[s.name], 0
        self.fresh()
        self.join()


def bcast(ap, n, axis):
    ap = ap.unsqueeze(axis)
    shape = list(ap.shape)
    shape[axis] = n
    return ap.broadcast_to(tuple(shape))


def drain(gen):
    while True:
        try:
            next(gen)
        except StopIteration as end:
            return end.value


class Program:
    def __init__(self, nc, turn_ends, ins, packed, out, debug):
        self.nc, self.ins, self.packed, self.out, self.debug = nc, ins, packed, out, debug
        c = self.c = Core(nc, turn_ends)
        self.pe, self.ve, self.ac, self.po = c.pe, c.ve, c.ac, c.po
        self.load = c.dma_stream(nc.sync, "load")
        self.stack, self.taken = ExitStack(), 0
        self.X = self.sb("X", [P, NT, D])
        self.bank = [Slot(c, f"bank{i}", nc.alloc_psum_tensor(f"bank{i}", [P, 512], F32)) for i in range(8)]
        self.pack = {}
        self.w = {}

    def weave(self, *gens):
        live = [[0.0, name, 0, g] for g, name in gens if g is not None]
        while live:
            x = min(live, key=lambda v: v[0])
            try:
                next(x[3])
                x[2] += 1
                x[0] = x[2] / self.c.turn_ends.get(("steps", x[1]), 1)
            except StopIteration:
                self.c.steps[("steps", x[1])] = x[2] + 1
                live.remove(x)

    @contextmanager
    def scope(self):
        outer, self.stack = self.stack, ExitStack()
        with self.stack:
            yield
            self.c.join()
        self.stack = outer

    def sb(self, name, shape, dt=F32):
        self.taken += 1
        return self.stack.enter_context(self.nc.sbuf_tensor(f"{name}_{self.taken}", shape, dt))

    def slot(self, name, shape, dt=F32):
        return Slot(self.c, name, self.sb(name, shape, dt))

    def load_all(self):
        ld = self.load
        ld.do(lambda e: e.dma_start(self.X[:, :, :], self.ins["x"].rearrange("(t p) d -> p t d", p=P)))
        self.dummy = self.sb("dummy", [P, 4])
        self.dummy_ve, self.dummy_po = Slot(self.c, "dummy_ve", None), Slot(self.c, "dummy_po", None)
        self.ve.do(lambda e: e.memset(self.dummy[:, :], 0.0))
        self.load_packs("wf")
        w, ve = self.w, self.ve
        small = {n: self.sb(n, [P, k], BF16) for n, k in (("identb", P), ("mask0", P), ("mask1", L), ("upto", P), ("onesb", P))}
        sel = self.sb("selb", [96, 2 * NS, P], BF16)
        with self.scope():
            self.load_packs("wb")
            for n, t in small.items():
                ve.do(lambda e: e.tensor_copy(t[:, :], w[n]))
                w[n] = t[:, :]
            ve.do(lambda e: e.tensor_copy(sel[:, :, :], bcast(w["sel"], P, 2)))
            w["sel"] = sel[:, :, :]

    def load_packs(self, *names):
        ld, marks = self.load, []
        for pname in names:
            width, parts = self.packed[pname]
            t = self.sb("pack_" + pname, [P, width])
            marks.append(ld.do(lambda e: e.dma_start(t[:, :], self.ins[pname])))
            for name, (o, rows, shape) in parts.items():
                n = int(np.prod(shape))
                ap = t[0:rows, o:o + n]
                if len(shape) == 2:
                    ap = ap.rearrange("p (a b) -> p a b", a=shape[0])
                if len(shape) == 3:
                    ap = ap.rearrange("p (a b c) -> p a b c", a=shape[0], b=shape[1])
                self.w[name] = ap
        self.c.join()

    def gate(self, *marks):
        self.dummy_ve.hand_back(self.ve.do(lambda e: e.tensor_copy(self.dummy[:, 0:1], self.dummy[:, 1:2]),
                                      self.dummy_ve.handed_back(), *marks))

    def gate_po(self, *marks):
        self.dummy_po.hand_back(self.po.do(lambda e: e.tensor_tensor(self.dummy[:, 2:3], self.dummy[:, 3:4],
                                                                self.dummy[:, 3:4], ALU.add), self.dummy_po.handed_back(), *marks))

    def alloc_common(self, layer):
        two = range(2)
        self.xs = self.slot("xs", [P, QT, D])
        self.xn = [self.slot(f"xn{i}", [P, QT, D]) for i in two]
        self.xnT = [self.slot(f"xnT{i}", [P, L]) for i in two]
        self.ln = [[self.slot(f"{n}{i}", [P] + sh) for n, sh in (("stats", [QT, 6]), ("mv", [QT, 2]), ("lnv", [QT]), ("rstd", [QT]))]
                   for i in two]
        self.Xw = Slot(self.c, f"Xw{layer}", None)
        if layer == 3:
            return
        g, hd = (8, A1) if layer == 1 else (4, 8)
        self.qT = [self.slot(f"qT{i}", [P, g, L]) for i in two]
        self.kT = [self.slot(f"kT{i}", [P, 1 if layer == 0 else g, L]) for i in two]
        self.v = [self.slot(f"v{i}", [P, QT, HEADS * hd]) for i in two]
        self.mx = [self.slot(f"mx{i}", [P, 4]) for i in two]
        self.nb = [self.slot(f"nb{i}", [P, 4]) for i in two]
        self.pr = [self.slot(f"pr{i}", [P, 512]) for i in range(2)]
        self.prT = [self.slot(f"prT{i}", [P, 512]) for i in range(2)]
        self.sums = [self.slot(f"sums{i}", [P, HEADS]) for i in range(QT)]
        self.rsum = [self.slot(f"rsum{i}", [P, HEADS]) for i in range(QT)]
        self.o = [self.slot(f"o{i}", [P, HEADS * hd]) for i in range(QT)]
        self.oT = [self.slot(f"oT{i}", [P, HEADS * hd // P, P]) for i in range(QT)]
        self.x1 = self.slot("x1", [P, QT, D])

    def normalise(self, src, dst, ready, which):
        ve, ac = self.ve, self.ac
        stats, mv, lnv, rstd = self.ln[which]
        for q in range(QT):
            t1 = ve.do(lambda e: e.bn_stats(stats[:, q, :], src[:, q, :]), ready)
        yield None
        self.gate(t1, mv.handed_back())
        for q in range(QT):
            t2 = ve.do(lambda e: e.bn_aggr(mv[:, q, :], stats[:, q, :]))
        t3 = ac.do(lambda e: e.activation(lnv[:, :], mv[:, :, 1], ACT.Ln, bias=self.w["eps"], scale=1.0), t2)
        t4 = ac.do(lambda e: e.activation(rstd[:, :], lnv[:, :], ACT.Exp, scale=-0.5), t3, rstd.handed_back())
        yield None
        for q in range(QT):
            t5 = ve.do(lambda e: e.tensor_scalar(dst[:, q, :], src[:, q, :], mv[:, q, 0:1], rstd[:, q:q + 1],
                                                 ALU.subtract, ALU.mult), t4, dst.handed_back() if dst is not src else None)
        mv.hand_back(t3, t5)
        rstd.hand_back(t5)
        yield t5

    def layer_norm(self, b, k, bk, ready=None):
        ve, ac, pe = self.ve, self.ac, self.pe
        xn, xnT = self.xn[k], self.xnT[k]
        self.gate(self.xs.handed_back(), ready, self.Xw.filled())
        t = ve.do(lambda e: e.tensor_copy(self.xs[:, :, :], self.X[:, bass.ds(b * QT, QT), :]))
        for t5 in self.normalise(self.xs, xn, t, 0):
            if t5 is None:
                yield
        self.xs.hand_back(t5)
        xn.fill(t5)
        yield
        for q in range(QT):
            t6 = pe.do(lambda e: e.transpose(bk[:, q * P:(q + 1) * P], xn[:, q, :], self.w["ident"]), t5, bk.handed_back())
        yield
        t7 = ac.do(lambda e: e.activation(xnT[:, :], bk[:, 0:L], ACT.Copy), t6, xnT.handed_back())
        bk.hand_back(t7)
        xnT.fill(t7)
        xn.hand_back(t6)
        yield

    def qkv(self, layer, k, bk):
        ve, ac, pe, w = self.ve, self.ac, self.pe, self.w
        hd = A1 if layer == 1 else 8
        groups = 8 if layer == 1 else 4
        kg = 1 if layer == 0 else groups
        xnT, v = self.xnT[k], self.v[k]
        nv = 8 if layer == 0 else HEADS * hd
        ta = tv = None
        turn = 0
        for dst, wt, bias, n in ((self.qT[k], w[f"wq{layer}"], w[f"bq{layer}"], groups),
                                 (self.kT[k], w[f"wk{layer}"], w[f"bk{layer}"], kg)):
            for g0 in range(0, n, 2):
                gs = range(g0, min(g0 + 2, n))
                for g in gs:
                    t = pe.do(lambda e: e.matmul(bk[:, (g - g0) * L:(g - g0 + 1) * L], wt[:, g, :], xnT[:, :], start=True,
                                                 stop=True), xnT.filled(), bk.handed_back() if g == g0 else None)
                yield
                for g in gs:
                    src = bk[:, (g - g0) * L:(g - g0 + 1) * L]
                    if turn % 2 == 0:
                        te = ta = ac.do(lambda e: e.activation(dst[:, g, :], src, ACT.Identity, bias=bias[:, g:g + 1]),
                                        t, dst.handed_back())
                    else:
                        te = tv = ve.do(lambda e: e.tensor_scalar(dst[:, g, :], src, bias[:, g:g + 1], None, ALU.add),
                                        t, dst.handed_back())
                bk.hand_back(te)
                turn += 1
                yield
        for q in range(QT):
            for c0 in range(0, nv, 512):
                cn = min(512, nv - c0)
                t = pe.do(lambda e: e.matmul(bk[:, 0:cn], xnT[:, q * P:(q + 1) * P], w[f"wv{layer}"][:, c0:c0 + cn],
                                             start=True, stop=True), bk.handed_back())
                yield
                tv = ve.do(lambda e: e.tensor_tensor(v[:, q, c0:c0 + cn], bk[:, 0:cn], w[f"bv{layer}"][:, c0:c0 + cn],
                                                     ALU.add), t, v.handed_back())
                bk.hand_back(tv)
                yield
        for dst in (self.qT[k], self.kT[k], v):
            dst.fill(ta, tv)
        xnT.hand_back(t)

    def attention(self, layer, k, sc, tr, vb):
        ve, ac, pe, w = self.ve, self.ac, self.pe, self.w
        hd = A1 if layer == 1 else 8
        scale = float(hd) ** -0.5
        groups, rows = (8, 64) if layer == 1 else (4, 32)
        per = P // rows
        qT, kT, v = self.qT[k], self.kT[k], self.v[k]
        tin = qT.filled() + v.filled()
        nv = 8 if layer == 0 else HEADS * hd
        order = sorted(range(HEADS), key=lambda h: (h % per, h))
        units = [(0, order[4 * u:4 * u + 4]) for u in range(4)] + [(1, order[2 * u:2 * u + 2]) for u in range(8)]
        half = 8 if hd == A1 else HEADS
        t_exp, t_sc, t_pT, t_pv = {}, {}, {}, {}

        def scores(u):
            q, heads = units[u]
            bk = sc[u % 2]
            wid = P * (q + 1)
            for n, h in enumerate(heads):
                r = rows * (h % per)
                kk = 0 if layer == 0 else h // per
                dst = bk[:, n * wid:(n + 1) * wid]
                pe.quiet(lambda e: e.matmul(dst, w["identb"], w[f"mask{q}"][:, 0:wid], start=True, stop=False),
                         bk.handed_back() if n == 0 else None, tin)
                f = lambda e: e.matmul(dst, qT[r:r + hd, h // per, q * P:(q + 1) * P],
                                       kT[r:r + hd, kk, 0:wid], start=False, stop=True)
                if n == len(heads) - 1:
                    t_sc[u] = pe.do(f)
                else:
                    pe.quiet(f)

        def softmax(u):
            q, heads = units[u]
            bk, nh, wid = sc[u % 2], len(heads), P * (q + 1)
            mx, nb, pr = self.mx[u % 2], self.nb[u % 2], self.pr[u % 2]
            v3 = bk[:, :].rearrange("p (h k) -> p h k", h=nh)
            t = ve.do(lambda e: e.tensor_reduce(mx[:, 0:nh], v3, AX.X, ALU.max), t_sc[u])
            t = ve.do(lambda e: e.tensor_scalar(nb[:, 0:nh], mx[:, 0:nh], -scale, None, ALU.mult), t, nb.handed_back())
            for n, h in enumerate(heads):
                te = ac.do(lambda e: e.activation(pr[:, n * wid:(n + 1) * wid], bk[:, n * wid:(n + 1) * wid], ACT.Exp,
                                                  bias=nb[:, n:n + 1], scale=scale,
                                                  accum_out=self.sums[q][:, h:h + 1]),
                           t, pr.handed_back(), self.sums[q].handed_back() if h == 0 else None)
            nb.hand_back(te)
            bk.hand_back(te)
            t_exp[u] = te

        def turn_p(u):
            bk, pr, prT = tr[u % len(tr)], self.pr[u % 2], self.prT[u % 2]
            for j in range(3):
                pe.quiet(lambda e: e.transpose(bk[:, j * P:(j + 1) * P], pr[:, j * P:(j + 1) * P], w["ident"]),
                         bk.handed_back(), t_exp[u])
            t = pe.do(lambda e: e.transpose(bk[:, 3 * P:], pr[:, 3 * P:], w["ident"]))
            pr.hand_back(t)
            if self.evac_act(layer, u):
                t = ac.do(lambda e: e.activation(prT[:, :], bk[:, :], ACT.Copy), t, prT.handed_back())
            else:
                t = ve.do(lambda e: e.tensor_copy(prT[:, :], bk[:, :]), t, prT.handed_back())
            bk.hand_back(t)
            t_pT[u] = t

        def values(u):
            q, heads = units[u]
            prT = self.prT[u % 2]
            for n, h in enumerate(heads):
                at = order.index(h) % half
                vc = 0 if layer == 0 else h * hd
                for kb in range(q + 1):
                    blk = n * (q + 1) + kb
                    f = lambda e: e.matmul(vb[:, at * hd:(at + 1) * hd], prT[:, blk * P:(blk + 1) * P],
                                           v[:, kb, vc:vc + hd], start=kb == 0, stop=kb == q)
                    fr = vb.handed_back() if at == 0 and kb == 0 else None
                    if kb == q and n == len(heads) - 1:
                        t_pv[u] = pe.do(f, t_pT[u], fr)
                    else:
                        pe.quiet(f, t_pT[u], fr)
            prT.hand_back(t_pv[u])

        def scale_rows(q, u, first):
            o, rs = self.o[q], self.rsum[q]
            p0 = order[first]
            t1 = t_exp[u]
            nt = half // (HEADS // per)
            if nt == 0:
                nt = 1
            cnt = half // nt
            for i in range(nt):
                h0 = order[first + i * cnt]
                hs = slice(h0, h0 + (cnt - 1) * per + 1, per)
                t1 = ve.do(lambda e: e.reciprocal(rs[:, first + i * cnt:first + (i + 1) * cnt], self.sums[q][:, hs]),
                           t_exp[u], rs.handed_back() if i == 0 else None)
            for i in range(nt):
                h0 = order[first + i * cnt]
                ov = o[:, :].rearrange("p (h d) -> p h d", d=hd)[:, h0:h0 + (cnt - 1) * per + 1:per, :]
                pv = vb[:, i * cnt * hd:(i + 1) * cnt * hd].rearrange("p (h d) -> p h d", h=cnt)
                t2 = ve.do(lambda e: e.tensor_tensor(ov, pv, bcast(rs[:, first + i * cnt:first + (i + 1) * cnt], hd, 2),
                                                     ALU.mult), t1, t_pv[u], o.handed_back() if first == 0 else None)
            vb.hand_back(t2)
            rs.hand_back(t2)
            if first + half == HEADS:
                self.sums[q].hand_back(t1)
            return t2

        def turn_o(q, t2):
            o, oT = self.o[q], self.oT[q]
            nch = HEADS * hd // P
            bk = tr[0]
            for c0 in range(0, nch, 4):
                cn = min(4, nch - c0)
                for ch in range(c0, c0 + cn):
                    t3 = pe.do(lambda e: e.transpose(bk[:, (ch - c0) * P:(ch - c0 + 1) * P], o[:, ch * P:(ch + 1) * P],
                                                     w["ident"]), t2, bk.handed_back())
                ts = ac.do(lambda e: e.activation(oT[:, c0:c0 + cn, :].rearrange("p c t -> p (c t)"),
                                                  bk[:, 0:cn * P], ACT.Copy), t3, oT.handed_back())
                bk.hand_back(ts)
            o.hand_back(t3)
            return ts

        t_o = {}
        n_u = len(units)
        full = {}
        seen = 0
        for u, (q, heads) in enumerate(units):
            seen += len(heads)
            if seen % half == 0:
                full[u] = (q, (seen - half) % HEADS)
        scores(0)
        yield
        for u in range(n_u + 2):
            if u + 1 < n_u:
                scores(u + 1)
            if u < n_u:
                softmax(u)
            yield
            if 1 <= u <= n_u:
                turn_p(u - 1)
            if u >= 2:
                values(u - 2)
                if u - 2 in full:
                    q, first = full[u - 2]
                    t2 = scale_rows(q, u - 2, first)
                    if first + half == HEADS:
                        t_o[q] = turn_o(q, t2)
            yield
        qT.hand_back(t_sc[n_u - 1])
        kT.hand_back(t_sc[n_u - 1])
        v.hand_back(t_pv[n_u - 1])
        nch = HEADS * hd // P
        bk = tr[-1]
        for q in range(QT):
            for ch in range(nch):
                f = lambda e: e.matmul(bk[:, q * P:(q + 1) * P], self.oT[q][:, ch, :], w[f"wo{layer}"][:, ch, :],
                                       start=ch == 0, stop=ch == nch - 1)
                t = pe.do(f, t_o[q], bk.handed_back() if q == 0 and ch == 0 else None)
            self.oT[q].hand_back(t)
        t1 = ve.do(lambda e: e.tensor_tensor(self.x1[:, :, :], bk[:, 0:L].rearrange("p (q d) -> p q d", q=QT),
                                             bcast(w[f"bo{layer}"], QT, 1), ALU.add), t, self.x1.handed_back())
        bk.hand_back(t1)
        self.t_x1 = t1
        yield

    def sigmoid_times(self, out, z, tmp, ready, free, z_is_psum_ok=True):
        t = self.ac.do(lambda e: e.activation(tmp, z, ACT.Exp, scale=-1.0), ready)
        yield
        t = self.ve.do(lambda e: e.tensor_scalar(tmp, tmp, 1e19, None, ALU.min), t)
        yield
        t = self.ac.do(lambda e: e.activation(tmp, tmp, ACT.Ln, bias=1.0), t)
        t = self.ac.do(lambda e: e.activation(tmp, tmp, ACT.Exp, scale=-1.0), t)
        yield
        return self.ve.do(lambda e: e.tensor_tensor(out, z, tmp, ALU.mult), t, free)

    def evac_act(self, layer, u):
        return u % 3 == 2

    def add_to_x(self, b, src, ready):
        xv = self.X[:, bass.ds(b * QT, QT), :]
        t = self.ve.do(lambda e: e.tensor_tensor(xv, xv, src, ALU.add), ready, self.Xw.filled())
        self.Xw.fill(t)
        return t

    def alloc_scan(self, CI):
        self.zin = self.slot("zin", [P, CI, L])
        self.zab = self.slot("zab", [P, CI, L])
        self.zmx = self.slot("zmx", [P, CI, L])
        self.delta = self.slot("delta", [P, CI, L])
        self.dtu = self.slot("dtu", [P, CI, L])
        self.split = self.slot("split", [96, L], BF16)
        self.sx = self.slot("sx", [96, L])
        self.sr = self.slot("sr", [96, L])
        self.sh = self.slot("sh", [96, L], BF16)
        self.dA = [[self.slot(f"dA{i}{j}", [P, NG, L]) for j in range(2)] for i in range(CI)]
        self.h = [[self.slot(f"h{i}{j}", [P, NG, L]) for j in range(2)] for i in range(CI)]
        self.Crep = [self.slot(f"Crep{j}", [P, NG, L]) for j in range(2)]
        for x in self.dA:
            for y in x:
                self.ve.do(lambda e: e.memset(y[:, :, 0:1], 0.0))
        self.yT = self.slot("yT", [P, CI, L])

    def softplus(self, n, ready):
        ve, ac = self.ve, self.ac
        z, a, m, dl = (x[:, 0:n, :] for x in (self.zin, self.zab, self.zmx, self.delta))
        t = ac.do(lambda e: e.activation(a, z, ACT.Abs), ready)
        t = ac.do(lambda e: e.activation(a, a, ACT.Exp, scale=-1.0), t)
        t = ac.do(lambda e: e.activation(a, a, ACT.Ln, bias=1.0), t)
        yield
        t1 = ve.do(lambda e: e.tensor_scalar(m, z, 0.0, None, ALU.max), ready)
        return ve.do(lambda e: e.tensor_tensor(dl, a, m, ALU.add), t, t1, self.delta.handed_back())

    def split3(self, ps, ready):
        ve = self.ve
        t0 = ve.do(lambda e: e.tensor_copy(self.sx[:, :], ps), ready)
        t = ve.do(lambda e: e.tensor_copy(self.sh[:, :], self.sx[:, :]), t0)
        t1 = ve.do(lambda e: e.tensor_copy(self.split[0:32, :], self.sh[0:32, :]), t, self.split.handed_back())
        t = ve.do(lambda e: e.tensor_tensor(self.sr[:, :], self.sx[:, :], self.sh[:, :], ALU.subtract), t)
        t = ve.do(lambda e: e.tensor_copy(self.sh[:, :], self.sr[:, :]), t)
        t1 = ve.do(lambda e: e.tensor_copy(self.split[32:64, :], self.sh[32:64, :]), t)
        yield
        t = ve.do(lambda e: e.tensor_tensor(self.sr[:, :], self.sr[:, :], self.sh[:, :], ALU.subtract), t)
        t = ve.do(lambda e: e.tensor_copy(self.split[64:96, :], self.sr[64:96, :]), t)
        return t0, t

    def scan(self, nch, A, u_ap, t_u, t_delta, t_split, banks, bank_y):
        ve, ac, pe, po, w = self.ve, self.ac, self.pe, self.po, self.w
        t_dtu = ve.do(lambda e: e.tensor_tensor(self.dtu[:, 0:nch, :], self.delta[:, 0:nch, :], u_ap, ALU.mult),
                      t_delta, t_u, self.dtu.handed_back())
        turn = 0
        late = []

        def spread(row, j):
            nonlocal turn
            bk = banks[turn % len(banks)]
            turn += 1
            for m in range(2):
                t = pe.do(lambda e: e.matmul(bk[:, m * L:(m + 1) * L], w["sel"][:, row + 2 * j + m, :], self.split[:, :],
                                             start=True, stop=True), t_split, bk.handed_back() if m == 0 else None)
            return bk, t

        def add_up(g, c, hv, th2):
            for n in range(2):
                tp = pe.do(lambda e: e.matmul(bank_y[:, c * L:(c + 1) * L], w["ident"], hv[:, n, :],
                                              start=g == 0 and n == 0 and c == 0, stop=g == NS // NG - 1 and n == 1,
                                              skip_group_check=True), th2,
                           bank_y.handed_back() if g == 0 and n == 0 and c == 0 else None)
            hv.hand_back(tp)

        flat = lambda x, a=0, b=NG: x[:, a:b, :].rearrange("p n t -> p (n t)")
        for g in range(NS // NG):
            r = g % 2
            Cr = self.Crep[r]
            t_dA, t_in = [None] * nch, [None] * nch
            for c in range(nch):
                for n in range(NG):
                    t_dA[c] = ac.do(lambda e: e.activation(self.dA[c][r][:, n, 1:], self.delta[:, c, 1:], ACT.Exp,
                                                           scale=A[:, c, g * NG + n:g * NG + n + 1]),
                                    t_delta, self.dA[c][r].handed_back() if n == 0 else None)
            for j in range(NG // 2):
                bk, t = spread(g * NG, j)
                for c in range(nch):
                    t_in[c] = ve.do(lambda e: e.tensor_tensor(self.h[c][r][:, 2 * j:2 * j + 2, :], bcast(self.dtu[:, c, :], 2, 1),
                                                              bk[:, :].rearrange("p (n t) -> p n t", n=2), ALU.mult),
                                    t, t_dtu, self.h[c][r].handed_back() if j == 0 else None)
                bk.hand_back(t_in[nch - 1])
                yield
            for j in range(NG // 2):
                bk, t = spread(NS + g * NG, j)
                tC = ac.do(lambda e: e.activation(flat(Cr, 2 * j, 2 * j + 2), bk[:, :], ACT.Copy), t,
                           Cr.handed_back() if j == 0 else None)
                bk.hand_back(tC)
                yield
            for f in late:
                f()
            late.clear()
            for c in range(nch):
                hv = self.h[c][r]
                t = ve.do(lambda e: e.tensor_tensor_scan(flat(hv), flat(self.dA[c][r]), flat(hv), 0.0, ALU.mult, ALU.add),
                          t_dA[c], t_in[c])
                self.dA[c][r].hand_back(t)
                th = po.do(lambda e: e.tensor_tensor(hv[:, :, :], hv[:, :, :], Cr[:, :, :], ALU.mult), t, tC)
                th2 = po.do(lambda e: e.tensor_tensor(hv[:, 0:2, :], hv[:, 0:2, :], hv[:, 2:4, :], ALU.add), th)
                late.append(lambda g=g, c=c, hv=hv, th2=th2: add_up(g, c, hv, th2))
                yield
            Cr.hand_back(th)
        yield
        for f in late:
            f()
            yield
        tp = pe.last()
        self.delta.hand_back(ac.last(), t_dtu)
        self.dtu.hand_back(t_in[nch - 1])
        self.split.hand_back(pe.last())
        self.t_scan = tp

    def alloc0(self):
        self.x1T = self.slot("x1T", [P, L])
        self.upad = self.sb("upad", [P, CI, CONV - 1 + L])
        self.upadb = Slot(self.c, "upadb", self.upad)
        self.sg = self.slot("sg", [P, CI, L])
        self.sgt = self.slot("sgt", [P, CI, L])
        self.cv = self.slot("cv", [P, CI, L])
        self.cvt = self.slot("cvt", [P, CI, L])
        self.u = self.slot("u", [P, CI, L])
        self.dtT = self.slot("dtT", [DTR, L])
        self.gz = self.slot("gz", [E0, L])
        self.gs = self.slot("gs", [E0, 4])
        self.gp = self.slot("gp", [E0, L])
        self.g8 = self.slot("g8", [E0, 8])
        self.gr = self.slot("gr", [E0, L])
        self.gv = self.slot("gv", [P, L])
        self.gvT = self.slot("gvT", [P, QT, E0])

    def gate0(self, b, k, bk):
        ve, ac, pe, w = self.ve, self.ac, self.pe, self.w
        xn, xnT = self.xn[k], self.xnT[k]
        t = pe.do(lambda e: e.matmul(bk[0:E0, 0:L], w["gate_w"], xnT[:, :], start=True, stop=True), xnT.filled(), bk.handed_back())
        t = ve.do(lambda e: e.tensor_scalar(self.gz[:, :], bk[0:E0, 0:L], w["gate_b"], None, ALU.add), t)
        bk.hand_back(t)
        yield
        t = ve.do(lambda e: e.tensor_reduce(self.gs[:, 0:1], self.gz[:, :], AX.X, ALU.max), t)
        t = ve.do(lambda e: e.tensor_scalar(self.gs[:, 1:2], self.gs[:, 0:1], -1.0, None, ALU.mult), t)
        yield
        t = ac.do(lambda e: e.activation(self.gp[:, :], self.gz[:, :], ACT.Exp, bias=self.gs[:, 1:2],
                                         accum_out=self.gs[:, 2:3]), t)
        yield
        t = ve.do(lambda e: e.reciprocal(self.gs[:, 3:4], self.gs[:, 2:3]), t)
        t = ve.do(lambda e: e.tensor_scalar(self.gp[:, :], self.gp[:, :], self.gs[:, 3:4], None, ALU.mult), t)
        self.gate(t)
        t = ve.do(lambda e: e.max(self.g8[:, :], self.gp[:, :]))
        self.gate(t)
        t = ve.do(lambda e: e.match_replace(self.gr[:, :], self.g8[:, :], self.gp[:, :], 0.0))
        yield
        t = ve.do(lambda e: e.tensor_tensor(self.gv[0:E0, :], self.gp[:, :], self.gr[:, :], ALU.subtract), t, self.gv.handed_back())
        ve.do(lambda e: e.tensor_copy(self.PT[:, bass.ds(b, 1), :].rearrange("p a t -> p (a t)"), self.gv[0:E0, :]), t)
        yield
        for q in range(QT):
            t1 = pe.do(lambda e: e.transpose(bk[:, q * P:(q + 1) * P], self.gv[:, q * P:(q + 1) * P], w["ident"]),
                       t, bk.handed_back())
        self.gv.hand_back(t1)
        yield
        t1 = ve.do(lambda e: e.tensor_copy(self.gvT[:, :, :], bk[:, 0:L].rearrange("p (q e) -> p q e", q=QT)[:, :, 0:E0]), t1,
                   self.gvT.handed_back())
        bk.hand_back(t1)
        for q in range(QT):
            t2 = pe.do(lambda e: e.matmul(bk[:, 256:256 + E0], xn[:, q, :], self.gvT[:, q, :], start=q == 0,
                                          stop=q == QT - 1), t1)
        self.gvT.hand_back(t2)
        xn.hand_back(t2)
        yield
        t2 = ve.do(lambda e: e.tensor_copy(self.merged[:, :, bass.ds(b, 1)],
                                           bk[:, 256:256 + E0].rearrange("p (e o) -> p e o", o=1)), t2)
        bk.hand_back(t2)

    def mamba(self, b):
        ve, ac, pe, w = self.ve, self.ac, self.pe, self.w
        B5, B6, B7 = self.bank[5], self.bank[6], self.bank[7]
        t = self.x1T.filled()
        for part, bk in ((0, B5), (1, B6)):
            for c in range(CI):
                tp = pe.do(lambda e: e.matmul(bk[:, c * L:(c + 1) * L], w["w_in"][:, part * CI + c, :], self.x1T[:, :],
                                              start=True, stop=True), t, bk.handed_back() if c == 0 else None)
            if part == 0:
                t0 = ac.do(lambda e: e.activation(self.upad[:, :, CONV - 1:], bk[:, :].rearrange("p (c t) -> p c t", c=CI),
                                                  ACT.Copy), tp, self.upadb.handed_back())
                bk.hand_back(t0)
            else:
                z = bk[:, :].rearrange("p (c t) -> p c t", c=CI)
                tg = yield from self.sigmoid_times(self.sg[:, :, :], z, self.sgt[:, :, :], tp, self.sg.handed_back())
                bk.hand_back(tg)
        self.x1T.hand_back(tp)
        yield
        for c in range(CI):
            t = ve.do(lambda e: e.tensor_scalar(self.cv[:, c, :], self.upad[:, c, 0:L], w["conv_w"][:, c, 0:1],
                                                w["conv_b"][:, c:c + 1], ALU.mult, ALU.add), t0)
            for j in range(1, CONV):
                t = ve.do(lambda e: e.scalar_tensor_tensor(self.cv[:, c, :], self.upad[:, c, j:j + L],
                                                           w["conv_w"][:, c, j:j + 1], self.cv[:, c, :], ALU.mult,
                                                           ALU.add), t)
            yield
        self.upadb.hand_back(t)
        tu = yield from self.sigmoid_times(self.u[:, :, :], self.cv[:, :, :], self.cvt[:, :, :], t, self.u.handed_back())
        yield
        for c in range(CI):
            t = pe.do(lambda e: e.matmul(B5[0:96, 0:L], w["w_bc"][:, c, :], self.u[:, c, :], start=c == 0,
                                         stop=c == CI - 1), tu, B5.handed_back())
        for c in range(CI):
            t = pe.do(lambda e: e.matmul(B6[0:DTR, 0:L], w["w_dtin"][:, c, :], self.u[:, c, :], start=c == 0,
                                         stop=c == CI - 1), B6.handed_back())
        yield
        td = ve.do(lambda e: e.tensor_copy(self.dtT[:, :], B6[0:DTR, 0:L]), t)
        B6.hand_back(td)
        t0, t_split = yield from self.split3(B5[0:96, 0:L], t)
        B5.hand_back(t0)
        for c in range(CI):
            t = pe.do(lambda e: e.matmul(B6[:, c * L:(c + 1) * L], w["w_dt"][:, c * P:(c + 1) * P], self.dtT[:, :],
                                         start=True, stop=True), td, B6.handed_back() if c == 0 else None)
        yield
        for c in range(CI):
            tz = ve.do(lambda e: e.tensor_scalar(self.zin[:, c, :], B6[:, c * L:(c + 1) * L], w["b_dt"][:, c:c + 1],
                                                 None, ALU.add), t)
        B6.hand_back(tz)
        t_delta = yield from self.softplus(CI, tz)
        yield
        yield from self.scan(CI, self.A0, self.u[:, :, :], tu, t_delta, t_split, (B5, B6), B7)
        for c in range(CI):
            t = ve.do(lambda e: e.scalar_tensor_tensor(self.yT[:, c, :], self.u[:, c, :], w["Dp"][:, c:c + 1],
                                                       B7[:, c * L:(c + 1) * L], ALU.mult, ALU.add),
                      self.t_scan, self.yT.handed_back())
        B7.hand_back(t)
        self.u.hand_back(t)
        yield
        t = ve.do(lambda e: e.tensor_tensor(self.yT[:, :, :], self.yT[:, :, :], self.sg[:, :, :], ALU.mult), t, tg)
        for q in range(QT):
            for c in range(CI):
                tp = pe.do(lambda e: e.matmul(B5[:, q * P:(q + 1) * P], self.yT[:, c, q * P:(q + 1) * P],
                                              w["w_out"][:, c, :], start=c == 0, stop=c == CI - 1), t,
                           B5.handed_back() if q == 0 and c == 0 else None)
        self.yT.hand_back(tp)
        yield
        t = self.add_to_x(b, B5[:, 0:L].rearrange("p (q d) -> p q d", q=QT), tp)
        B5.hand_back(t)

    def neg_exp(self, name, src, n):
        t = self.sb(name, [P, n, NS])
        m = self.ac.do(lambda e: e.activation(t[:, :, :], src, ACT.Exp))
        self.ve.do(lambda e: e.tensor_scalar(t[:, :, :], t[:, :, :], -1.0, None, ALU.mult), m)
        return t

    def layer0(self):
        ve = self.ve
        self.A0 = self.neg_exp("A0", self.w["A_log0"], CI)
        ve.do(lambda e: e.memset(self.upad[:, :, 0:CONV - 1], 0.0))
        ve.do(lambda e: e.memset(self.gv[:, :], 0.0))

        B = self.bank

        def pre(b, k):
            yield from self.layer_norm(b, k, B[4])
            yield from self.gate0(b, k, B[4])
            yield from self.qkv(0, k, B[4])

        def attend(b, k):
            yield from self.attention(0, k, B[0:2], B[2:3], B[3])
            t = ve.do(lambda e: e.tensor_tensor(self.x1[:, :, :], self.x1[:, :, :], self.xn[k][:, :, :], ALU.add), self.t_x1)
            self.xn[k].hand_back(t)
            tx = self.add_to_x(b, self.x1[:, :, :], t)
            bk = B[2]
            for q in range(QT):
                tp = self.pe.do(lambda e: e.transpose(bk[:, q * P:(q + 1) * P], self.x1[:, q, :], self.w["ident"]), t, bk.handed_back())
            self.x1.hand_back(tx, tp)
            t = ve.do(lambda e: e.tensor_copy(self.x1T[:, :], bk[:, 0:L]), tp, self.x1T.handed_back())
            bk.hand_back(t)
            self.x1T.fill(t)

        def step(b, k, last=False, mamba=True):
            self.weave((attend(b, k), "attend0"), (self.mamba(b - 1) if mamba else None, "mamba"), (None if last else pre(b + 1, 1 - k), "pre0"))

        def body(i):
            step(2 * i + 1, 1)
            step(2 * i + 2, 0)

        drain(pre(0, 0))
        step(0, 0, mamba=False)
        self.c.loop("layer0", NB // 2 - 1, body)
        step(NB - 1, 1, last=True)
        drain(self.mamba(NB - 1))

    def experts0(self):
        ve, ac, pe, w, nc = self.ve, self.ac, self.pe, self.w, self.nc
        R = 4
        w1r = [self.slot(f"w1r{i}", [P, H0]) for i in range(R)]
        w2r = [self.slot(f"w2r{i}", [P, H0 // P, D]) for i in range(R)]
        hz = [self.slot(f"hz{i}", [P, H0 // P, NB]) for i in range(2)]
        hg = [self.slot(f"hg{i}", [P, H0 // P, NB]) for i in range(2)]
        lds = [(self.c.dma_stream(nc.sync, f"e0a{i}"), self.c.dma_stream(nc.sync, f"e0b{i}")) for i in range(R)]
        w1d = self.ins["m_w1"]
        w2d = self.ins["m_w2"]
        J = H0 // P

        def body(i):
            ld = []
            for s in range(R):
                ex = i * R + s
                la = lds[s][0].do(lambda e: e.dma_start(w1r[s][:, :], w1d[bass.ds(ex, 1), 0:D, :].rearrange("a p h -> (a p) h")), w1r[s].handed_back())
                lb = lds[s][1].do(lambda e: e.dma_start(w2r[s][:, :, :], w2d[bass.ds(ex, 1), 0:H0, :].rearrange("a (j p) d -> p (a j) d", p=P)), w2r[s].handed_back())
                ld.append((la, lb))
            for s in range(R):
                ex = i * R + s
                bk, bo = self.bank[s % 2], self.bank[2 + s % 2]
                for j in range(J):
                    t = pe.do(lambda e: e.matmul(bk[:, j * NB:(j + 1) * NB], w1r[s][:, j * P:(j + 1) * P],
                                                 self.merged[:, bass.ds(ex, 1), :].rearrange("p a b -> p (a b)"), start=True, stop=True),
                              ld[s][0], bk.handed_back())
                w1r[s].hand_back(t)
                b1v = w["m_b1"][:, bass.ds(ex, 1), :].rearrange("p a j -> p (a j)")
                t = ve.do(lambda e: e.tensor_tensor(hz[s % 2][:, :, :], bk[:, 0:J * NB].rearrange("p (j b) -> p j b", j=J),
                                                    bcast(b1v, NB, 2), ALU.add), t, hz[s % 2].handed_back())
                bk.hand_back(t)
                t = ac.do(lambda e: e.activation(hg[s % 2][:, :, :], hz[s % 2][:, :, :], ACT.Gelu), t, hg[s % 2].handed_back())
                hz[s % 2].hand_back(t)
                for j in range(J):
                    t1 = pe.do(lambda e: e.matmul(bo[:, 0:NB], w2r[s][:, j, :], hg[s % 2][:, j, :], start=j == 0,
                                                  stop=j == J - 1), t, ld[s][1], bo.handed_back())
                w2r[s].hand_back(t1)
                hg[s % 2].hand_back(t1)
                b2v = w["m_b2"][:, bass.ds(ex, 1)]
                t = ve.do(lambda e: e.tensor_tensor(self.oall[:, :, bass.ds(ex, 1)], bo[:, 0:NB].rearrange("p (b o) -> p b o", o=1),
                                                    bcast(b2v, NB, 1), ALU.add), t1)
                bo.hand_back(t)
        self.c.loop("experts0", E0 // R, body, "gelu_and_others")

    def spread0(self, b, bk):
        ve, pe, w, po = self.ve, self.pe, self.w, self.po
        self.gate(self.ob.handed_back(), self.pts.handed_back())
        t = ve.do(lambda e: e.tensor_copy(self.ob[:, :], self.oall[:, bass.ds(b, 1), :].rearrange("p a e -> p (a e)")))
        tp = ve.do(lambda e: e.tensor_copy(self.pts[:, :], self.PT[:, bass.ds(b, 1), :].rearrange("p a t -> p (a t)")))
        yield
        t = pe.do(lambda e: e.transpose(bk[0:E0, 256:256 + D], self.ob[:, :], w["ident"]), t, bk.handed_back())
        self.ob.hand_back(t)
        yield
        t = ve.do(lambda e: e.tensor_copy(self.oe[:, :], bk[0:E0, 256:256 + D]), t, self.oe.handed_back())
        for q in range(QT):
            t1 = pe.do(lambda e: e.matmul(bk[:, q * P:(q + 1) * P], self.pts[:, q * P:(q + 1) * P], self.oe[:, :],
                                          start=True, stop=True), t, tp)
        yield
        self.oe.hand_back(t1)
        self.pts.hand_back(t1)
        t = self.add_to_x(b, bk[:, 0:L].rearrange("p (q d) -> p q d", q=QT), t1)
        bk.hand_back(t)
        return t

    def fp4(self, name, out, src, nblk, ready, free):
        ve, po = self.ve, self.po
        a, t_, wv_ = (x[:, 0:nblk, :] for x in self.f4)
        am, sc, hs = (x[:, 0:nblk] for x in self.f4s)
        ta = self.ac.do(lambda e: e.activation(a, src, ACT.Abs), ready, ve.last())
        t = ve.do(lambda e: e.tensor_reduce(am, src, AX.X, ALU.max, apply_absolute_value=True), ready)
        t = ve.do(lambda e: e.tensor_scalar(sc, am, float(np.float32(1.0) / np.float32(6.0)), 1e-12, ALU.mult, ALU.max), t)
        th = ve.do(lambda e: e.tensor_scalar(hs, sc, 0.5, None, ALU.mult), t)
        t = ve.do(lambda e: e.reciprocal(am, sc), t)
        yield
        t = ve.do(lambda e: e.tensor_tensor(a, a, bcast(am, BLK, 2), ALU.mult), t, ta)
        yield
        t1 = t = ve.do(lambda e: e.tensor_scalar(wv_, a, 1.75, None, ALU.is_gt), t)
        t = ve.do(lambda e: e.tensor_scalar(t_, a, 5.0, 2.0, ALU.is_gt, ALU.mult), t)
        for m in (3.5, 2.5):
            yield
            t = ve.do(lambda e: e.scalar_tensor_tensor(t_, a, m, t_, ALU.is_gt, ALU.add), t)
        yield
        t = ve.do(lambda e: e.scalar_tensor_tensor(t_, t_, 2.0, wv_, ALU.mult, ALU.add), t, t1)
        for m in (1.25, 0.75, 0.25):
            yield
            t = ve.do(lambda e: e.scalar_tensor_tensor(t_, a, m, t_, ALU.is_gt, ALU.add), t)
        t = ve.do(lambda e: e.tensor_tensor(t_, t_, bcast(hs, BLK, 2), ALU.mult), t)
        return ve.do(lambda e: e.scalar_tensor_tensor(out.bitcast(U32), src.bitcast(U32), 0x80000000, t_.bitcast(U32),
                                                      ALU.bitwise_and, ALU.bitwise_or), t, free)

    def layer1(self):
        ve, ac, pe, w = self.ve, self.ac, self.pe, self.w
        NBH = I1 // BLK
        self.f4 = [self.sb(f"f4{i}", [P, QT * NBH, BLK]) for i in range(3)]
        self.f4s = [self.sb(f"f4s{i}", [P, QT * NBH]) for i in range(3)]
        wqt = self.sb("wgu_q", [P, 6, P])
        wdq = self.sb("wd_q", [P, I1])
        wgT = self.sb("wgT", [P, I1])
        wuT = self.sb("wuT", [P, I1])
        wdT = self.sb("wdT", [P, 3, D])
        xq = self.slot("xq", [P, QT, D])
        xqT = self.slot("xqT", [P, L])
        hh = self.slot("hh", [P, QT, I1])
        he = self.slot("he", [P, I1])
        hq = self.slot("hq", [P, QT, I1])
        hqT = self.slot("hqT", [P, 3, L])
        blk = lambda ap: ap.rearrange("p (n k) -> p n k", k=BLK)
        B6, B7 = self.bank[6], self.bank[7]
        t = ve.last()
        raw = w["wgu1"]
        for i in range(6):
            t = drain(self.fp4("w", blk(wqt[:, i, :]), blk(raw[:, i, :]), D // BLK, t, None))
        t = drain(self.fp4("w", blk(wdq[:, :]), blk(w["wd1"]), NBH, t, None))
        for i in range(6):
            dst = wgT if i < 3 else wuT
            rows = min(P, I1 - (i % 3) * P)
            tp = pe.do(lambda e: e.transpose(B6[:, 0:rows], wqt[0:rows, i, :], w["ident"][0:rows, 0:rows]), t, B6.handed_back())
            tc = ve.do(lambda e: e.tensor_copy(dst[:, (i % 3) * P:(i % 3) * P + rows], B6[:, 0:rows]), tp)
            B6.hand_back(tc)
        for i in range(3):
            rows = min(P, I1 - i * P)
            tp = pe.do(lambda e: e.transpose(B6[0:rows, 0:P], wdq[:, i * P:i * P + rows], w["ident"]), t, B6.handed_back())
            tc = ve.do(lambda e: e.tensor_copy(wdT[0:rows, i, :], B6[0:rows, 0:P]), tp)
            B6.hand_back(tc)

        def ffn(b, k):
            xn = self.xn[k]
            t = yield from self.fp4("x", xq[:, :, :].rearrange("p q (n k) -> p (q n) k", k=BLK),
                         xn[:, :, :].rearrange("p q (n k) -> p (q n) k", k=BLK), QT * D // BLK, xn.filled(), xq.handed_back())
            xn.hand_back(t, pe.last())
            for q in range(QT):
                tp = pe.do(lambda e: e.transpose(B7[:, q * P:(q + 1) * P], xq[:, q, :], w["ident"]), t, B7.handed_back())
            xq.hand_back(tp)
            yield
            t = ac.do(lambda e: e.activation(xqT[:, :], B7[:, 0:L], ACT.Copy), tp, xqT.handed_back())
            B7.hand_back(t)
            yield
            for q in range(QT):
                tg = pe.do(lambda e: e.matmul(B6[:, 0:I1], xqT[:, q * P:(q + 1) * P], wgT[:, :], start=True, stop=True), t, B6.handed_back())
                tu = pe.do(lambda e: e.matmul(B7[:, 0:I1], xqT[:, q * P:(q + 1) * P], wuT[:, :], start=True, stop=True), B7.handed_back())
                ts = yield from self.sigmoid_times(hh[:, q, :], B6[:, 0:I1], he[:, :], tg, None)
                B6.hand_back(ts)
                th = ve.do(lambda e: e.tensor_tensor(hh[:, q, :], hh[:, q, :], B7[:, 0:I1], ALU.mult), ts, tu)
                B7.hand_back(th)
                yield
            xqT.hand_back(tu)
            t = yield from self.fp4("h", hq[:, :, :].rearrange("p q (n k) -> p (q n) k", k=BLK),
                         hh[:, :, :].rearrange("p q (n k) -> p (q n) k", k=BLK), QT * NBH, th, hq.handed_back())
            yield
            for ch in range(3):
                rows = min(P, I1 - ch * P)
                bk = B6 if ch % 2 == 0 else B7
                for q in range(QT):
                    tp = pe.do(lambda e: e.transpose(bk[0:rows, q * P:(q + 1) * P], hq[:, q, ch * P:ch * P + rows],
                                                     w["ident"]), t, bk.handed_back())
                yield
                tc = ac.do(lambda e: e.activation(hqT[0:rows, ch, :], bk[0:rows, 0:L], ACT.Copy), tp, hqT.handed_back())
                bk.hand_back(tc)
            hq.hand_back(tp)
            for q in range(QT):
                for ch in range(3):
                    rows = min(P, I1 - ch * P)
                    tp = pe.do(lambda e: e.matmul(B7[:, q * P:(q + 1) * P], hqT[0:rows, ch, q * P:(q + 1) * P],
                                                  wdT[0:rows, ch, :], start=ch == 0, stop=ch == 2), tc, B7.handed_back() if q == 0 and ch == 0 else None)
            hqT.hand_back(tp)
            yield
            t = self.add_to_x(b, B7[:, 0:L].rearrange("p (q d) -> p q d", q=QT), tp)
            B7.hand_back(t)
            yield

        B = self.bank

        def pre(b, k):
            t = (yield from self.spread0(b, B[4])) if 0 in self.debug else None
            yield from self.layer_norm(b, k, B[4], t)
            yield from self.qkv(1, k, B[4])

        def attend(b, k):
            yield from self.attention(1, k, B[0:2], [B[2], B[5]], B[3])
            t = self.add_to_x(b, self.x1[:, :, :], self.t_x1)
            self.x1.hand_back(t)

        def step(b, k, last=False):
            self.weave((attend(b, k), "attend1"), (ffn(b, k), "ffn1"), (None if last else pre(b + 1, 1 - k), "pre1"))

        self.steps("layer1", pre, step)

    def steps(self, name, pre, step):
        def body(i):
            step(2 * i, 0)
            step(2 * i + 1, 1)

        drain(pre(0, 0))
        self.c.loop(name, NB // 2 - 1, body)
        step(NB - 2, 0)
        step(NB - 1, 1, last=True)

    def layer2(self):
        ve, ac, pe, po, w, nc = self.ve, self.ac, self.pe, self.po, self.w, self.nc
        XN = self.sb("XN", [P, NT, D])
        LG = self.sb("LG", [P, NT, E2])
        if 0 in self.debug and 1 not in self.debug:
            self.c.loop("spread0", NB, lambda b: drain(self.spread0(b, self.bank[7])))
        zero = self.sb("zero", [P, 512])
        t = ve.do(lambda e: e.memset(zero[:, :], 0.0))
        rows = nc.dram_tensor("slots", [E2 * CAP + NB * L, D], F32, kind="Internal").ap()
        zr = self.c.dma_stream(nc.sync, "zero_slots")
        ow = [self.c.dma_stream(nc.sync, f"own_rows{k}") for k in range(2)]
        for i in range(4):
            zr.do(lambda e: e.dma_start(rows[i * 512:(i + 1) * 512, :].rearrange("(p r) d -> p (r d)", p=P), zero[:, :]), t)
        own = rows[E2 * CAP:, :].rearrange("(t p) d -> p t d", p=P)

        B = self.bank

        def pre(b, k):
            bk, xn, xnT = B[4], self.xn[k], self.xnT[k]
            yield from self.layer_norm(b, k, bk)
            for q in range(QT):
                t = pe.do(lambda e: e.matmul(bk[:, q * E2:(q + 1) * E2], xnT[:, q * P:(q + 1) * P], w["w_switch"],
                                             start=True, stop=True), xnT.filled(), bk.handed_back())
            t = ve.do(lambda e: e.tensor_tensor(LG[:, bass.ds(b * QT, QT), :], bk[:, 0:QT * E2].rearrange("p (q e) -> p q e", q=QT),
                                                bcast(w["b_switch"], QT, 1), ALU.add), t)
            bk.hand_back(t)
            self.gate_po(xn.filled())
            t = po.do(lambda e: e.tensor_copy(XN[:, bass.ds(b * QT, QT), :], xn[:, :, :]))
            td = ow[k].do(lambda e: e.dma_start(own[:, bass.ds(b * QT, QT), :], xn[:, :, :]), xn.filled())
            xn.hand_back(t, td, pe.last())
            yield from self.qkv(2, k, bk)

        def attend(b, k):
            yield from self.attention(2, k, B[0:2], [B[2], B[5]], B[3])
            t = self.add_to_x(b, self.x1[:, :, :], self.t_x1)
            self.x1.hand_back(t)

        self.steps("layer2", pre, lambda b, k, last=False: self.weave((attend(b, k), "attend2"), (None if last else pre(b + 1, 1 - k), "pre2")))

        prb = self.sb("prb", [P, NT, E2])
        m1 = self.sb("m1", [P, NT])
        pm = self.sb("pm", [P, NT])
        m8 = self.sb("m8", [P, NT, 8])
        i8 = self.sb("i8", [P, NT, 8], U32)
        rt = self.sb("rt", [P, NT])
        oh = self.sb("oh", [P, NT, E2])
        ohb = self.sb("ohb", [P, NT * E2], BF16)
        tot = self.sb("tot", [P, NT, E2])
        off = self.sb("off", [P, NT, E2])
        pos = self.sb("pos", [P, NT])
        keep = self.sb("keep", [P, NT])
        slot = self.sb("slot", [P, NT])
        sloti = self.sb("sloti", [P, NT], I32)
        B0, B1 = self.bank[0], self.bank[1]
        do = lambda f, *n: ve.do(f, ve.last(), *n)
        self.c.join()
        do(lambda e: e.tensor_reduce(m1[:, :], LG[:, :, :], AX.X, ALU.max))
        t = do(lambda e: e.tensor_tensor(prb[:, :, :], LG[:, :, :], bcast(m1[:, :], E2, 2), ALU.subtract))
        t = ac.do(lambda e: e.activation(prb[:, :, :], prb[:, :, :], ACT.Exp), t)
        do(lambda e: e.tensor_reduce(m1[:, :], prb[:, :, :], AX.X, ALU.add), t)
        do(lambda e: e.reciprocal(m1[:, :], m1[:, :]))
        do(lambda e: e.tensor_tensor(prb[:, :, :], prb[:, :, :], bcast(m1[:, :], E2, 2), ALU.mult))
        do(lambda e: e.tensor_reduce(pm[:, :], prb[:, :, :], AX.X, ALU.max))
        do(lambda e: e.reciprocal(m1[:, :], pm[:, :]))
        scl = self.sb("scl", [P, NT])
        do(lambda e: e.tensor_tensor(scl[:, :], pm[:, :], m1[:, :], ALU.mult))
        t = ve.last()
        self.gate(t)
        for i in range(NT):
            t = ve.do(lambda e: e.max(m8[:, i, :], prb[:, i, :]))
        self.gate(t)
        for i in range(NT):
            ve.do(lambda e: e.max_index(i8[:, i, :], m8[:, i, :], prb[:, i, :]))
        do(lambda e: e.tensor_copy(rt[:, :], i8[:, :, 0]))
        t = do(lambda e: e.tensor_tensor(oh[:, :, :], bcast(w["iota8"], NT, 1), bcast(rt[:, :], E2, 2), ALU.is_equal))
        t = do(lambda e: e.tensor_copy(ohb[:, :], oh[:, :, :].rearrange("p t e -> p (t e)")))
        ta = pe.do(lambda e: e.matmul(B0[:, 0:NT * E2], w["upto"], ohb[:, :], start=True, stop=True), t, B0.handed_back())
        tb = pe.do(lambda e: e.matmul(B1[:, 0:NT * E2], w["onesb"], ohb[:, :], start=True, stop=True), B1.handed_back())
        do(lambda e: e.tensor_copy(tot[:, :, :], B1[:, 0:NT * E2].rearrange("p (t e) -> p t e", t=NT)), tb)
        do(lambda e: e.memset(off[:, 0, :], 0.0))
        for i in range(1, NT):
            do(lambda e: e.tensor_tensor(off[:, i, :], off[:, i - 1, :], tot[:, i - 1, :], ALU.add))
        do(lambda e: e.tensor_tensor(off[:, :, :], off[:, :, :], B0[:, 0:NT * E2].rearrange("p (t e) -> p t e", t=NT), ALU.add), ta)
        do(lambda e: e.tensor_tensor(off[:, :, :], off[:, :, :], oh[:, :, :], ALU.mult))
        do(lambda e: e.tensor_reduce(pos[:, :], off[:, :, :], AX.X, ALU.add))
        do(lambda e: e.tensor_scalar(pos[:, :], pos[:, :], -1.0, None, ALU.add))
        do(lambda e: e.tensor_scalar(keep[:, :], pos[:, :], float(CAP), None, ALU.is_lt))
        do(lambda e: e.scalar_tensor_tensor(slot[:, :], rt[:, :], float(CAP), pos[:, :], ALU.mult, ALU.add))
        do(lambda e: e.tensor_tensor(slot[:, :], slot[:, :], w["own"], ALU.subtract))
        do(lambda e: e.tensor_tensor(slot[:, :], slot[:, :], keep[:, :], ALU.mult))
        do(lambda e: e.tensor_tensor(slot[:, :], slot[:, :], w["own"], ALU.add))
        t = do(lambda e: e.tensor_copy(sloti[:, :], slot[:, :]))
        sct = self.c.dma_stream(nc.gpsimd, "scatter")
        self.c.join()
        for i in range(NT):
            sct.do(lambda e: e.indirect_dma_start(out=rows, out_offset=bass.IndirectOffsetOnAxis(ap=sloti[:, i:i + 1].bitcast(U32), axis=0),
                                                  in_=XN[:, i, :], in_offset=None))
        w1r = [self.slot(f"w1s{i}", [P, H2]) for i in range(2)]
        w2r = [self.slot(f"w2s{i}", [P, H2 // P, D]) for i in range(2)]
        bb = [self.slot(f"bb{i}", [P, QT, D]) for i in range(2)]
        bT = [self.slot(f"bT{i}", [P, CAP]) for i in range(2)]
        hT = [self.slot(f"hT{i}", [P, H2 // P, CAP]) for i in range(2)]
        yy = [self.slot(f"yy{i}", [P, QT, D]) for i in range(2)]
        lw = [(self.c.dma_stream(nc.sync, f"e2a{i}"), self.c.dma_stream(nc.sync, f"e2b{i}"), self.c.dma_stream(nc.sync, f"e2c{i}"),
               self.c.dma_stream(nc.scalar, f"e2d{i}")) for i in range(2)]
        J = H2 // P

        def ebody(i):
            lds = []
            for s in range(2):
                ex = i * 2 + s
                la = lw[s][0].do(lambda e: e.dma_start(w1r[s][:, :], self.ins["s_w1"][bass.ds(ex, 1), :, :].rearrange("a p h -> (a p) h")), w1r[s].handed_back())
                lb = lw[s][1].do(lambda e: e.dma_start(w2r[s][:, :, :], self.ins["s_w2"][bass.ds(ex, 1), :, :].rearrange("a (j p) d -> p (a j) d", p=P)), w2r[s].handed_back())
                lc = lw[s][2].do(lambda e: e.dma_start(bb[s][:, :, :], rows[bass.ds(ex * CAP, CAP), :].rearrange("(q p) d -> p q d", p=P)), bb[s].handed_back())
                lds.append((la, lb, lc))
            for s in range(2):
                ex = i * 2 + s
                la, lb, lc = lds[s]
                bt = self.bank[s]
                for q in range(QT):
                    t = pe.do(lambda e: e.transpose(bt[:, q * P:(q + 1) * P], bb[s][:, q, :], w["ident"]), lc, bt.handed_back())
                bb[s].hand_back(t)
                tT = ve.do(lambda e: e.tensor_copy(bT[s][:, :], bt[:, 0:CAP]), t, bT[s].handed_back())
                bt.hand_back(tT)
                for j in range(J):
                    bh = self.bank[2 + j % 4]
                    t = pe.do(lambda e: e.matmul(bh[:, 0:CAP], w1r[s][:, j * P:(j + 1) * P], bT[s][:, :], start=True, stop=True),
                              la, tT, bh.handed_back())
                    th = ac.do(lambda e: e.activation(hT[s][:, j, :], bh[:, 0:CAP], ACT.Relu,
                                                      bias=w["s_b1"][:, bass.ds(ex, 1), j:j + 1].rearrange("p a j -> p (a j)")),
                               t, hT[s].handed_back() if j == 0 else None)
                    bh.hand_back(th)
                w1r[s].hand_back(t)
                bT[s].hand_back(t)
                by = self.bank[6 + s]
                for q in range(QT):
                    for j in range(J):
                        t = pe.do(lambda e: e.matmul(by[:, q * P:(q + 1) * P], hT[s][:, j, q * P:(q + 1) * P], w2r[s][:, j, :],
                                                     start=j == 0, stop=j == J - 1), th, lb, by.handed_back() if q == 0 and j == 0 else None)
                w2r[s].hand_back(t)
                hT[s].hand_back(t)
                t = ve.do(lambda e: e.tensor_tensor(yy[s][:, :, :], by[:, 0:CAP].rearrange("p (q d) -> p q d", q=QT),
                                                    bcast(w["s_b2"][:, bass.ds(ex, 1), :].rearrange("p a d -> p (a d)"), QT, 1), ALU.add),
                          t, yy[s].handed_back())
                by.hand_back(t)
                t = lw[s][3].do(lambda e: e.dma_start(rows[bass.ds(ex * CAP, CAP), :].rearrange("(q p) d -> p q d", p=P), yy[s][:, :, :]), t, lc)
                yy[s].hand_back(t)
        self.c.loop("experts2", E2 // 2, ebody)
        gat = self.c.dma_stream(nc.gpsimd, "gather")
        YG = XN
        for i in range(NT):
            t = gat.do(lambda e: e.indirect_dma_start(out=YG[:, i, :], out_offset=None, in_=rows,
                                                      in_offset=bass.IndirectOffsetOnAxis(ap=sloti[:, i:i + 1].bitcast(U32), axis=0)))
        do(lambda e: e.tensor_tensor(YG[:, :, :], YG[:, :, :], bcast(scl[:, :], D, 2), ALU.mult), t)
        do(lambda e: e.tensor_tensor(self.X[:, :, :], self.X[:, :, :], YG[:, :, :], ALU.add))

    def layer3(self):
        ve, ac, pe, po, w = self.ve, self.ac, self.pe, self.po, self.w
        A3 = self.neg_exp("A3", w["A_log3"], 1)
        m = ve.do(lambda e: e.tensor_scalar(w["ctx"], w["ctx"], w["ctx_scale"], None, ALU.mult))
        sT = self.slot("sT", [P, L])
        st = self.slot("st", [P, QT, D])
        lT = self.slot("lT", [P, L])
        lg = self.slot("lg3", [P, QT, E3])
        m8 = self.slot("m83", [P, QT, 8])
        i8 = self.slot("i83", [P, QT, 8], U32)
        rf = self.slot("rf3", [P, QT, 8])
        g2 = self.slot("g23", [P, QT, 2])
        gt = self.slot("gt3", [P, QT, E3])
        gt2 = self.slot("gt23", [P, QT, E3])
        NH = E3 * H3
        hz = self.slot("hz3", [P, NH + SH3 * H3])
        hs = self.slot("hs3", [P, NH + SH3 * H3])
        he = self.slot("he3", [P, NH + SH3 * H3])
        hT = self.slot("hT3", [P, 5, P])
        acc = self.slot("acc3", [P, QT, D])
        B = self.bank
        st_out = self.c.dma_stream(self.nc.sync, "store")
        outv = self.out.rearrange("(t p) d -> p t d", p=P)

        def ssm(b, k):
            B5, B6, B7 = B[5], B[6], B[7]
            xnT = self.xnT[k]
            txnT = xnT.filled()
            t = pe.do(lambda e: e.matmul(B5[0:96, 0:L], w["w_bc3"], xnT[:, :], start=True, stop=True), txnT, B5.handed_back())
            yield
            t0, t_split = yield from self.split3(B5[0:96, 0:L], t)
            B5.hand_back(t0)
            t = pe.do(lambda e: e.matmul(B6[:, 0:L], w["w_delta"], xnT[:, :], start=True, stop=True), B6.handed_back())
            yield
            t = ve.do(lambda e: e.tensor_copy(self.zin[:, 0, :], B6[:, 0:L]), t)
            B6.hand_back(t)
            t_delta = yield from self.softplus(1, t)
            u = xnT[:, :].rearrange("p (c t) -> p c t", c=1)
            yield from self.scan(1, A3, u, txnT, t_delta, t_split, (B5, B6), B7)
            yield
            t = ac.do(lambda e: e.activation(sT[:, :], B7[:, 0:L], ACT.Copy), self.t_scan, sT.handed_back())
            B7.hand_back(t)
            for q in range(QT):
                t1 = pe.do(lambda e: e.transpose(B5[:, q * P:(q + 1) * P], sT[:, q * P:(q + 1) * P], w["ident"]), t, B5.handed_back())
            sT.hand_back(t1)
            yield
            t = ve.do(lambda e: e.tensor_copy(st[:, :, :], B5[:, 0:L].rearrange("p (q d) -> p q d", q=QT)), t1, st.handed_back())
            B5.hand_back(t)
            for t5 in self.normalise(st, st, t, 1):
                if t5 is None:
                    yield
            for q in range(QT):
                t1 = pe.do(lambda e: e.transpose(B5[:, q * P:(q + 1) * P], st[:, q, :], w["ident"]), t5, B5.handed_back())
            st.hand_back(t1)
            yield
            t = ve.do(lambda e: e.tensor_scalar(lT[:, :], B5[:, 0:L], w["gamma"], w["beta"], ALU.mult, ALU.add), t1, lT.handed_back())
            B5.hand_back(t)
            for q in range(QT):
                t1 = pe.do(lambda e: e.matmul(B5[:, q * P:(q + 1) * P], lT[:, q * P:(q + 1) * P], w["ctx"], start=True, stop=True), t, B5.handed_back() if q == 0 else None)
            lT.hand_back(t1)
            yield
            t = self.add_to_x(b, B5[:, 0:L].rearrange("p (q d) -> p q d", q=QT), t1)
            B5.hand_back(t)
            yield

        def moe(b, k):
            xnT = self.xnT[k]
            for q in range(QT):
                t = pe.do(lambda e: e.matmul(B[3][:, q * E3:(q + 1) * E3], xnT[:, q * P:(q + 1) * P], w["router_w"],
                                             start=True, stop=True), xnT.filled(), B[3].handed_back())
            yield
            t = ve.do(lambda e: e.tensor_tensor(lg[:, :, :], B[3][:, 0:QT * E3].rearrange("p (q e) -> p q e", q=QT),
                                                bcast(w["router_b"], QT, 1), ALU.add), t)
            B[3].hand_back(t)
            self.gate(t)
            for q in range(QT):
                t = ve.do(lambda e: e.max(m8[:, q, :], lg[:, q, :]))
            self.gate(t)
            for q in range(QT):
                t = ve.do(lambda e: e.max_index(i8[:, q, :], m8[:, q, :], lg[:, q, :]))
            yield
            do = lambda f, *n: ve.do(f, ve.last(), *n)
            t = do(lambda e: e.tensor_tensor(g2[:, :, 1], m8[:, :, 1], m8[:, :, 0], ALU.subtract))
            t = ac.do(lambda e: e.activation(g2[:, :, 1], g2[:, :, 1], ACT.Exp), t)
            do(lambda e: e.tensor_copy(rf[:, :, :], i8[:, :, :]))
            yield
            do(lambda e: e.tensor_scalar(g2[:, :, 0], g2[:, :, 1], 1.0, None, ALU.add), t)
            do(lambda e: e.reciprocal(g2[:, :, 0], g2[:, :, 0]))
            do(lambda e: e.tensor_tensor(g2[:, :, 1], g2[:, :, 1], g2[:, :, 0], ALU.mult))
            yield
            for k, dst in ((0, gt), (1, gt2)):
                do(lambda e: e.tensor_tensor(dst[:, :, :], bcast(w["iota8"], QT, 1), bcast(rf[:, :, k], E3, 2), ALU.is_equal))
                do(lambda e: e.tensor_tensor(dst[:, :, :], dst[:, :, :], bcast(g2[:, :, k], E3, 2), ALU.mult))
            tgt = do(lambda e: e.tensor_tensor(gt[:, :, :], gt[:, :, :], gt2[:, :, :], ALU.add))
            yield
            NA = NH + SH3 * H3
            for q in range(QT):
                xl = xnT[:, q * P:(q + 1) * P]
                tm = []
                for bk, wt, c0, cn in ((B[0], "x_w1", 0, 512), (B[1], "x_w1", 512, 128), (B[2], "x_w3", 0, 512), (B[3], "x_w3", 512, 128)):
                    tm.append(pe.do(lambda e: e.matmul(bk[:, 0:cn], xl, w[wt][:, c0:c0 + cn], start=True, stop=True), bk.handed_back()))
                for j, (c0, cn) in enumerate(((0, 512), (512, 128))):
                    t = yield from self.sigmoid_times(hs[:, c0:c0 + cn], B[j][:, 0:cn], he[:, c0:c0 + cn], tm[j], hs.handed_back() if j == 0 else None)
                    B[j].hand_back(t)
                    yield
                    t = ve.do(lambda e: e.tensor_tensor(hs[:, c0:c0 + cn], hs[:, c0:c0 + cn], B[2 + j][:, 0:cn], ALU.mult), t, tm[2 + j])
                    B[2 + j].hand_back(t)
                v = hs[:, 0:NH].rearrange("p (e h) -> p e h", e=E3)
                tg = ve.do(lambda e: e.tensor_tensor(v, v, bcast(gt[:, q, :], H3, 2), ALU.mult), t, tgt)
                yield
                for ch in range(5):
                    bk, o = (B[0], ch * P) if ch < 4 else (B[1], 0)
                    t = pe.do(lambda e: e.transpose(bk[:, o:o + P], hs[:, ch * P:(ch + 1) * P], w["ident"]), tg, bk.handed_back() if ch in (0, 4) else None)
                hs.hand_back(t)
                yield
                t1 = ac.do(lambda e: e.activation(hT[:, 0:4, :].rearrange("p c t -> p (c t)"), B[0][:, :], ACT.Copy), t, hT.handed_back())
                t2 = ac.do(lambda e: e.activation(hT[:, 4, :], B[1][:, 0:P], ACT.Copy), t)
                B[0].hand_back(t1)
                B[1].hand_back(t2)
                for ch in range(5):
                    t = pe.do(lambda e: e.matmul(B[3][:, 0:D], hT[:, ch, :], w["x_w2"][:, ch, :], start=ch == 0, stop=ch == 4),
                              t2, B[3].handed_back() if ch == 0 else None)
                hT.hand_back(t)
                yield
                xv = self.X[:, bass.ds(b * QT + q, 1), :].rearrange("p a d -> p (a d)")
                t = ve.do(lambda e: e.tensor_tensor(xv, xv, B[3][:, 0:D], ALU.add), t, self.Xw.filled())
                self.Xw.fill(t)
                B[3].hand_back(t)
                yield
            gt.hand_back(tg)

        def pre(b, k):
            yield from self.layer_norm(b, k, B[4])

        def step(b, k, last=False):
            self.weave((ssm(b, k), "ssm3"), (moe(b, k), "moe3"), (None if last else pre(b + 1, 1 - k), "pre3"))
            self.xnT[k].hand_back(pe.last(), ve.last())
            st_out.do(lambda e: e.dma_start(outv[:, bass.ds(b * QT, QT), :], self.X[:, bass.ds(b * QT, QT), :]), self.Xw.filled())

        self.steps("layer3", pre, step)

    def build(self):
        self.load_all()
        self.PT = self.sb("PT", [E0, NB, L])
        self.merged = self.sb("merged", [P, E0, NB])
        self.oall = self.sb("oall", [P, NB, E0])
        self.ob = self.slot("ob", [P, E0])
        self.oe = self.slot("oe", [E0, D])
        self.pts = self.slot("pts", [E0, L])
        if 0 in self.debug:
            with self.scope():
                self.load_packs("wf0")
                self.alloc_common(0)
                self.alloc_scan(CI)
                self.alloc0()
                self.layer0()
            with self.scope():
                self.load_packs("wf0e")
                self.experts0()
        if 1 in self.debug:
            with self.scope():
                self.load_packs("wf1")
                self.alloc_common(1)
                self.layer1()
        if 2 in self.debug:
            with self.scope():
                self.load_packs("wf2")
                self.alloc_common(2)
                self.layer2()
        if 3 in self.debug:
            with self.scope():
                self.load_packs("wf3")
                self.alloc_common(3)
                self.alloc_scan(1)
                self.layer3()
        else:
            if 0 in self.debug and 1 not in self.debug and 2 not in self.debug:
                self.c.loop("spread0", NB, lambda b: drain(self.spread0(b, self.bank[7])))
            st = self.c.dma_stream(self.nc.sync, "store")
            st.do(lambda e: e.dma_start(self.out.rearrange("(t p) d -> p t d", p=P), self.X[:, :, :]))
        self.c.join()
        self.stack.close()


def _packs(i):
    f = lambda a: np.asarray(a, np.float32) if np.asarray(a).dtype != np.float32 else np.asarray(a)
    g = {k: f(v) for k, v in i.items()}
    packs = {"wf": []}
    bf = []
    cur = ["wf"]

    def layer(name):
        packs[name] = []
        cur[0] = name

    def put(name, a, shape=None):
        a = np.asarray(a)
        shape = shape or a.shape[1:]
        packs[cur[0]].append((name, a.reshape(a.shape[0], -1), tuple(shape)))

    def rep(v):
        return np.broadcast_to(np.asarray(v).reshape(1, -1), (P, np.asarray(v).size))

    def heads4(wm):
        out = np.zeros((wm.shape[0], 4, 4, 32), np.float32)
        out[:, :, :, 0:8] = wm.reshape(wm.shape[0], 4, 4, 8)
        return out.reshape(wm.shape[0], 4, P)

    def bias4(b):
        return heads4(b.reshape(1, P))[0].T

    put("ident", np.eye(P, dtype=np.float32))
    put("eps", np.full((P, 1), EPS, np.float32))
    put("iota8", rep(np.arange(8, dtype=np.float32)))
    put("own", (E2 * CAP + np.arange(NT)[None, :] * P + np.arange(P)[:, None]).astype(np.float32))
    layer("wf0")
    wqkv, bqkv = g["L0_attn_wqkv"], g["L0_attn_bqkv"]
    put("wq0", heads4(wqkv[:, :P]))
    put("bq0", bias4(bqkv[:P]))
    put("wk0", heads4(np.tile(wqkv[:, P:P + 8], (1, HEADS)))[:, 0:1])
    put("bk0", bias4(np.tile(bqkv[P:P + 8], HEADS))[:, 0:1])
    put("wv0", wqkv[:, P + 8:])
    put("bv0", rep(bqkv[P + 8:]))
    put("wo0", g["L0_attn_w_attn_out"].reshape(P, 1, D))
    put("bo0", rep(g["L0_attn_b_attn_out"]))
    put("w_in", g["L0_attn_w_in"].reshape(D, 2 * CI, P))
    ch = lambda a: np.swapaxes(a.reshape(CI, P, -1), 0, 1)
    put("conv_w", ch(g["L0_attn_conv_w"]))
    put("conv_b", ch(g["L0_attn_conv_b"])[:, :, 0])
    xp = ch(g["L0_attn_w_xproj"])
    put("w_dtin", np.ascontiguousarray(xp[:, :, :DTR]))
    put("w_bc", np.tile(xp[:, :, DTR:], (1, 1, 3)))
    put("w_dt", g["L0_attn_w_dt"])
    put("b_dt", ch(g["L0_attn_b_dt"])[:, :, 0])
    put("A_log0", ch(g["L0_attn_A_log"]))
    put("Dp", ch(g["L0_attn_Dp"])[:, :, 0])
    put("w_out", ch(g["L0_attn_w_out"]))
    put("gate_w", g["L0_ffn_gate_w"].T)
    put("gate_b", g["L0_ffn_gate_b"].reshape(E0, 1))
    layer("wf0e")
    w1, w2 = g["L0_ffn_w1"], g["L0_ffn_w2"]
    put("m_b1", w1[:, D, :].reshape(E0, H0 // P, P).transpose(2, 0, 1))
    put("m_b2", w2[:, H0, :].T)
    layer("wf1")
    for n in "qk":
        put(f"w{n}1", g[f"L1_attn_W{n}"].transpose(1, 0, 2).reshape(D, 8, P))
        put(f"b{n}1", g[f"L1_attn_b{n}"].reshape(8, P).T)
    put("wv1", g["L1_attn_Wv"].transpose(1, 0, 2).reshape(D, HEADS * A1))
    put("bv1", rep(g["L1_attn_bv"]))
    put("wo1", g["L1_attn_Wo"].reshape(8, P, D).transpose(1, 0, 2))
    put("bo1", rep(g["L1_attn_bo"]))
    pad = lambda a: np.concatenate([a, np.zeros((3 * P - I1, a.shape[1]), np.float32)]).reshape(3, P, -1).transpose(1, 0, 2)
    put("wgu1", np.concatenate([pad(g["L1_ffn_w_gate"]), pad(g["L1_ffn_w_up"])], 1))
    put("wd1", g["L1_ffn_w_down"])
    layer("wf2")
    for n in "qk":
        put(f"w{n}2", heads4(g[f"L2_attn_W{n}"].T))
        put(f"b{n}2", bias4(g[f"L2_attn_b{n}"]))
    put("wv2", g["L2_attn_Wv"].T)
    put("bv2", rep(g["L2_attn_bv"]))
    put("wo2", g["L2_attn_Wo"].T.reshape(P, 1, D))
    put("bo2", rep(g["L2_attn_bo"]))
    put("w_switch", g["L2_ffn_w_switch"])
    put("b_switch", rep(g["L2_ffn_b_switch"]))
    put("s_b1", g["L2_ffn_b1"].reshape(E2, H2 // P, P).transpose(2, 0, 1))
    put("s_b2", rep(g["L2_ffn_b2"]), (E2, D))
    layer("wf3")
    put("A_log3", g["L3_attn_A_log"].reshape(P, 1, NS))
    put("w_delta", g["L3_attn_W_delta"].T)
    put("w_bc3", np.tile(np.concatenate([g["L3_attn_W_B"], g["L3_attn_W_C"]]).T, (1, 3)))
    put("gamma", g["L3_attn_ln_gamma"].reshape(P, 1))
    put("beta", g["L3_attn_ln_beta"].reshape(P, 1))
    put("ctx", g["L3_attn_W_ctx"].T)
    put("ctx_scale", rep(g["L3_attn_context_scale"]))
    put("router_w", g["L3_ffn_router_w"])
    put("router_b", rep(g["L3_ffn_router_b"]))
    for n in ("w1", "w3"):
        a = np.concatenate([g["L3_ffn_routed_" + n], g["L3_ffn_shared_" + n]])
        put("x_" + n, a.transpose(1, 0, 2).reshape(D, -1))
    a = np.concatenate([g["L3_ffn_routed_w2"], g["L3_ffn_shared_w2"]])
    put("x_w2", a.reshape(5, P, D).transpose(1, 0, 2))
    tri = np.where(np.arange(P)[:, None] >= np.arange(P)[None, :], 0.0, NEG)

    def putb(name, a):
        a = np.asarray(a)
        bf.append((name, a.reshape(a.shape[0], -1).astype(np.float32), tuple(a.shape[1:])))

    putb("identb", np.eye(P))
    putb("mask0", tri)
    putb("mask1", np.concatenate([np.zeros((P, P)), tri], 1))
    putb("upto", (np.arange(P)[:, None] <= np.arange(P)[None, :]).astype(np.float32))
    putb("onesb", np.ones((P, P)))
    putb("sel", np.arange(96)[:, None] % 32 == np.arange(32)[None, :])

    packed, arrays = {}, {}
    packs["wb"] = bf
    for pname, items in packs.items():
        off, parts, cols = 0, {}, []
        for name, a, shape in items:
            parts[name] = (off, a.shape[0], shape)
            full = np.zeros((P, a.shape[1]), a.dtype)
            full[:a.shape[0]] = a
            cols.append(full)
            off += a.shape[1]
        arrays[pname] = np.ascontiguousarray(np.concatenate(cols, 1))
        packed[pname] = (off, parts)
    return packed, arrays


LAYERS = (0, 1, 2, 3)


def kernel(**inputs):
    import concourse.bacc as _bacc
    from concourse.bass_utils import run_bass_kernel_spmd as _run

    inputs = {k: np.asarray(v) for k, v in inputs.items()}
    packed, arrays = _packs(inputs)
    arrays["x"] = np.ascontiguousarray(inputs["L0_attn_x"]).reshape(NB * L, D)
    arrays["m_w1"] = np.ascontiguousarray(inputs["L0_ffn_w1"])
    arrays["m_w2"] = np.ascontiguousarray(inputs["L0_ffn_w2"])
    arrays["s_w1"] = np.ascontiguousarray(inputs["L2_ffn_w1"])
    arrays["s_w2"] = np.ascontiguousarray(inputs["L2_ffn_w2"])
    turn_ends = {}
    for _ in range(3):
        nc = _bacc.Bacc("TRN2", target_bir_lowering=False, num_devices=1)
        ins = {n: nc.dram_tensor(n, list(a.shape), mybir.dt.from_np(a.dtype), kind="ExternalInput").ap()
               for n, a in arrays.items()}
        out = nc.dram_tensor("out", [NB * L, D], F32, kind="ExternalOutput").ap()
        program = Program(nc, turn_ends, ins, packed, out, LAYERS)
        program.build()
        turn_ends.update(program.c.steps)
    r = _run(nc, [arrays], core_ids=[0])
    return r.results[0]["out"].reshape(NB, L, D)
```

```python
from contextlib import ExitStack, contextmanager

import numpy as np
import concourse.bass as bass
from concourse import mybir
from concourse.alu_op_type import AluOpType as ALU

ACT = mybir.ActivationFunctionType
AX = mybir.AxisListType
F32, BF16, U32, I32 = mybir.dt.float32, mybir.dt.bfloat16, mybir.dt.uint32, mybir.dt.int32

P = 128
D = 128
NB, L = 16, 256
QT = L // P
NT = NB * QT
HEADS = 16
NG = 4
DI, NS, DTR, CONV = 256, 16, 8, 4
CI = DI // P
E0, H0 = 32, 512
A1 = 64
I1, BLK = 352, 16
E2, H2, CAP = 8, 512, NB * L // 16
E3, SH3, H3 = 8, 2, 64
EPS = 1e-5
NEG = -1e30
PACE = {0: (1, 0), 1: (1, 1), 2: (0, 1)}
SPAN = {"pre2": (0.15, 0.9), "moe3": (0.05, 1)}
LAG_SUM = {1: 5, 2: 7}


class Mark:

    def __init__(self, stream, off, turn):
        self.stream, self.off, self.turn = stream, off, turn


class Stream:

    def __init__(self, core, eng, name, step=1):
        self.core, self.eng, self.name, self.step = core, eng, name, step
        self.sem = core.nc.alloc_semaphore("s_" + name)
        self.base = self.off = 0
        self.waited = {}
        core.streams.append(self)

    def need(self, mark):
        core = self.core
        if mark is None:
            return
        back = 0 if mark.turn == core.turn else 1
        if back and core.loop_name is None:
            return
        if self.waited.get(mark.stream.name, (-1, 0)) >= (-back, mark.off):
            return
        self.waited[mark.stream.name] = (-back, mark.off)
        self.eng.wait_ge(mark.stream.sem, core.value(mark.stream, mark.off, back))

    def needs(self, marks):
        for m in marks:
            if isinstance(m, (list, tuple)):
                self.needs(m)
            else:
                self.need(m)

    def do(self, issue, *marks):
        self.needs(marks)
        issue(self.eng).then_inc(self.sem, self.step)
        self.off += self.step
        return Mark(self, self.off, self.core.turn)

    def quiet(self, issue, *marks):
        self.needs(marks)
        issue(self.eng)

    def last(self):
        return Mark(self, self.off, self.core.turn) if self.off else None


class Slot:

    def __init__(self, core, name, tensor):
        self.core, self.name, self.t, self.back, self.full = core, name, tensor, None, None
        core.slots.append(self)

    def __getitem__(self, key):
        return self.t[key]

    def handed_back(self):
        if self.back is not None:
            return self.back
        return [Mark(self.core.by_name[s], off, "before")
                for s, off in self.core.turn_ends.get((self.core.loop_name, self.name), [])]

    def hand_back(self, *marks):
        self.back = [m for m in marks if m is not None]

    def fill(self, *marks):
        self.full = [m for m in marks if m is not None]

    def filled(self):
        if self.full is not None:
            return self.full
        return [Mark(self.core.by_name[s], off, "before")
                for s, off in self.core.turn_ends.get((self.core.loop_name, self.name, "full"), [])]


class Core:
    def __init__(self, nc, turn_ends):
        self.nc, self.turn_ends = nc, turn_ends
        self.steps, self.ahead = {}, []
        self.streams, self.slots, self.loop_name, self.i, self.turn = [], [], None, None, 0
        self.pe = Stream(self, nc.tensor, "pe")
        self.ve = Stream(self, nc.vector, "ve")
        self.ac = Stream(self, nc.scalar, "ac")
        self.po = Stream(self, nc.gpsimd, "po")
        self.by_name = {s.name: s for s in self.streams}

    def dma_stream(self, eng, name):
        s = Stream(self, eng, name, 16)
        self.by_name[name] = s
        return s

    def value(self, stream, off, back):
        if self.loop_name is None:
            return stream.base + off
        per = self.turn_ends.get((self.loop_name, "per", stream.name), 0)
        return stream.base + per * (1 - back) + off + self.i * per

    def join(self):
        for eng in (self.nc.tensor, self.nc.vector, self.nc.scalar, self.nc.gpsimd, self.nc.sync):
            for s in self.streams:
                if s.base + s.off:
                    eng.wait_ge(s.sem, s.base + s.off)
        self.fresh()

    def fresh(self):
        self.turn += 1
        for s in self.streams:
            s.base, s.off, s.waited = s.base + s.off, 0, {}
        for b in self.slots:
            b.back = b.full = None

    def loop(self, name, n, body, tables="natural_log_exp_and_others"):
        self.join()
        for issue in self.ahead:
            issue()
        self.ahead = []
        self.fresh()
        pers = {s.name: self.turn_ends.get((name, "per", s.name), 0) for s in self.streams}
        for s in self.streams:
            if pers[s.name]:
                self.nc.sync.nop().then_inc(s.sem, pers[s.name])
        self.loop_name = name
        self.nc.scalar.preload_act_table_set(tables)
        with self.nc.Fori(0, n) as i:
            self.i = i
            body(i)
        self.loop_name = None
        for b in self.slots:
            if b.back is not None:
                self.turn_ends[(name, b.name)] = [(m.stream.name, m.off) for m in b.back]
            if b.full is not None:
                self.turn_ends[(name, b.name, "full")] = [(m.stream.name, m.off) for m in b.full]
        for s in self.streams:
            self.turn_ends[(name, "per", s.name)] = s.off
            s.base, s.off = s.base + s.off * n + pers[s.name], 0
        self.fresh()
        self.join()


def bcast(ap, n, axis):
    ap = ap.unsqueeze(axis)
    shape = list(ap.shape)
    shape[axis] = n
    return ap.broadcast_to(tuple(shape))


def drain(gen):
    while True:
        try:
            next(gen)
        except StopIteration as end:
            return end.value


class Program:
    divide_on_pool = (0, 1, 2)

    def __init__(self, nc, turn_ends, ins, packed, out, debug):
        self.nc, self.ins, self.packed, self.out, self.debug = nc, ins, packed, out, debug
        c = self.c = Core(nc, turn_ends)
        self.pe, self.ve, self.ac, self.po = c.pe, c.ve, c.ac, c.po
        self.load = c.dma_stream(nc.sync, "load")
        self.stack, self.taken = ExitStack(), 0
        self.X = self.sb("X", [P, NT, D])
        self.bank = [Slot(c, f"bank{i}", nc.alloc_psum_tensor(f"bank{i}", [P, 512], F32)) for i in range(8)]
        self.pack = {}
        self.w = {}

    def weave(self, *gens):
        live = [[SPAN.get(name, (0, 1))[0], name, 0, g] for g, name in gens if g is not None]
        while live:
            x = min(live, key=lambda v: v[0])
            try:
                x[2] += next(x[3]) or 1
                start, end = SPAN.get(x[1], (0, 1))
                x[0] = start + (end - start) * x[2] / self.c.turn_ends.get(("steps", x[1]), 1)
            except StopIteration:
                self.c.steps[("steps", x[1])] = x[2] + 1
                live.remove(x)

    @contextmanager
    def scope(self):
        outer, self.stack = self.stack, ExitStack()
        with self.stack:
            yield
            self.c.join()
        self.stack = outer

    def sb(self, name, shape, dt=F32):
        self.taken += 1
        return self.stack.enter_context(self.nc.sbuf_tensor(f"{name}_{self.taken}", shape, dt))

    def slot(self, name, shape, dt=F32):
        return Slot(self.c, name, self.sb(name, shape, dt))

    def load_all(self):
        ld = self.load
        ld.do(lambda e: e.dma_start(self.X[:, :, :], self.ins["x"].rearrange("(t p) d -> p t d", p=P)))
        self.dummy = self.sb("dummy", [P, 4])
        self.dummy_ve, self.dummy_po = Slot(self.c, "dummy_ve", None), Slot(self.c, "dummy_po", None)
        self.ve.do(lambda e: e.memset(self.dummy[:, :], 0.0))
        self.load_packs("wf")
        w, ve = self.w, self.ve
        small = {n: self.sb(n, [P, k], BF16) for n, k in (("identb", P), ("mask", 4 * P), ("upto", P), ("onesb", P))}
        sel = self.sb("selb", [96, 2 * NS, P], BF16)
        with self.scope():
            self.load_packs("wb")
            for n, t in small.items():
                ve.do(lambda e: e.tensor_copy(t[:, :], w[n]))
                w[n] = t[:, :]
            ve.do(lambda e: e.tensor_copy(sel[:, :, :], bcast(w["sel"], P, 2)))
            w["sel"] = sel[:, :, :]

    def reserve(self, pname):
        width, parts = self.packed[pname]
        t = self.sb("pack_" + pname, [P, width])
        for name, (o, rows, shape) in parts.items():
            n = int(np.prod(shape))
            ap = t[0:rows, o:o + n]
            if len(shape) == 2:
                ap = ap.rearrange("p (a b) -> p a b", a=shape[0])
            if len(shape) == 3:
                ap = ap.rearrange("p (a b c) -> p a b c", a=shape[0], b=shape[1])
            self.w[name] = ap
        return lambda: self.load.do(lambda e: e.dma_start(t[:, :], self.ins[pname]))

    def load_packs(self, *names):
        for pname in names:
            self.reserve(pname)()
        self.c.join()

    def gate(self, *marks):
        self.dummy_ve.hand_back(self.ve.do(lambda e: e.tensor_copy(self.dummy[:, 0:1], self.dummy[:, 1:2]),
                                      self.dummy_ve.handed_back(), *marks))

    def gate_po(self, *marks):
        self.dummy_po.hand_back(self.po.do(lambda e: e.tensor_tensor(self.dummy[:, 2:3], self.dummy[:, 3:4],
                                                                self.dummy[:, 3:4], ALU.add), self.dummy_po.handed_back(), *marks))

    def alloc_common(self, layer):
        two = range(2)
        self.xs = self.slot("xs", [P, QT, D])
        self.xn = [self.slot(f"xn{i}", [P, QT, D]) for i in two]
        self.xnT = [self.slot(f"xnT{i}", [P, L]) for i in two]
        self.ln = [[self.slot(f"{n}{i}", [P] + sh) for n, sh in (("stats", [QT, 6]), ("mv", [QT, 2]), ("lnv", [QT]), ("rstd", [QT]))]
                   for i in two]
        self.Xw = Slot(self.c, f"Xw{layer}", None)
        if layer == 3:
            return
        g, hd = (8, A1) if layer == 1 else (4, 8)
        self.qT = [self.slot(f"qT{i}", [P, g, L]) for i in two]
        self.kT = [self.slot(f"kT{i}", [P, 1 if layer == 0 else g, L]) for i in two]
        vh, vc = (1, 32) if layer == 0 else (HEADS, max(hd, 32))
        self.v = [self.slot(f"v{i}", [P, QT, vh, vc]) for i in two]
        if vc > hd:
            for v in self.v:
                self.ve.do(lambda e: e.memset(v[:, :, :, hd:], 0.0))
        self.mx = [self.slot(f"mx{i}", [P, 4]) for i in two]
        self.nb = [self.slot(f"nb{i}", [P, 4]) for i in two]
        self.pr = [self.slot(f"pr{i}", [P, 512]) for i in range(3)]
        self.prT = [self.slot(f"prT{i}", [P, 512]) for i in range(2)]
        self.sums = [self.slot(f"sums{i}", [P, 4]) for i in range(3)]
        self.rsum = [self.slot(f"rsum{i}", [P, 4]) for i in range(3)]
        self.oT = [self.slot(f"oT{i}", [P, g, P]) for i in range(QT)]
        self.x1 = self.slot("x1", [P, QT, D])

    def normalise(self, src, dst, ready, which):
        ve, ac = self.ve, self.ac
        stats, mv, lnv, rstd = self.ln[which]
        for q in range(QT):
            t1 = ve.do(lambda e: e.bn_stats(stats[:, q, :], src[:, q, :]), ready)
        yield None
        self.gate(t1, mv.handed_back())
        for q in range(QT):
            t2 = ve.do(lambda e: e.bn_aggr(mv[:, q, :], stats[:, q, :]))
        t3 = ac.do(lambda e: e.activation(lnv[:, :], mv[:, :, 1], ACT.Ln, bias=self.w["eps"], scale=1.0), t2)
        t4 = ac.do(lambda e: e.activation(rstd[:, :], lnv[:, :], ACT.Exp, scale=-0.5), t3, rstd.handed_back())
        yield None
        for q in range(QT):
            t5 = ve.do(lambda e: e.tensor_scalar(dst[:, q, :], src[:, q, :], mv[:, q, 0:1], rstd[:, q:q + 1],
                                                 ALU.subtract, ALU.mult), t4, dst.handed_back() if dst is not src else None)
        mv.hand_back(t3, t5)
        rstd.hand_back(t5)
        yield t5

    def layer_norm(self, b, k, bk, ready=None):
        ve, ac, pe = self.ve, self.ac, self.pe
        xn, xnT = self.xn[k], self.xnT[k]
        self.gate(self.xs.handed_back(), ready, self.Xw.filled())
        t = ve.do(lambda e: e.tensor_copy(self.xs[:, :, :], self.X[:, bass.ds(b * QT, QT), :]))
        for t5 in self.normalise(self.xs, xn, t, 0):
            if t5 is None:
                yield
        self.xs.hand_back(t5)
        xn.fill(t5)
        yield
        for q in range(QT):
            t6 = pe.do(lambda e: e.transpose(bk[:, q * P:(q + 1) * P], xn[:, q, :], self.w["ident"]), t5, bk.handed_back())
        yield
        t7 = ac.do(lambda e: e.activation(xnT[:, :], bk[:, 0:L], ACT.Copy), t6, xnT.handed_back())
        bk.hand_back(t7)
        xnT.fill(t7)
        xn.hand_back(t6)
        yield

    def qkv(self, layer, k, bk):
        ve, ac, pe, w = self.ve, self.ac, self.pe, self.w
        hd = A1 if layer == 1 else 8
        groups = 8 if layer == 1 else 4
        kg = 1 if layer == 0 else groups
        xnT, v = self.xnT[k], self.v[k]
        nv = 8 if layer == 0 else HEADS * hd
        ta = tv = None
        turn = 0
        for dst, wt, bias, n in ((self.qT[k], w[f"wq{layer}"], w[f"bq{layer}"], groups),
                                 (self.kT[k], w[f"wk{layer}"], w[f"bk{layer}"], kg)):
            for g0 in range(0, n, 2):
                gs = range(g0, min(g0 + 2, n))
                for g in gs:
                    t = pe.do(lambda e: e.matmul(bk[:, (g - g0) * L:(g - g0 + 1) * L], wt[:, g, :], xnT[:, :], start=True,
                                                 stop=True), xnT.filled(), bk.handed_back() if g == g0 else None)
                yield
                for g in gs:
                    src = bk[:, (g - g0) * L:(g - g0 + 1) * L]
                    if turn % 2 == 0:
                        te = ta = ac.do(lambda e: e.activation(dst[:, g, :], src, ACT.Identity, bias=bias[:, g:g + 1]),
                                        t, dst.handed_back())
                    else:
                        te = tv = ve.do(lambda e: e.tensor_scalar(dst[:, g, :], src, bias[:, g:g + 1], None, ALU.add),
                                        t, dst.handed_back())
                bk.hand_back(te)
                turn += 1
                yield
        for q in range(QT):
            for c0 in range(0, nv, 512):
                cn = min(512, nv - c0)
                t = pe.do(lambda e: e.matmul(bk[:, 0:cn], xnT[:, q * P:(q + 1) * P], w[f"wv{layer}"][:, c0:c0 + cn],
                                             start=True, stop=True), bk.handed_back())
                yield
                vo = v[:, q, c0 // hd:(c0 + cn) // hd, 0:hd]
                tv = ve.do(lambda e: e.tensor_tensor(vo, bk[:, 0:cn].rearrange("p (h d) -> p h d", d=hd),
                                                     w[f"bv{layer}"][:, c0:c0 + cn].rearrange("p (h d) -> p h d", d=hd),
                                                     ALU.add), t, v.handed_back())
                bk.hand_back(tv)
                yield
        for dst in (self.qT[k], self.kT[k], v):
            dst.fill(ta, tv)
        xnT.hand_back(t)

    def attention(self, layer, k, sc, tr, vb):
        ve, ac, pe, w = self.ve, self.ac, self.pe, self.w
        hd = A1 if layer == 1 else 8
        scale = float(hd) ** -0.5
        groups, rows = (8, 64) if layer == 1 else (4, 32)
        per = P // rows
        qT, kT, v = self.qT[k], self.kT[k], self.v[k]
        tin = qT.filled() + v.filled()
        half = 8 if hd == A1 else HEADS
        order = sorted(range(HEADS), key=lambda h: (h // half, h % per, h))
        units = [(0, order[4 * u:4 * u + 4]) for u in range(4)] + [(1, order[2 * u:2 * u + 2]) for u in range(8)]
        t_sc, t_mx, t_exp, t_pn, t_tp, t_pT, t_pv = {}, {}, {}, {}, {}, {}, {}

        def scores(u):
            q, heads = units[u]
            bk = sc[u % 2]
            wid, nh = P * (q + 1), len(heads)
            for n, h in enumerate(heads):
                r = rows * (h % per)
                kk = 0 if layer == 0 else h // per
                pe.quiet(lambda e: e.matmul(bk[:, n * wid:(n + 1) * wid], qT[r:r + hd, h // per, q * P:(q + 1) * P],
                                            kT[r:r + hd, kk, 0:wid], start=n == 0, stop=True, skip_group_check=True),
                         bk.handed_back() if n == 0 else None, tin)
            last = bk[:, :].rearrange("p (n k) -> p n k", n=nh)[:, :, q * P:]
            t_sc[u] = pe.do(lambda e: e.matmul(last, w["identb"], w["mask"][:, 0:nh * P], start=False, stop=True,
                                               skip_group_check=True))

        y1, y3 = PACE[layer]

        def maxima(u):
            q, heads = units[u]
            bk, nh = sc[u % 2], len(heads)
            mx, nb = self.mx[u % 2], self.nb[u % 2]
            v3 = bk[:, :].rearrange("p (h k) -> p h k", h=nh)
            t = ve.do(lambda e: e.tensor_reduce(mx[:, 0:nh], v3, AX.X, ALU.max), t_sc[u])
            t = ve.do(lambda e: e.tensor_scalar(nb[:, 0:nh], mx[:, 0:nh], -scale, None, ALU.mult), t, nb.handed_back())
            t_mx[u] = t

        def exponentials(u):
            q, heads = units[u]
            bk, wid = sc[u % 2], P * (q + 1)
            nb, pr, sm = self.nb[u % 2], self.pr[u % 3], self.sums[u % 3]
            for n, h in enumerate(heads):
                te = ac.do(lambda e: e.activation(pr[:, n * wid:(n + 1) * wid], bk[:, n * wid:(n + 1) * wid], ACT.Exp,
                                                  bias=nb[:, n:n + 1], scale=scale, accum_out=sm[:, n:n + 1]),
                           t_mx[u], pr.handed_back(), sm.handed_back())
            nb.hand_back(te)
            bk.hand_back(te)
            t_exp[u] = te

        def divide(u):
            q, heads = units[u]
            nh = len(heads)
            pr, sm, rs = self.pr[u % 3], self.sums[u % 3], self.rsum[u % 3]
            t = ve.do(lambda e: e.reciprocal(rs[:, 0:nh], sm[:, 0:nh]), t_exp[u], rs.handed_back())
            sm.hand_back(t)
            if layer in self.divide_on_pool:
                p3 = pr[:, :].rearrange("p (h k) -> p h k", h=nh)
                t = self.po.do(lambda e: e.tensor_tensor(p3, p3, bcast(rs[:, 0:nh], P * (q + 1), 2), ALU.mult), t)
            else:
                t_rs = t
                for n in range(nh):
                    ph = pr[:, n * P * (q + 1):(n + 1) * P * (q + 1)]
                    t = ve.do(lambda e: e.tensor_scalar(ph, ph, rs[:, n:n + 1], None, ALU.mult), t_rs)
            rs.hand_back(t)
            t_pn[u] = t

        def turn_p(u):
            bk, pr = tr[u % len(tr)], self.pr[u % 3]
            for j in range(3):
                pe.quiet(lambda e: e.transpose(bk[:, j * P:(j + 1) * P], pr[:, j * P:(j + 1) * P], w["ident"]),
                         bk.handed_back(), t_pn[u])
            t = pe.do(lambda e: e.transpose(bk[:, 3 * P:], pr[:, 3 * P:], w["ident"]))
            pr.hand_back(t)
            t_tp[u] = t

        def take_p(u):
            bk, prT, t = tr[u % len(tr)], self.prT[u % 2], t_tp[u]
            if self.evac_act(layer, u):
                t = ac.do(lambda e: e.activation(prT[:, :], bk[:, :], ACT.Copy), t, prT.handed_back())
            else:
                t = ve.do(lambda e: e.tensor_copy(prT[:, :], bk[:, :]), t, prT.handed_back())
            bk.hand_back(t)
            t_pT[u] = t

        def values(u):
            q, heads = units[u]
            prT = self.prT[u % 2]
            for n, h in enumerate(heads):
                r, gr = rows * (h % per), h // per % 4
                vh = 0 if layer == 0 else h
                for kb in range(q + 1):
                    blk = n * (q + 1) + kb
                    f = lambda e: e.matmul(vb[r:r + rows, gr * P:(gr + 1) * P], v[:, kb, vh, :],
                                           prT[:, blk * P:(blk + 1) * P], start=kb == 0, stop=kb == q,
                                           tile_position=(0, r))
                    if kb == q and n == len(heads) - 1:
                        t_pv[u] = pe.do(f, t_pT[u], vb.handed_back())
                    else:
                        pe.quiet(f, t_pT[u], vb.handed_back())
            prT.hand_back(t_pv[u])

        def take_o(q, first, u):
            oT = self.oT[q]
            g0 = first // half * 4
            t = ac.do(lambda e: e.activation(oT[:, g0:g0 + 4, :].rearrange("p c t -> p (c t)"), vb[:, :], ACT.Copy),
                      t_pv[u], oT.handed_back())
            vb.hand_back(t)
            return t

        t_o = {}
        n_u = len(units)
        full = {}
        seen = 0
        for u, (q, heads) in enumerate(units):
            seen += len(heads)
            if seen % half == 0:
                full[u] = (q, (seen - half) % HEADS)
        scores(0)
        yield
        for u in range(n_u + 3):
            if u + 1 < n_u:
                scores(u + 1)
            if u < n_u:
                maxima(u)
            if y1:
                yield y1
            if 1 <= u <= n_u:
                divide(u - 1)
            if u < n_u:
                exponentials(u)
            yield
            if 2 <= u <= n_u + 1:
                turn_p(u - 2)
            if u >= 3:
                values(u - 3)
            if y3:
                yield y3
            if 2 <= u <= n_u + 1:
                take_p(u - 2)
            if u >= 3:
                if u - 3 in full:
                    q, first = full[u - 3]
                    t_o[q] = take_o(q, first, u - 3)
            yield
        qT.hand_back(t_sc[n_u - 1])
        kT.hand_back(t_sc[n_u - 1])
        v.hand_back(t_pv[n_u - 1])
        nch = groups
        bk = tr[-1]
        for q in range(QT):
            for ch in range(nch):
                f = lambda e: e.matmul(bk[:, q * P:(q + 1) * P], self.oT[q][:, ch, :], w[f"wo{layer}"][:, ch, :],
                                       start=ch == 0, stop=ch == nch - 1)
                t = pe.do(f, t_o[q], bk.handed_back() if q == 0 and ch == 0 else None)
            self.oT[q].hand_back(t)
        yield 2
        t1 = ve.do(lambda e: e.tensor_tensor(self.x1[:, :, :], bk[:, 0:L].rearrange("p (q d) -> p q d", q=QT),
                                             bcast(w[f"bo{layer}"], QT, 1), ALU.add), t, self.x1.handed_back())
        bk.hand_back(t1)
        self.t_x1 = t1
        yield

    def sigmoid_times(self, out, z, tmp, ready, free):
        t = self.ac.do(lambda e: e.activation(tmp, z, ACT.Exp, scale=-1.0), ready)
        yield
        t = self.ve.do(lambda e: e.tensor_scalar(tmp, tmp, 1e19, None, ALU.min), t)
        yield
        t = self.ac.do(lambda e: e.activation(tmp, tmp, ACT.Ln, bias=1.0), t)
        t = self.ac.do(lambda e: e.activation(tmp, tmp, ACT.Exp, scale=-1.0), t)
        yield
        return self.ve.do(lambda e: e.tensor_tensor(out, z, tmp, ALU.mult), t, free)

    def evac_act(self, layer, u):
        return layer == 1 or u % 3 != 0

    def add_to_x(self, b, src, ready):
        xv = self.X[:, bass.ds(b * QT, QT), :]
        t = self.ve.do(lambda e: e.tensor_tensor(xv, xv, src, ALU.add), ready, self.Xw.filled())
        self.Xw.fill(t)
        return t

    def alloc_scan(self, CI):
        self.zin = self.slot("zin", [P, CI, L])
        self.zab = self.slot("zab", [P, CI, L])
        self.zmx = self.slot("zmx", [P, CI, L])
        self.delta = self.slot("delta", [P, CI, L])
        self.dtu = self.slot("dtu", [P, CI, L])
        self.split = self.slot("split", [96, L], BF16)
        self.sx = self.slot("sx", [96, L])
        self.sr = self.slot("sr", [96, L])
        self.sh = self.slot("sh", [96, L], BF16)
        self.dA = [[self.slot(f"dA{i}{j}", [P, NG, L]) for j in range(2)] for i in range(CI)]
        self.h = [[self.slot(f"h{i}{j}", [P, NG, L]) for j in range(2)] for i in range(CI)]
        self.Crep = [self.slot(f"Crep{j}", [P, NG, L]) for j in range(2)]
        for x in self.dA:
            for y in x:
                self.ve.do(lambda e: e.memset(y[:, :, 0:1], 0.0))
        self.yT = self.slot("yT", [P, CI, L])

    def softplus(self, n, ready):
        ve, ac = self.ve, self.ac
        z, a, m, dl = (x[:, 0:n, :] for x in (self.zin, self.zab, self.zmx, self.delta))
        t = ac.do(lambda e: e.activation(a, z, ACT.Abs), ready)
        t = ac.do(lambda e: e.activation(a, a, ACT.Exp, scale=-1.0), t)
        t = ac.do(lambda e: e.activation(a, a, ACT.Ln, bias=1.0), t)
        yield
        t1 = ve.do(lambda e: e.tensor_scalar(m, z, 0.0, None, ALU.max), ready)
        return ve.do(lambda e: e.tensor_tensor(dl, a, m, ALU.add), t, t1, self.delta.handed_back())

    def split3(self, ps, ready):
        ve = self.ve
        t0 = ve.do(lambda e: e.tensor_copy(self.sx[:, :], ps), ready)
        t = ve.do(lambda e: e.tensor_copy(self.sh[:, :], self.sx[:, :]), t0)
        t1 = ve.do(lambda e: e.tensor_copy(self.split[0:32, :], self.sh[0:32, :]), t, self.split.handed_back())
        t = ve.do(lambda e: e.tensor_tensor(self.sr[:, :], self.sx[:, :], self.sh[:, :], ALU.subtract), t)
        t = ve.do(lambda e: e.tensor_copy(self.sh[:, :], self.sr[:, :]), t)
        t1 = ve.do(lambda e: e.tensor_copy(self.split[32:64, :], self.sh[32:64, :]), t)
        yield
        t = ve.do(lambda e: e.tensor_tensor(self.sr[:, :], self.sr[:, :], self.sh[:, :], ALU.subtract), t)
        t = ve.do(lambda e: e.tensor_copy(self.split[64:96, :], self.sr[64:96, :]), t)
        return t0, t

    def scan(self, nch, A, u_ap, t_u, t_delta, t_split, banks, bank_y):
        ve, ac, pe, po, w = self.ve, self.ac, self.pe, self.po, self.w
        t_dtu = ve.do(lambda e: e.tensor_tensor(self.dtu[:, 0:nch, :], self.delta[:, 0:nch, :], u_ap, ALU.mult),
                      t_delta, t_u, self.dtu.handed_back())
        turn = 0
        late = []

        def spread(row, j):
            nonlocal turn
            bk = banks[turn % len(banks)]
            turn += 1
            for m in range(2):
                t = pe.do(lambda e: e.matmul(bk[:, m * L:(m + 1) * L], w["sel"][:, row + 2 * j + m, :], self.split[:, :],
                                             start=True, stop=True), t_split, bk.handed_back() if m == 0 else None)
            return bk, t

        def add_up(g, c, hv, th2):
            for n in range(2):
                tp = pe.do(lambda e: e.matmul(bank_y[:, c * L:(c + 1) * L], w["ident"], hv[:, n, :],
                                              start=g == 0 and n == 0 and c == 0, stop=g == NS // NG - 1 and n == 1,
                                              skip_group_check=True), th2,
                           bank_y.handed_back() if g == 0 and n == 0 and c == 0 else None)
            hv.hand_back(tp)

        flat = lambda x, a=0, b=NG: x[:, a:b, :].rearrange("p n t -> p (n t)")
        for g in range(NS // NG):
            r = g % 2
            Cr = self.Crep[r]
            t_dA, t_in = [None] * nch, [None] * nch
            for c in range(nch):
                for n in range(NG):
                    t_dA[c] = ac.do(lambda e: e.activation(self.dA[c][r][:, n, 1:], self.delta[:, c, 1:], ACT.Exp,
                                                           scale=A[:, c, g * NG + n:g * NG + n + 1]),
                                    t_delta, self.dA[c][r].handed_back() if n == 0 else None)
            for j in range(NG // 2):
                bk, t = spread(g * NG, j)
                for c in range(nch):
                    t_in[c] = ve.do(lambda e: e.tensor_tensor(self.h[c][r][:, 2 * j:2 * j + 2, :], bcast(self.dtu[:, c, :], 2, 1),
                                                              bk[:, :].rearrange("p (n t) -> p n t", n=2), ALU.mult),
                                    t, t_dtu, self.h[c][r].handed_back() if j == 0 else None)
                bk.hand_back(t_in[nch - 1])
                yield
            for j in range(NG // 2):
                bk, t = spread(NS + g * NG, j)
                tC = ac.do(lambda e: e.activation(flat(Cr, 2 * j, 2 * j + 2), bk[:, :], ACT.Copy), t,
                           Cr.handed_back() if j == 0 else None)
                bk.hand_back(tC)
                yield
            for f in late:
                f()
            late.clear()
            for c in range(nch):
                hv = self.h[c][r]
                t = ve.do(lambda e: e.tensor_tensor_scan(flat(hv), flat(self.dA[c][r]), flat(hv), 0.0, ALU.mult, ALU.add),
                          t_dA[c], t_in[c])
                self.dA[c][r].hand_back(t)
                th = po.do(lambda e: e.tensor_tensor(hv[:, :, :], hv[:, :, :], Cr[:, :, :], ALU.mult), t, tC)
                th2 = po.do(lambda e: e.tensor_tensor(hv[:, 0:2, :], hv[:, 0:2, :], hv[:, 2:4, :], ALU.add), th)
                late.append(lambda g=g, c=c, hv=hv, th2=th2: add_up(g, c, hv, th2))
                yield
            Cr.hand_back(th)
        yield LAG_SUM[nch]
        for f in late:
            f()
            yield
        tp = pe.last()
        self.delta.hand_back(ac.last(), t_dtu)
        self.dtu.hand_back(t_in[nch - 1])
        self.split.hand_back(pe.last())
        self.t_scan = tp

    def alloc0(self):
        self.x1T = self.slot("x1T", [P, L])
        self.upad = self.sb("upad", [P, CI, CONV - 1 + L])
        self.upadb = Slot(self.c, "upadb", self.upad)
        self.sg = self.slot("sg", [P, CI, L])
        self.sgt = self.slot("sgt", [P, CI, L])
        self.cv = self.slot("cv", [P, CI, L])
        self.cvt = self.slot("cvt", [P, CI, L])
        self.u = self.slot("u", [P, CI, L])
        self.dtT = self.slot("dtT", [DTR, L])
        self.gz = self.slot("gz", [E0, L])
        self.gs = self.slot("gs", [E0, 4])
        self.gp = self.slot("gp", [E0, L])
        self.g8 = self.slot("g8", [E0, 8])
        self.gr = self.slot("gr", [E0, L])
        self.gv = self.slot("gv", [P, L])
        self.gvT = self.slot("gvT", [P, QT, E0])

    def gate0(self, b, k, bk):
        ve, ac, pe, w = self.ve, self.ac, self.pe, self.w
        xn, xnT = self.xn[k], self.xnT[k]
        t = pe.do(lambda e: e.matmul(bk[0:E0, 0:L], w["gate_w"], xnT[:, :], start=True, stop=True), xnT.filled(), bk.handed_back())
        yield
        t = ve.do(lambda e: e.tensor_scalar(self.gz[:, :], bk[0:E0, 0:L], w["gate_b"], None, ALU.add), t)
        bk.hand_back(t)
        yield
        t = ve.do(lambda e: e.tensor_reduce(self.gs[:, 0:1], self.gz[:, :], AX.X, ALU.max), t)
        t = ve.do(lambda e: e.tensor_scalar(self.gs[:, 1:2], self.gs[:, 0:1], -1.0, None, ALU.mult), t)
        yield
        t = ac.do(lambda e: e.activation(self.gp[:, :], self.gz[:, :], ACT.Exp, bias=self.gs[:, 1:2],
                                         accum_out=self.gs[:, 2:3]), t)
        yield
        t = ve.do(lambda e: e.reciprocal(self.gs[:, 3:4], self.gs[:, 2:3]), t)
        t = ve.do(lambda e: e.tensor_scalar(self.gp[:, :], self.gp[:, :], self.gs[:, 3:4], None, ALU.mult), t)
        self.gate(t)
        t = ve.do(lambda e: e.max(self.g8[:, :], self.gp[:, :]))
        self.gate(t)
        t = ve.do(lambda e: e.match_replace(self.gr[:, :], self.g8[:, :], self.gp[:, :], 0.0))
        yield
        t = ve.do(lambda e: e.tensor_tensor(self.gv[0:E0, :], self.gp[:, :], self.gr[:, :], ALU.subtract), t, self.gv.handed_back())
        ve.do(lambda e: e.tensor_copy(self.PT[:, bass.ds(b, 1), :].rearrange("p a t -> p (a t)"), self.gv[0:E0, :]), t)
        yield
        for q in range(QT):
            t1 = pe.do(lambda e: e.transpose(bk[:, q * P:(q + 1) * P], self.gv[:, q * P:(q + 1) * P], w["ident"]),
                       t, bk.handed_back())
        self.gv.hand_back(t1)
        yield
        t1 = ve.do(lambda e: e.tensor_copy(self.gvT[:, :, :], bk[:, 0:L].rearrange("p (q e) -> p q e", q=QT)[:, :, 0:E0]), t1,
                   self.gvT.handed_back())
        bk.hand_back(t1)
        for q in range(QT):
            t2 = pe.do(lambda e: e.matmul(bk[:, 256:256 + E0], xn[:, q, :], self.gvT[:, q, :], start=q == 0,
                                          stop=q == QT - 1), t1)
        self.gvT.hand_back(t2)
        xn.hand_back(t2)
        yield
        t2 = ve.do(lambda e: e.tensor_copy(self.merged[:, :, bass.ds(b, 1)],
                                           bk[:, 256:256 + E0].rearrange("p (e o) -> p e o", o=1)), t2)
        bk.hand_back(t2)

    def mamba(self, b):
        ve, ac, pe, w = self.ve, self.ac, self.pe, self.w
        B5, B6, B7 = self.bank[5], self.bank[6], self.bank[7]
        yield
        t = self.x1T.filled()
        t_in = []
        for part, bk in ((0, B5), (1, B6)):
            for c in range(CI):
                tp = pe.do(lambda e: e.matmul(bk[:, c * L:(c + 1) * L], w["w_in"][:, part * CI + c, :], self.x1T[:, :],
                                              start=True, stop=True), t, bk.handed_back() if c == 0 else None)
            t_in.append(tp)
        self.x1T.hand_back(tp)
        yield 2
        t0 = ac.do(lambda e: e.activation(self.upad[:, :, CONV - 1:], B5[:, :].rearrange("p (c t) -> p c t", c=CI),
                                          ACT.Copy), t_in[0], self.upadb.handed_back())
        B5.hand_back(t0)
        z = B6[:, :].rearrange("p (c t) -> p c t", c=CI)
        tg = yield from self.sigmoid_times(self.sg[:, :, :], z, self.sgt[:, :, :], t_in[1], self.sg.handed_back())
        B6.hand_back(tg)
        yield
        for c in range(CI):
            t = ve.do(lambda e: e.tensor_scalar(self.cv[:, c, :], self.upad[:, c, 0:L], w["conv_w"][:, c, 0:1],
                                                w["conv_b"][:, c:c + 1], ALU.mult, ALU.add), t0)
            for j in range(1, CONV):
                t = ve.do(lambda e: e.scalar_tensor_tensor(self.cv[:, c, :], self.upad[:, c, j:j + L],
                                                           w["conv_w"][:, c, j:j + 1], self.cv[:, c, :], ALU.mult,
                                                           ALU.add), t)
            yield
        self.upadb.hand_back(t)
        tu = yield from self.sigmoid_times(self.u[:, :, :], self.cv[:, :, :], self.cvt[:, :, :], t, self.u.handed_back())
        yield
        for c in range(CI):
            t = pe.do(lambda e: e.matmul(B5[0:96, 0:L], w["w_bc"][:, c, :], self.u[:, c, :], start=c == 0,
                                         stop=c == CI - 1), tu, B5.handed_back())
        for c in range(CI):
            t = pe.do(lambda e: e.matmul(B6[0:DTR, 0:L], w["w_dtin"][:, c, :], self.u[:, c, :], start=c == 0,
                                         stop=c == CI - 1), B6.handed_back())
        yield
        td = ve.do(lambda e: e.tensor_copy(self.dtT[:, :], B6[0:DTR, 0:L]), t)
        B6.hand_back(td)
        t0, t_split = yield from self.split3(B5[0:96, 0:L], t)
        B5.hand_back(t0)
        for c in range(CI):
            t = pe.do(lambda e: e.matmul(B6[:, c * L:(c + 1) * L], w["w_dt"][:, c * P:(c + 1) * P], self.dtT[:, :],
                                         start=True, stop=True), td, B6.handed_back() if c == 0 else None)
        yield
        for c in range(CI):
            tz = ve.do(lambda e: e.tensor_scalar(self.zin[:, c, :], B6[:, c * L:(c + 1) * L], w["b_dt"][:, c:c + 1],
                                                 None, ALU.add), t)
        B6.hand_back(tz)
        t_delta = yield from self.softplus(CI, tz)
        yield
        yield from self.scan(CI, self.A0, self.u[:, :, :], tu, t_delta, t_split, (B5, B6), B7)
        for c in range(CI):
            t = ve.do(lambda e: e.scalar_tensor_tensor(self.yT[:, c, :], self.u[:, c, :], w["Dp"][:, c:c + 1],
                                                       B7[:, c * L:(c + 1) * L], ALU.mult, ALU.add),
                      self.t_scan, self.yT.handed_back())
        B7.hand_back(t)
        self.u.hand_back(t)
        yield
        t = ve.do(lambda e: e.tensor_tensor(self.yT[:, :, :], self.yT[:, :, :], self.sg[:, :, :], ALU.mult), t, tg)
        for q in range(QT):
            for c in range(CI):
                tp = pe.do(lambda e: e.matmul(B5[:, q * P:(q + 1) * P], self.yT[:, c, q * P:(q + 1) * P],
                                              w["w_out"][:, c, :], start=c == 0, stop=c == CI - 1), t,
                           B5.handed_back() if q == 0 and c == 0 else None)
        self.yT.hand_back(tp)
        yield
        t = self.add_to_x(b, B5[:, 0:L].rearrange("p (q d) -> p q d", q=QT), tp)
        B5.hand_back(t)

    def neg_exp(self, name, src, n):
        t = self.sb(name, [P, n, NS])
        m = self.ac.do(lambda e: e.activation(t[:, :, :], src, ACT.Exp))
        self.ve.do(lambda e: e.tensor_scalar(t[:, :, :], t[:, :, :], -1.0, None, ALU.mult), m)
        return t

    def layer0(self):
        ve = self.ve
        self.A0 = self.neg_exp("A0", self.w["A_log0"], CI)
        ve.do(lambda e: e.memset(self.upad[:, :, 0:CONV - 1], 0.0))
        ve.do(lambda e: e.memset(self.gv[:, :], 0.0))

        B = self.bank

        def pre(b, k):
            yield from self.layer_norm(b, k, B[4])
            yield from self.gate0(b, k, B[4])
            yield from self.qkv(0, k, B[4])

        def attend(b, k):
            yield from self.attention(0, k, B[0:2], B[2:3], B[3])
            t = ve.do(lambda e: e.tensor_tensor(self.x1[:, :, :], self.x1[:, :, :], self.xn[k][:, :, :], ALU.add), self.t_x1)
            self.xn[k].hand_back(t)
            tx = self.add_to_x(b, self.x1[:, :, :], t)
            bk = B[2]
            yield
            for q in range(QT):
                tp = self.pe.do(lambda e: e.transpose(bk[:, q * P:(q + 1) * P], self.x1[:, q, :], self.w["ident"]), t, bk.handed_back())
            self.x1.hand_back(tx, tp)
            yield
            t = ve.do(lambda e: e.tensor_copy(self.x1T[:, :], bk[:, 0:L]), tp, self.x1T.handed_back())
            bk.hand_back(t)
            self.x1T.fill(t)

        def step(b, k, last=False, mamba=True):
            self.weave((attend(b, k), "attend0"), (self.mamba(b - 1) if mamba else None, "mamba0"), (None if last else pre(b + 1, 1 - k), "pre0"))

        def body(i):
            step(2 * i + 1, 1)
            step(2 * i + 2, 0)

        drain(pre(0, 0))
        step(0, 0, mamba=False)
        self.c.loop("layer0", NB // 2 - 1, body)
        step(NB - 1, 1, last=True)
        drain(self.mamba(NB - 1))

    def experts0(self):
        ve, ac, pe, w, nc = self.ve, self.ac, self.pe, self.w, self.nc
        R = 8
        w1r = [self.slot(f"w1r{i}", [P, H0]) for i in range(R)]
        w2r = [self.slot(f"w2r{i}", [P, H0 // P, D]) for i in range(R)]
        hz = [self.slot(f"hz{i}", [P, H0 // P, NB]) for i in range(2)]
        hg = [self.slot(f"hg{i}", [P, H0 // P, NB]) for i in range(2)]
        lds = [(self.c.dma_stream(nc.sync, f"e0a{i}"), self.c.dma_stream(nc.sync, f"e0b{i}")) for i in range(R)]
        w1d = self.ins["m_w1"]
        w2d = self.ins["m_w2"]
        J = H0 // P

        def body(i):
            ld = []
            for s in range(R):
                ex = i * R + s
                la = lds[s][0].do(lambda e: e.dma_start(w1r[s][:, :], w1d[bass.ds(ex, 1), 0:D, :].rearrange("a p h -> (a p) h")), w1r[s].handed_back())
                lb = lds[s][1].do(lambda e: e.dma_start(w2r[s][:, :, :], w2d[bass.ds(ex, 1), 0:H0, :].rearrange("a (j p) d -> p (a j) d", p=P)), w2r[s].handed_back())
                ld.append((la, lb))
            def hidden(s):
                ex = i * R + s
                bk = self.bank[s % 2]
                for j in range(J):
                    t = pe.do(lambda e: e.matmul(bk[:, j * NB:(j + 1) * NB], w1r[s][:, j * P:(j + 1) * P],
                                                 self.merged[:, bass.ds(ex, 1), :].rearrange("p a b -> p (a b)"), start=True, stop=True),
                              ld[s][0], bk.handed_back())
                w1r[s].hand_back(t)
                b1v = w["m_b1"][:, bass.ds(ex, 1), :].rearrange("p a j -> p (a j)")
                t = ve.do(lambda e: e.tensor_tensor(hz[s % 2][:, :, :], bk[:, 0:J * NB].rearrange("p (j b) -> p j b", j=J),
                                                    bcast(b1v, NB, 2), ALU.add), t, hz[s % 2].handed_back())
                bk.hand_back(t)
                t = ac.do(lambda e: e.activation(hg[s % 2][:, :, :], hz[s % 2][:, :, :], ACT.Gelu), t, hg[s % 2].handed_back())
                hz[s % 2].hand_back(t)
                return t

            def output(s, t):
                ex = i * R + s
                bo = self.bank[2 + s % 2]
                for j in range(J):
                    t1 = pe.do(lambda e: e.matmul(bo[:, 0:NB], w2r[s][:, j, :], hg[s % 2][:, j, :], start=j == 0,
                                                  stop=j == J - 1), t, ld[s][1], bo.handed_back())
                w2r[s].hand_back(t1)
                hg[s % 2].hand_back(t1)
                b2v = w["m_b2"][:, bass.ds(ex, 1)]
                t = ve.do(lambda e: e.tensor_tensor(self.oall[:, :, bass.ds(ex, 1)], bo[:, 0:NB].rearrange("p (b o) -> p b o", o=1),
                                                    bcast(b2v, NB, 1), ALU.add), t1)
                bo.hand_back(t)

            t_h = hidden(0)
            for s in range(R):
                t_next = hidden(s + 1) if s + 1 < R else None
                output(s, t_h)
                t_h = t_next
        self.c.loop("experts0", E0 // R, body, "gelu_and_others")

    def spread0(self, b, bk):
        ve, pe, w, po = self.ve, self.pe, self.w, self.po
        self.gate(self.ob.handed_back(), self.pts.handed_back())
        t = ve.do(lambda e: e.tensor_copy(self.ob[:, :], self.oall[:, bass.ds(b, 1), :].rearrange("p a e -> p (a e)")))
        tp = ve.do(lambda e: e.tensor_copy(self.pts[:, :], self.PT[:, bass.ds(b, 1), :].rearrange("p a t -> p (a t)")))
        yield
        t = pe.do(lambda e: e.transpose(bk[0:E0, 256:256 + D], self.ob[:, :], w["ident"]), t, bk.handed_back())
        self.ob.hand_back(t)
        yield
        t = ve.do(lambda e: e.tensor_copy(self.oe[:, :], bk[0:E0, 256:256 + D]), t, self.oe.handed_back())
        for q in range(QT):
            t1 = pe.do(lambda e: e.matmul(bk[:, q * P:(q + 1) * P], self.pts[:, q * P:(q + 1) * P], self.oe[:, :],
                                          start=True, stop=True), t, tp)
        yield
        self.oe.hand_back(t1)
        self.pts.hand_back(t1)
        t = self.add_to_x(b, bk[:, 0:L].rearrange("p (q d) -> p q d", q=QT), t1)
        bk.hand_back(t)
        return t

    def fp4(self, name, out, src, nblk, ready, free):
        ve, po = self.ve, self.po
        a, t_, wv_ = (x[:, 0:nblk, :] for x in self.f4)
        am, sc, hs = (x[:, 0:nblk] for x in self.f4s)
        ta = self.ac.do(lambda e: e.activation(a, src, ACT.Abs), ready, ve.last())
        t = ve.do(lambda e: e.tensor_reduce(am, src, AX.X, ALU.max, apply_absolute_value=True), ready)
        t = ve.do(lambda e: e.tensor_scalar(sc, am, float(np.float32(1.0) / np.float32(6.0)), 1e-12, ALU.mult, ALU.max), t)
        th = ve.do(lambda e: e.tensor_scalar(hs, sc, 0.5, None, ALU.mult), t)
        t = ve.do(lambda e: e.reciprocal(am, sc), t)
        yield
        t = ve.do(lambda e: e.tensor_tensor(a, a, bcast(am, BLK, 2), ALU.mult), t, ta)
        yield
        t1 = t = ve.do(lambda e: e.tensor_scalar(wv_, a, 1.75, None, ALU.is_gt), t)
        t = ve.do(lambda e: e.tensor_scalar(t_, a, 5.0, 2.0, ALU.is_gt, ALU.mult), t)
        for m in (3.5, 2.5):
            yield
            t = ve.do(lambda e: e.scalar_tensor_tensor(t_, a, m, t_, ALU.is_gt, ALU.add), t)
        yield
        t = ve.do(lambda e: e.scalar_tensor_tensor(t_, t_, 2.0, wv_, ALU.mult, ALU.add), t, t1)
        for m in (1.25, 0.75, 0.25):
            yield
            t = ve.do(lambda e: e.scalar_tensor_tensor(t_, a, m, t_, ALU.is_gt, ALU.add), t)
        t = ve.do(lambda e: e.tensor_tensor(t_, t_, bcast(hs, BLK, 2), ALU.mult), t)
        return ve.do(lambda e: e.scalar_tensor_tensor(out.bitcast(U32), src.bitcast(U32), 0x80000000, t_.bitcast(U32),
                                                      ALU.bitwise_and, ALU.bitwise_or), t, free)

    def layer1(self):
        ve, ac, pe, w = self.ve, self.ac, self.pe, self.w
        NBH = I1 // BLK
        self.f4 = [self.sb(f"f4{i}", [P, QT * NBH, BLK]) for i in range(3)]
        self.f4s = [self.sb(f"f4s{i}", [P, QT * NBH]) for i in range(3)]
        wqt = self.sb("wgu_q", [P, 6, P])
        wdq = self.sb("wd_q", [P, I1])
        wgT = self.sb("wgT", [P, I1])
        wuT = self.sb("wuT", [P, I1])
        wdT = self.sb("wdT", [P, 3, D])
        xq = self.slot("xq", [P, QT, D])
        xqT = self.slot("xqT", [P, L])
        hh = self.slot("hh", [P, QT, I1])
        he = self.slot("he", [P, I1])
        hq = self.slot("hq", [P, QT, I1])
        hqT = self.slot("hqT", [P, 3, L])
        blk = lambda ap: ap.rearrange("p (n k) -> p n k", k=BLK)
        B6, B7 = self.bank[6], self.bank[7]
        t = ve.last()
        raw = w["wgu1"]
        for i in (0, 3):
            three = lambda x: x[:, i:i + 3, :].rearrange("p a (n k) -> p (a n) k", k=BLK)
            t = drain(self.fp4("w", three(wqt), three(raw), 3 * D // BLK, t, None))
        t = drain(self.fp4("w", blk(wdq[:, :]), blk(w["wd1"]), NBH, t, None))
        for i in range(6):
            dst = wgT if i < 3 else wuT
            rows = min(P, I1 - (i % 3) * P)
            tp = pe.do(lambda e: e.transpose(B6[:, 0:rows], wqt[0:rows, i, :], w["ident"][0:rows, 0:rows]), t, B6.handed_back())
            tc = ve.do(lambda e: e.tensor_copy(dst[:, (i % 3) * P:(i % 3) * P + rows], B6[:, 0:rows]), tp)
            B6.hand_back(tc)
        for i in range(3):
            rows = min(P, I1 - i * P)
            tp = pe.do(lambda e: e.transpose(B6[0:rows, 0:P], wdq[:, i * P:i * P + rows], w["ident"]), t, B6.handed_back())
            tc = ve.do(lambda e: e.tensor_copy(wdT[0:rows, i, :], B6[0:rows, 0:P]), tp)
            B6.hand_back(tc)

        def ffn(b, k):
            xn = self.xn[k]
            t = yield from self.fp4("x", xq[:, :, :].rearrange("p q (n k) -> p (q n) k", k=BLK),
                         xn[:, :, :].rearrange("p q (n k) -> p (q n) k", k=BLK), QT * D // BLK, xn.filled(), xq.handed_back())
            xn.hand_back(t, pe.last())
            for q in range(QT):
                tp = pe.do(lambda e: e.transpose(B7[:, q * P:(q + 1) * P], xq[:, q, :], w["ident"]), t, B7.handed_back())
            xq.hand_back(tp)
            yield
            t = ac.do(lambda e: e.activation(xqT[:, :], B7[:, 0:L], ACT.Copy), tp, xqT.handed_back())
            B7.hand_back(t)
            yield
            for q in range(QT):
                tg = pe.do(lambda e: e.matmul(B6[:, 0:I1], xqT[:, q * P:(q + 1) * P], wgT[:, :], start=True, stop=True), t, B6.handed_back())
                tu = pe.do(lambda e: e.matmul(B7[:, 0:I1], xqT[:, q * P:(q + 1) * P], wuT[:, :], start=True, stop=True), B7.handed_back())
                ts = yield from self.sigmoid_times(hh[:, q, :], B6[:, 0:I1], he[:, :], tg, None)
                B6.hand_back(ts)
                th = ve.do(lambda e: e.tensor_tensor(hh[:, q, :], hh[:, q, :], B7[:, 0:I1], ALU.mult), ts, tu)
                B7.hand_back(th)
                yield
            xqT.hand_back(tu)
            t = yield from self.fp4("h", hq[:, :, :].rearrange("p q (n k) -> p (q n) k", k=BLK),
                         hh[:, :, :].rearrange("p q (n k) -> p (q n) k", k=BLK), QT * NBH, th, hq.handed_back())
            yield
            for ch in range(3):
                rows = min(P, I1 - ch * P)
                bk = B6 if ch % 2 == 0 else B7
                for q in range(QT):
                    tp = pe.do(lambda e: e.transpose(bk[0:rows, q * P:(q + 1) * P], hq[:, q, ch * P:ch * P + rows],
                                                     w["ident"]), t, bk.handed_back())
                yield
                tc = ac.do(lambda e: e.activation(hqT[0:rows, ch, :], bk[0:rows, 0:L], ACT.Copy), tp, hqT.handed_back())
                bk.hand_back(tc)
            hq.hand_back(tp)
            for q in range(QT):
                for ch in range(3):
                    rows = min(P, I1 - ch * P)
                    tp = pe.do(lambda e: e.matmul(B7[:, q * P:(q + 1) * P], hqT[0:rows, ch, q * P:(q + 1) * P],
                                                  wdT[0:rows, ch, :], start=ch == 0, stop=ch == 2), tc, B7.handed_back() if q == 0 and ch == 0 else None)
            hqT.hand_back(tp)
            yield
            t = self.add_to_x(b, B7[:, 0:L].rearrange("p (q d) -> p q d", q=QT), tp)
            B7.hand_back(t)
            yield

        B = self.bank

        def pre(b, k):
            t = (yield from self.spread0(b, B[4])) if 0 in self.debug else None
            yield from self.layer_norm(b, k, B[4], t)
            yield from self.qkv(1, k, B[4])

        def attend(b, k):
            yield from self.attention(1, k, B[0:2], [B[2], B[5]], B[3])
            t = self.add_to_x(b, self.x1[:, :, :], self.t_x1)
            self.x1.hand_back(t)

        def step(b, k, last=False):
            self.weave((attend(b, k), "attend1"), (ffn(b, k), "ffn1"), (None if last else pre(b + 1, 1 - k), "pre1"))

        self.steps("layer1", pre, step)

    def steps(self, name, pre, step):
        def body(i):
            step(2 * i, 0)
            step(2 * i + 1, 1)

        drain(pre(0, 0))
        self.c.loop(name, NB // 2 - 1, body)
        step(NB - 2, 0)
        step(NB - 1, 1, last=True)

    def layer2(self):
        ve, ac, pe, po, w, nc = self.ve, self.ac, self.pe, self.po, self.w, self.nc
        XN = self.sb("XN", [P, NT, D])
        LG = self.sb("LG", [P, NT, E2])
        if 0 in self.debug and 1 not in self.debug:
            self.c.loop("spread0", NB, lambda b: drain(self.spread0(b, self.bank[7])))
        zero = self.sb("zero", [P, 512])
        t = ve.do(lambda e: e.memset(zero[:, :], 0.0))
        rows = nc.dram_tensor("slots", [E2 * CAP + NB * L, D], F32, kind="Internal").ap()
        zr = self.c.dma_stream(nc.sync, "zero_slots")
        ow = [self.c.dma_stream(nc.sync, f"own_rows{k}") for k in range(2)]
        for i in range(4):
            zr.do(lambda e: e.dma_start(rows[i * 512:(i + 1) * 512, :].rearrange("(p r) d -> p (r d)", p=P), zero[:, :]), t)
        own = rows[E2 * CAP:, :].rearrange("(t p) d -> p t d", p=P)

        B = self.bank

        def pre(b, k):
            bk, xn, xnT = B[4], self.xn[k], self.xnT[k]
            yield from self.layer_norm(b, k, bk)
            for q in range(QT):
                t = pe.do(lambda e: e.matmul(bk[:, q * E2:(q + 1) * E2], xnT[:, q * P:(q + 1) * P], w["w_switch"],
                                             start=True, stop=True), xnT.filled(), bk.handed_back())
            t = ve.do(lambda e: e.tensor_tensor(LG[:, bass.ds(b * QT, QT), :], bk[:, 0:QT * E2].rearrange("p (q e) -> p q e", q=QT),
                                                bcast(w["b_switch"], QT, 1), ALU.add), t)
            bk.hand_back(t)
            self.gate_po(xn.filled())
            t = po.do(lambda e: e.tensor_copy(XN[:, bass.ds(b * QT, QT), :], xn[:, :, :]))
            td = ow[k].do(lambda e: e.dma_start(own[:, bass.ds(b * QT, QT), :], xn[:, :, :]), xn.filled())
            xn.hand_back(t, td, pe.last())
            yield from self.qkv(2, k, bk)

        def attend(b, k):
            yield from self.attention(2, k, B[0:2], [B[2], B[5]], B[3])
            t = self.add_to_x(b, self.x1[:, :, :], self.t_x1)
            self.x1.hand_back(t)

        self.steps("layer2", pre, lambda b, k, last=False: self.weave((attend(b, k), "attend2"), (None if last else pre(b + 1, 1 - k), "pre2")))

        prb = self.sb("prb", [P, NT, E2])
        m1 = self.sb("m1", [P, NT])
        pm = self.sb("pm", [P, NT])
        m8 = self.sb("m8", [P, NT, 8])
        i8 = self.sb("i8", [P, NT, 8], U32)
        rt = self.sb("rt", [P, NT])
        oh = self.sb("oh", [P, NT, E2])
        ohb = self.sb("ohb", [P, NT * E2], BF16)
        tot = self.sb("tot", [P, NT, E2])
        off = self.sb("off", [P, NT, E2])
        pos = self.sb("pos", [P, NT])
        keep = self.sb("keep", [P, NT])
        slot = self.sb("slot", [P, NT])
        sloti = self.sb("sloti", [P, NT], I32)
        B0, B1 = self.bank[0], self.bank[1]
        do = lambda f, *n: ve.do(f, ve.last(), *n)
        self.c.join()
        do(lambda e: e.tensor_reduce(m1[:, :], LG[:, :, :], AX.X, ALU.max))
        t = do(lambda e: e.tensor_tensor(prb[:, :, :], LG[:, :, :], bcast(m1[:, :], E2, 2), ALU.subtract))
        t = ac.do(lambda e: e.activation(prb[:, :, :], prb[:, :, :], ACT.Exp), t)
        do(lambda e: e.tensor_reduce(m1[:, :], prb[:, :, :], AX.X, ALU.add), t)
        do(lambda e: e.reciprocal(m1[:, :], m1[:, :]))
        do(lambda e: e.tensor_tensor(prb[:, :, :], prb[:, :, :], bcast(m1[:, :], E2, 2), ALU.mult))
        do(lambda e: e.tensor_reduce(pm[:, :], prb[:, :, :], AX.X, ALU.max))
        do(lambda e: e.reciprocal(m1[:, :], pm[:, :]))
        scl = self.sb("scl", [P, NT])
        do(lambda e: e.tensor_tensor(scl[:, :], pm[:, :], m1[:, :], ALU.mult))
        t = ve.last()
        self.gate(t)
        for i in range(NT):
            t = ve.do(lambda e: e.max(m8[:, i, :], prb[:, i, :]))
        self.gate(t)
        for i in range(NT):
            ve.do(lambda e: e.max_index(i8[:, i, :], m8[:, i, :], prb[:, i, :]))
        do(lambda e: e.tensor_copy(rt[:, :], i8[:, :, 0]))
        t = do(lambda e: e.tensor_tensor(oh[:, :, :], bcast(w["iota8"], NT, 1), bcast(rt[:, :], E2, 2), ALU.is_equal))
        t = do(lambda e: e.tensor_copy(ohb[:, :], oh[:, :, :].rearrange("p t e -> p (t e)")))
        ta = pe.do(lambda e: e.matmul(B0[:, 0:NT * E2], w["upto"], ohb[:, :], start=True, stop=True), t, B0.handed_back())
        tb = pe.do(lambda e: e.matmul(B1[:, 0:NT * E2], w["onesb"], ohb[:, :], start=True, stop=True), B1.handed_back())
        do(lambda e: e.tensor_copy(tot[:, :, :], B1[:, 0:NT * E2].rearrange("p (t e) -> p t e", t=NT)), tb)
        do(lambda e: e.memset(off[:, 0, :], 0.0))
        for i in range(1, NT):
            do(lambda e: e.tensor_tensor(off[:, i, :], off[:, i - 1, :], tot[:, i - 1, :], ALU.add))
        do(lambda e: e.tensor_tensor(off[:, :, :], off[:, :, :], B0[:, 0:NT * E2].rearrange("p (t e) -> p t e", t=NT), ALU.add), ta)
        do(lambda e: e.tensor_tensor(off[:, :, :], off[:, :, :], oh[:, :, :], ALU.mult))
        do(lambda e: e.tensor_reduce(pos[:, :], off[:, :, :], AX.X, ALU.add))
        do(lambda e: e.tensor_scalar(pos[:, :], pos[:, :], -1.0, None, ALU.add))
        do(lambda e: e.tensor_scalar(keep[:, :], pos[:, :], float(CAP), None, ALU.is_lt))
        do(lambda e: e.scalar_tensor_tensor(slot[:, :], rt[:, :], float(CAP), pos[:, :], ALU.mult, ALU.add))
        do(lambda e: e.tensor_tensor(slot[:, :], slot[:, :], w["own"], ALU.subtract))
        do(lambda e: e.tensor_tensor(slot[:, :], slot[:, :], keep[:, :], ALU.mult))
        do(lambda e: e.tensor_tensor(slot[:, :], slot[:, :], w["own"], ALU.add))
        t = do(lambda e: e.tensor_copy(sloti[:, :], slot[:, :]))
        sct = self.c.dma_stream(nc.gpsimd, "scatter")
        self.c.join()
        for i in range(NT):
            sct.do(lambda e: e.indirect_dma_start(out=rows, out_offset=bass.IndirectOffsetOnAxis(ap=sloti[:, i:i + 1].bitcast(U32), axis=0),
                                                  in_=XN[:, i, :], in_offset=None))
        w1r = [self.slot(f"w1s{i}", [P, H2]) for i in range(2)]
        w2r = [self.slot(f"w2s{i}", [P, H2 // P, D]) for i in range(2)]
        bb = [self.slot(f"bb{i}", [P, QT, D]) for i in range(2)]
        bT = [self.slot(f"bT{i}", [P, CAP]) for i in range(2)]
        hT = [self.slot(f"hT{i}", [P, H2 // P, CAP]) for i in range(2)]
        yy = [self.slot(f"yy{i}", [P, QT, D]) for i in range(2)]
        lw = [(self.c.dma_stream(nc.sync, f"e2a{i}"), self.c.dma_stream(nc.sync, f"e2b{i}"), self.c.dma_stream(nc.sync, f"e2c{i}"),
               self.c.dma_stream(nc.scalar, f"e2d{i}")) for i in range(2)]
        J = H2 // P

        def ebody(i):
            lds = []
            for s in range(2):
                ex = i * 2 + s
                la = lw[s][0].do(lambda e: e.dma_start(w1r[s][:, :], self.ins["s_w1"][bass.ds(ex, 1), :, :].rearrange("a p h -> (a p) h")), w1r[s].handed_back())
                lb = lw[s][1].do(lambda e: e.dma_start(w2r[s][:, :, :], self.ins["s_w2"][bass.ds(ex, 1), :, :].rearrange("a (j p) d -> p (a j) d", p=P)), w2r[s].handed_back())
                lc = lw[s][2].do(lambda e: e.dma_start(bb[s][:, :, :], rows[bass.ds(ex * CAP, CAP), :].rearrange("(q p) d -> p q d", p=P)), bb[s].handed_back())
                lds.append((la, lb, lc))
            for s in range(2):
                ex = i * 2 + s
                la, lb, lc = lds[s]
                bt = self.bank[s]
                for q in range(QT):
                    t = pe.do(lambda e: e.transpose(bt[:, q * P:(q + 1) * P], bb[s][:, q, :], w["ident"]), lc, bt.handed_back())
                bb[s].hand_back(t)
                tT = ve.do(lambda e: e.tensor_copy(bT[s][:, :], bt[:, 0:CAP]), t, bT[s].handed_back())
                bt.hand_back(tT)
                for j in range(J):
                    bh = self.bank[2 + j % 4]
                    t = pe.do(lambda e: e.matmul(bh[:, 0:CAP], w1r[s][:, j * P:(j + 1) * P], bT[s][:, :], start=True, stop=True),
                              la, tT, bh.handed_back())
                    th = ac.do(lambda e: e.activation(hT[s][:, j, :], bh[:, 0:CAP], ACT.Relu,
                                                      bias=w["s_b1"][:, bass.ds(ex, 1), j:j + 1].rearrange("p a j -> p (a j)")),
                               t, hT[s].handed_back() if j == 0 else None)
                    bh.hand_back(th)
                w1r[s].hand_back(t)
                bT[s].hand_back(t)
                by = self.bank[6 + s]
                for q in range(QT):
                    for j in range(J):
                        t = pe.do(lambda e: e.matmul(by[:, q * P:(q + 1) * P], hT[s][:, j, q * P:(q + 1) * P], w2r[s][:, j, :],
                                                     start=j == 0, stop=j == J - 1), th, lb, by.handed_back() if q == 0 and j == 0 else None)
                w2r[s].hand_back(t)
                hT[s].hand_back(t)
                t = ve.do(lambda e: e.tensor_tensor(yy[s][:, :, :], by[:, 0:CAP].rearrange("p (q d) -> p q d", q=QT),
                                                    bcast(w["s_b2"][:, bass.ds(ex, 1), :].rearrange("p a d -> p (a d)"), QT, 1), ALU.add),
                          t, yy[s].handed_back())
                by.hand_back(t)
                t = lw[s][3].do(lambda e: e.dma_start(rows[bass.ds(ex * CAP, CAP), :].rearrange("(q p) d -> p q d", p=P), yy[s][:, :, :]), t, lc)
                yy[s].hand_back(t)
        self.c.loop("experts2", E2 // 2, ebody)
        YG = XN
        PART = NT // 4
        for g in range(4):
            gat = self.c.dma_stream(nc.gpsimd, f"gather{g}")
            ts = slice(g * PART, (g + 1) * PART)
            for i in range(g * PART, (g + 1) * PART):
                t = gat.do(lambda e: e.indirect_dma_start(out=YG[:, i, :], out_offset=None, in_=rows,
                                                          in_offset=bass.IndirectOffsetOnAxis(ap=sloti[:, i:i + 1].bitcast(U32), axis=0)))
            t = ve.do(lambda e: e.tensor_tensor(YG[:, ts, :], YG[:, ts, :], bcast(scl[:, ts], D, 2), ALU.mult), t)
            ve.do(lambda e: e.tensor_tensor(self.X[:, ts, :], self.X[:, ts, :], YG[:, ts, :], ALU.add), t)

    def layer3(self):
        ve, ac, pe, po, w = self.ve, self.ac, self.pe, self.po, self.w
        A3 = self.neg_exp("A3", w["A_log3"], 1)
        m = ve.do(lambda e: e.tensor_scalar(w["ctx"], w["ctx"], w["ctx_scale"], None, ALU.mult))
        sT = self.slot("sT", [P, L])
        st = self.slot("st", [P, QT, D])
        lT = self.slot("lT", [P, L])
        lg = self.slot("lg3", [P, QT, E3])
        m8 = self.slot("m83", [P, QT, 8])
        i8 = self.slot("i83", [P, QT, 8], U32)
        rf = self.slot("rf3", [P, QT, 8])
        g2 = self.slot("g23", [P, QT, 2])
        gt = [self.slot(f"gt3{i}", [P, QT, E3]) for i in range(2)]
        gt2 = self.slot("gt23", [P, QT, E3])
        NH = E3 * H3
        hz = self.slot("hz3", [P, NH + SH3 * H3])
        hs = self.slot("hs3", [P, NH + SH3 * H3])
        he = self.slot("he3", [P, NH + SH3 * H3])
        hT = self.slot("hT3", [P, 5, P])
        acc = self.slot("acc3", [P, QT, D])
        B = self.bank
        st_out = self.c.dma_stream(self.nc.sync, "store")
        outv = self.out.rearrange("(t p) d -> p t d", p=P)

        def ssm(b, k):
            B5, B6, B7 = B[5], B[6], B[7]
            xnT = self.xnT[k]
            txnT = xnT.filled()
            t = pe.do(lambda e: e.matmul(B5[0:96, 0:L], w["w_bc3"], xnT[:, :], start=True, stop=True), txnT, B5.handed_back())
            yield
            t0, t_split = yield from self.split3(B5[0:96, 0:L], t)
            B5.hand_back(t0)
            t = pe.do(lambda e: e.matmul(B6[:, 0:L], w["w_delta"], xnT[:, :], start=True, stop=True), B6.handed_back())
            yield
            t = ve.do(lambda e: e.tensor_copy(self.zin[:, 0, :], B6[:, 0:L]), t)
            B6.hand_back(t)
            t_delta = yield from self.softplus(1, t)
            u = xnT[:, :].rearrange("p (c t) -> p c t", c=1)
            yield from self.scan(1, A3, u, txnT, t_delta, t_split, (B5, B6), B7)
            yield
            t = ac.do(lambda e: e.activation(sT[:, :], B7[:, 0:L], ACT.Copy), self.t_scan, sT.handed_back())
            B7.hand_back(t)
            for q in range(QT):
                t1 = pe.do(lambda e: e.transpose(B5[:, q * P:(q + 1) * P], sT[:, q * P:(q + 1) * P], w["ident"]), t, B5.handed_back())
            sT.hand_back(t1)
            yield
            t = ve.do(lambda e: e.tensor_copy(st[:, :, :], B5[:, 0:L].rearrange("p (q d) -> p q d", q=QT)), t1, st.handed_back())
            B5.hand_back(t)
            for t5 in self.normalise(st, st, t, 1):
                if t5 is None:
                    yield
            for q in range(QT):
                t1 = pe.do(lambda e: e.transpose(B5[:, q * P:(q + 1) * P], st[:, q, :], w["ident"]), t5, B5.handed_back())
            st.hand_back(t1)
            yield
            t = ve.do(lambda e: e.tensor_scalar(lT[:, :], B5[:, 0:L], w["gamma"], w["beta"], ALU.mult, ALU.add), t1, lT.handed_back())
            B5.hand_back(t)
            for q in range(QT):
                t1 = pe.do(lambda e: e.matmul(B5[:, q * P:(q + 1) * P], lT[:, q * P:(q + 1) * P], w["ctx"], start=True, stop=True), t, B5.handed_back() if q == 0 else None)
            lT.hand_back(t1)
            yield
            t = self.add_to_x(b, B5[:, 0:L].rearrange("p (q d) -> p q d", q=QT), t1)
            B5.hand_back(t)
            yield

        def route(k):
            xnT, bk = self.xnT[k], B[4]
            for q in range(QT):
                t = pe.do(lambda e: e.matmul(bk[:, q * E3:(q + 1) * E3], xnT[:, q * P:(q + 1) * P], w["router_w"],
                                             start=True, stop=True), xnT.filled(), bk.handed_back())
            yield
            t = ve.do(lambda e: e.tensor_tensor(lg[:, :, :], bk[:, 0:QT * E3].rearrange("p (q e) -> p q e", q=QT),
                                                bcast(w["router_b"], QT, 1), ALU.add), t)
            bk.hand_back(t)
            self.gate(t)
            for q in range(QT):
                t = ve.do(lambda e: e.max(m8[:, q, :], lg[:, q, :]))
            self.gate(t)
            for q in range(QT):
                t = ve.do(lambda e: e.max_index(i8[:, q, :], m8[:, q, :], lg[:, q, :]))
            yield
            do = lambda f, *n: ve.do(f, ve.last(), *n)
            t = do(lambda e: e.tensor_tensor(g2[:, :, 1], m8[:, :, 1], m8[:, :, 0], ALU.subtract))
            t = ac.do(lambda e: e.activation(g2[:, :, 1], g2[:, :, 1], ACT.Exp), t)
            do(lambda e: e.tensor_copy(rf[:, :, :], i8[:, :, :]))
            yield
            do(lambda e: e.tensor_scalar(g2[:, :, 0], g2[:, :, 1], 1.0, None, ALU.add), t)
            do(lambda e: e.reciprocal(g2[:, :, 0], g2[:, :, 0]))
            do(lambda e: e.tensor_tensor(g2[:, :, 1], g2[:, :, 1], g2[:, :, 0], ALU.mult))
            yield
            for r, dst in ((0, gt[k]), (1, gt2)):
                do(lambda e: e.tensor_tensor(dst[:, :, :], bcast(w["iota8"], QT, 1), bcast(rf[:, :, r], E3, 2), ALU.is_equal),
                   gt[k].handed_back())
                do(lambda e: e.tensor_tensor(dst[:, :, :], dst[:, :, :], bcast(g2[:, :, r], E3, 2), ALU.mult))
            gt[k].fill(do(lambda e: e.tensor_tensor(gt[k][:, :, :], gt[k][:, :, :], gt2[:, :, :], ALU.add)))
            yield

        def moe(b, k):
            xnT = self.xnT[k]
            NA = NH + SH3 * H3
            for q in range(QT):
                xl = xnT[:, q * P:(q + 1) * P]
                tm = []
                for bk, wt, c0, cn in ((B[0], "x_w1", 0, 512), (B[1], "x_w1", 512, 128), (B[2], "x_w3", 0, 512), (B[3], "x_w3", 512, 128)):
                    tm.append(pe.do(lambda e: e.matmul(bk[:, 0:cn], xl, w[wt][:, c0:c0 + cn], start=True, stop=True), xnT.filled(), bk.handed_back()))
                yield
                parts = ((0, 0, 512), (1, 512, 128))
                for j, c0, cn in parts:
                    t = ac.do(lambda e: e.activation(he[:, c0:c0 + cn], B[j][:, 0:cn], ACT.Exp, scale=-1.0), tm[j])
                yield
                t = ve.do(lambda e: e.tensor_scalar(he[:, :], he[:, :], 1e19, None, ALU.min), t)
                yield
                t = ac.do(lambda e: e.activation(he[:, :], he[:, :], ACT.Ln, bias=1.0), t)
                t = ac.do(lambda e: e.activation(he[:, :], he[:, :], ACT.Exp, scale=-1.0), t)
                yield 2
                for j, c0, cn in parts:
                    ts = ve.do(lambda e: e.tensor_tensor(hs[:, c0:c0 + cn], he[:, c0:c0 + cn], B[j][:, 0:cn], ALU.mult),
                               t, hs.handed_back())
                    B[j].hand_back(ts)
                for j, c0, cn in parts:
                    t = ve.do(lambda e: e.tensor_tensor(hs[:, c0:c0 + cn], hs[:, c0:c0 + cn], B[2 + j][:, 0:cn], ALU.mult), ts, tm[2 + j])
                    B[2 + j].hand_back(t)
                v = hs[:, 0:NH].rearrange("p (e h) -> p e h", e=E3)
                tg = ve.do(lambda e: e.tensor_tensor(v, v, bcast(gt[k][:, q, :], H3, 2), ALU.mult), t, gt[k].filled())
                yield
                for ch in range(5):
                    bk, o = (B[0], ch * P) if ch < 4 else (B[1], 0)
                    t = pe.do(lambda e: e.transpose(bk[:, o:o + P], hs[:, ch * P:(ch + 1) * P], w["ident"]), tg, bk.handed_back() if ch in (0, 4) else None)
                hs.hand_back(t)
                yield
                t1 = ac.do(lambda e: e.activation(hT[:, 0:4, :].rearrange("p c t -> p (c t)"), B[0][:, :], ACT.Copy), t, hT.handed_back())
                t2 = ac.do(lambda e: e.activation(hT[:, 4, :], B[1][:, 0:P], ACT.Copy), t)
                B[0].hand_back(t1)
                B[1].hand_back(t2)
                for ch in range(5):
                    t = pe.do(lambda e: e.matmul(B[3][:, 0:D], hT[:, ch, :], w["x_w2"][:, ch, :], start=ch == 0, stop=ch == 4),
                              t2, B[3].handed_back() if ch == 0 else None)
                hT.hand_back(t)
                yield
                xv = self.X[:, bass.ds(b * QT + q, 1), :].rearrange("p a d -> p (a d)")
                t = ve.do(lambda e: e.tensor_tensor(xv, xv, B[3][:, 0:D], ALU.add), t, self.Xw.filled())
                self.Xw.fill(t)
                B[3].hand_back(t)
                yield
            gt[k].hand_back(tg)

        def pre(b, k):
            yield from self.layer_norm(b, k, B[4])
            yield from route(k)

        def step(b, k, last=False):
            self.weave((ssm(b, k), "ssm3"), (moe(b, k), "moe3"), (None if last else pre(b + 1, 1 - k), "pre3"))
            self.xnT[k].hand_back(pe.last(), ve.last())
            st_out.do(lambda e: e.dma_start(outv[:, bass.ds(b * QT, QT), :], self.X[:, bass.ds(b * QT, QT), :]), self.Xw.filled())

        self.steps("layer3", pre, step)

    def build(self):
        self.load_all()
        self.PT = self.sb("PT", [E0, NB, L])
        self.merged = self.sb("merged", [P, E0, NB])
        self.oall = self.sb("oall", [P, NB, E0])
        self.ob = self.slot("ob", [P, E0])
        self.oe = self.slot("oe", [E0, D])
        self.pts = self.slot("pts", [E0, L])
        if 0 in self.debug:
            with self.scope():
                self.load_packs("wf0")
                self.alloc_common(0)
                self.alloc_scan(CI)
                self.alloc0()
                self.layer0()
        with self.scope():
            fetch = self.reserve("wf1") if 1 in self.debug else None
            if 0 in self.debug:
                with self.scope():
                    self.load_packs("wf0e")
                    if fetch:
                        self.c.ahead.append(fetch)
                    self.experts0()
            elif fetch:
                fetch()
                self.c.join()
            if 1 in self.debug:
                self.alloc_common(1)
                self.layer1()
        with self.scope():
            fetch = self.reserve("wf3") if 3 in self.debug else None
            if 2 in self.debug:
                with self.scope():
                    self.load_packs("wf2")
                    if fetch:
                        self.c.ahead.append(fetch)
                    self.alloc_common(2)
                    self.layer2()
            elif fetch:
                fetch()
                self.c.join()
            if 3 in self.debug:
                self.alloc_common(3)
                self.alloc_scan(1)
                self.layer3()
        if 3 not in self.debug:
            if 0 in self.debug and 1 not in self.debug and 2 not in self.debug:
                self.c.loop("spread0", NB, lambda b: drain(self.spread0(b, self.bank[7])))
            st = self.c.dma_stream(self.nc.sync, "store")
            st.do(lambda e: e.dma_start(self.out.rearrange("(t p) d -> p t d", p=P), self.X[:, :, :]))
        self.c.join()
        self.stack.close()


def _packs(i):
    f = lambda a: np.asarray(a, np.float32) if np.asarray(a).dtype != np.float32 else np.asarray(a)
    g = {k: f(v) for k, v in i.items()}
    packs = {"wf": []}
    bf = []
    cur = ["wf"]

    def layer(name):
        packs[name] = []
        cur[0] = name

    def put(name, a, shape=None):
        a = np.asarray(a)
        shape = shape or a.shape[1:]
        packs[cur[0]].append((name, a.reshape(a.shape[0], -1), tuple(shape)))

    def rep(v):
        return np.broadcast_to(np.asarray(v).reshape(1, -1), (P, np.asarray(v).size))

    def heads4(wm):
        out = np.zeros((wm.shape[0], 4, 4, 32), np.float32)
        out[:, :, :, 0:8] = wm.reshape(wm.shape[0], 4, 4, 8)
        return out.reshape(wm.shape[0], 4, P)

    def bias4(b):
        return heads4(b.reshape(1, P))[0].T

    def out4(wm):
        return heads4(wm.T).transpose(2, 1, 0)

    put("ident", np.eye(P, dtype=np.float32))
    put("eps", np.full((P, 1), EPS, np.float32))
    put("iota8", rep(np.arange(8, dtype=np.float32)))
    put("own", (E2 * CAP + np.arange(NT)[None, :] * P + np.arange(P)[:, None]).astype(np.float32))
    layer("wf0")
    wqkv, bqkv = g["L0_attn_wqkv"], g["L0_attn_bqkv"]
    put("wq0", heads4(wqkv[:, :P]))
    put("bq0", bias4(bqkv[:P]))
    put("wk0", heads4(np.tile(wqkv[:, P:P + 8], (1, HEADS)))[:, 0:1])
    put("bk0", bias4(np.tile(bqkv[P:P + 8], HEADS))[:, 0:1])
    put("wv0", wqkv[:, P + 8:])
    put("bv0", rep(bqkv[P + 8:]))
    put("wo0", out4(g["L0_attn_w_attn_out"]))
    put("bo0", rep(g["L0_attn_b_attn_out"]))
    put("w_in", g["L0_attn_w_in"].reshape(D, 2 * CI, P))
    ch = lambda a: np.swapaxes(a.reshape(CI, P, -1), 0, 1)
    put("conv_w", ch(g["L0_attn_conv_w"]))
    put("conv_b", ch(g["L0_attn_conv_b"])[:, :, 0])
    xp = ch(g["L0_attn_w_xproj"])
    put("w_dtin", np.ascontiguousarray(xp[:, :, :DTR]))
    put("w_bc", np.tile(xp[:, :, DTR:], (1, 1, 3)))
    put("w_dt", g["L0_attn_w_dt"])
    put("b_dt", ch(g["L0_attn_b_dt"])[:, :, 0])
    put("A_log0", ch(g["L0_attn_A_log"]))
    put("Dp", ch(g["L0_attn_Dp"])[:, :, 0])
    put("w_out", ch(g["L0_attn_w_out"]))
    put("gate_w", g["L0_ffn_gate_w"].T)
    put("gate_b", g["L0_ffn_gate_b"].reshape(E0, 1))
    layer("wf0e")
    w1, w2 = g["L0_ffn_w1"], g["L0_ffn_w2"]
    put("m_b1", w1[:, D, :].reshape(E0, H0 // P, P).transpose(2, 0, 1))
    put("m_b2", w2[:, H0, :].T)
    layer("wf1")
    for n in "qk":
        put(f"w{n}1", g[f"L1_attn_W{n}"].transpose(1, 0, 2).reshape(D, 8, P))
        put(f"b{n}1", g[f"L1_attn_b{n}"].reshape(8, P).T)
    put("wv1", g["L1_attn_Wv"].transpose(1, 0, 2).reshape(D, HEADS * A1))
    put("bv1", rep(g["L1_attn_bv"]))
    put("wo1", g["L1_attn_Wo"].reshape(8, P, D).transpose(1, 0, 2))
    put("bo1", rep(g["L1_attn_bo"]))
    pad = lambda a: np.concatenate([a, np.zeros((3 * P - I1, a.shape[1]), np.float32)]).reshape(3, P, -1).transpose(1, 0, 2)
    put("wgu1", np.concatenate([pad(g["L1_ffn_w_gate"]), pad(g["L1_ffn_w_up"])], 1))
    put("wd1", g["L1_ffn_w_down"])
    layer("wf2")
    for n in "qk":
        put(f"w{n}2", heads4(g[f"L2_attn_W{n}"].T))
        put(f"b{n}2", bias4(g[f"L2_attn_b{n}"]))
    put("wv2", g["L2_attn_Wv"].T)
    put("bv2", rep(g["L2_attn_bv"]))
    put("wo2", out4(g["L2_attn_Wo"].T))
    put("bo2", rep(g["L2_attn_bo"]))
    put("w_switch", g["L2_ffn_w_switch"])
    put("b_switch", rep(g["L2_ffn_b_switch"]))
    put("s_b1", g["L2_ffn_b1"].reshape(E2, H2 // P, P).transpose(2, 0, 1))
    put("s_b2", rep(g["L2_ffn_b2"]), (E2, D))
    layer("wf3")
    put("A_log3", g["L3_attn_A_log"].reshape(P, 1, NS))
    put("w_delta", g["L3_attn_W_delta"].T)
    put("w_bc3", np.tile(np.concatenate([g["L3_attn_W_B"], g["L3_attn_W_C"]]).T, (1, 3)))
    put("gamma", g["L3_attn_ln_gamma"].reshape(P, 1))
    put("beta", g["L3_attn_ln_beta"].reshape(P, 1))
    put("ctx", g["L3_attn_W_ctx"].T)
    put("ctx_scale", rep(g["L3_attn_context_scale"]))
    put("router_w", g["L3_ffn_router_w"])
    put("router_b", rep(g["L3_ffn_router_b"]))
    for n in ("w1", "w3"):
        a = np.concatenate([g["L3_ffn_routed_" + n], g["L3_ffn_shared_" + n]])
        put("x_" + n, a.transpose(1, 0, 2).reshape(D, -1))
    a = np.concatenate([g["L3_ffn_routed_w2"], g["L3_ffn_shared_w2"]])
    put("x_w2", a.reshape(5, P, D).transpose(1, 0, 2))
    tri = np.where(np.arange(P)[:, None] >= np.arange(P)[None, :], 0.0, NEG)

    def putb(name, a):
        a = np.asarray(a)
        bf.append((name, a.reshape(a.shape[0], -1).astype(np.float32), tuple(a.shape[1:])))

    putb("identb", np.eye(P))
    putb("mask", np.tile(tri, (1, 4)))
    putb("upto", (np.arange(P)[:, None] <= np.arange(P)[None, :]).astype(np.float32))
    putb("onesb", np.ones((P, P)))
    putb("sel", np.arange(96)[:, None] % 32 == np.arange(32)[None, :])

    packed, arrays = {}, {}
    packs["wb"] = bf
    for pname, items in packs.items():
        off, parts, cols = 0, {}, []
        for name, a, shape in items:
            parts[name] = (off, a.shape[0], shape)
            full = np.zeros((P, a.shape[1]), a.dtype)
            full[:a.shape[0]] = a
            cols.append(full)
            off += a.shape[1]
        arrays[pname] = np.ascontiguousarray(np.concatenate(cols, 1))
        packed[pname] = (off, parts)
    return packed, arrays


LAYERS = (0, 1, 2, 3)


def kernel(**inputs):
    import concourse.bacc as _bacc
    from concourse.bass_utils import run_bass_kernel_spmd as _run

    inputs = {k: np.asarray(v) for k, v in inputs.items()}
    packed, arrays = _packs(inputs)
    arrays["x"] = np.ascontiguousarray(inputs["L0_attn_x"]).reshape(NB * L, D)
    arrays["m_w1"] = np.ascontiguousarray(inputs["L0_ffn_w1"])
    arrays["m_w2"] = np.ascontiguousarray(inputs["L0_ffn_w2"])
    arrays["s_w1"] = np.ascontiguousarray(inputs["L2_ffn_w1"])
    arrays["s_w2"] = np.ascontiguousarray(inputs["L2_ffn_w2"])
    turn_ends = {}
    for _ in range(3):
        nc = _bacc.Bacc("TRN2", target_bir_lowering=False, num_devices=1)
        ins = {n: nc.dram_tensor(n, list(a.shape), mybir.dt.from_np(a.dtype), kind="ExternalInput").ap()
               for n, a in arrays.items()}
        out = nc.dram_tensor("out", [NB * L, D], F32, kind="ExternalOutput").ap()
        program = Program(nc, turn_ends, ins, packed, out, LAYERS)
        program.build()
        turn_ends.update(program.c.steps)
    r = _run(nc, [arrays], core_ids=[0])
    return r.results[0]["out"].reshape(NB, L, D)
```
